# Optimizing a Trainium2 kernel written in Bass

```python
import numpy as np
import jax
import jax.numpy as jnp

def _softmax(x, axis=-1):
    return jax.nn.softmax(x, axis=axis)

def _gelu(x):
    return jax.nn.gelu(x, approximate=True)

def _silu(x):
    return jax.nn.silu(x)

def _sigmoid(x):
    return jax.nn.sigmoid(x)

def _layernorm(x, axis=-1, eps=1e-05):
    m = jnp.mean(x, axis=axis, keepdims=True)
    v = jnp.var(x, axis=axis, keepdims=True)
    return (x - m) / jnp.sqrt(v + eps)

def _scatter_add(tgt, idx, src, axis=0):
    return tgt.at[idx].add(src)

def _segment_sum(src, seg, n):
    return jax.ops.segment_sum(src, seg, n)
kernel_name = 'mk_xattn_ffn_d1_seqx_r8_5f9640'

def setup_inputs(seed: int=0):
    np.random.seed(seed)
    _w = jnp.asarray

    def _rec_inputs():
        import jax
        import jax.numpy as jnp
        _rk = jax.random.key(seed)
        x = -0.000125 + 0.9999 * jax.random.normal(jax.random.fold_in(_rk, 1), (64, 128, 128), jnp.float32)
        _lenS = 128 - jax.random.randint(jax.random.fold_in(_rk, 7), (64,), 0, max(1, 128 // 4) + 1, jnp.int32)
        _lenS2 = 77 - jax.random.randint(jax.random.fold_in(_rk, 8), (64,), 0, max(1, 77 // 4) + 1, jnp.int32)
        _ctx_768P = jax.random.normal(jax.random.fold_in(_rk, 11), (64, 16, 96), jnp.float32)
        _ctx_768c = jax.random.dirichlet(jax.random.fold_in(_rk, 511), 0.3 * jnp.ones((16,), jnp.float32), (64, 77))
        _ctx_768t = jnp.einsum('bsk,bkd->bsd', _ctx_768c, _ctx_768P)
        _ctx_768t = _ctx_768t * jax.lax.rsqrt(jnp.mean(jnp.square(_ctx_768t)) + 1e-12) * 0.953939
        ctx_768 = -7.36909e-05 + 0.999899 * (_ctx_768t + 0.3 * jax.random.normal(jax.random.fold_in(_rk, 611), (64, 77, 96), jnp.float32))
        return (x, ctx_768)
    x, ctx_768 = _rec_inputs()

    def _L0_xattn_setup():
        import jax, jax.numpy as jnp
        import numpy as np
        import math
        E = 128
        EV = 128
        FFN = 512
        DINO = 96
        B, S, P = (64, 64, 32)

        def bitnet_linear(x, W, b):
            w_scale = jnp.maximum(jnp.mean(jnp.abs(W)), 1e-05)
            qW = jnp.sign(W) * (jnp.abs(W) > 0.5 * w_scale).astype(W.dtype)
            i_scale = jnp.maximum(jnp.max(jnp.abs(x)), 1e-08) / 127.0
            qx = jnp.clip(jnp.round(x / i_scale), -128.0, 127.0)
            out = jnp.einsum('...i,oi->...o', qx, qW) * (w_scale * i_scale)
            return out + b
        key = jax.random.key(seed)
        ks = iter(jax.random.split(key, 32))

        def lin_w(fin, fout):
            return jax.random.normal(next(ks), (fout, fin), jnp.float32) * math.sqrt(2.0 / fin)
        return {'text_embeddings': jax.random.normal(next(ks), (B, S, E), jnp.float32), 'dinov2_features': jax.random.normal(next(ks), (B, P, DINO), jnp.float32), 'W_d2v': lin_w(DINO, EV), 'b_d2v': jnp.zeros((EV,), jnp.float32), 'W_img': lin_w(EV, E), 'b_img': jnp.zeros((E,), jnp.float32), 'W_txt': lin_w(E, E), 'b_txt': jnp.zeros((E,), jnp.float32), 'W_att0': lin_w(E, E // 2), 'b_att0': jnp.zeros((E // 2,), jnp.float32), 'W_att1': lin_w(E, E // 2), 'b_att1': jnp.zeros((E // 2,), jnp.float32), 'W_f1': lin_w(2 * E, FFN), 'b_f1': jnp.zeros((FFN,), jnp.float32), 'W_f2': lin_w(FFN, E), 'b_f2': jnp.zeros((E,), jnp.float32)}
    _L0_xattn_all = _L0_xattn_setup()
    _L0_xattn_in = {k: v for k, v in _L0_xattn_all.items() if k in ('W_d2v', 'b_d2v', 'W_img', 'b_img', 'W_txt', 'b_txt', 'W_att0', 'b_att0', 'W_att1', 'b_att1', 'W_f1', 'b_f1', 'W_f2', 'b_f2')}
    del _L0_xattn_all

    def _L0_ffn_setup():
        import math
        import jax, jax.numpy as jnp
        import numpy as np
        D_MODEL = 128
        D_FF = 512
        N_EXPERTS = 8
        CAPACITY_FACTOR = 1.25
        L, B = (64, 8)

        def _route(tokens, router_w):
            T = tokens.shape[0]
            E = router_w.shape[0]
            capacity = int(math.ceil(T / E * CAPACITY_FACTOR))
            logits = tokens @ router_w.T
            probs = jax.nn.softmax(logits, axis=-1)
            top1_idx = jnp.argmax(probs, axis=-1)
            top1_prob = jnp.max(probs, axis=-1)
            order = jnp.lexsort((-top1_prob, top1_idx))
            sorted_e = top1_idx[order]
            counts = jnp.bincount(top1_idx, length=E)
            start = jnp.cumsum(counts) - counts
            pos_in_group = jnp.arange(T) - start[sorted_e]
            keep_sorted = pos_in_group < capacity
            keep = jnp.zeros((T,), bool).at[order].set(keep_sorted)
            return jnp.where(keep, top1_idx, 0).astype(jnp.int32)
        key = jax.random.key(seed)
        ks = jax.random.split(key, 6)
        s_in = 1.0 / math.sqrt(D_MODEL)
        s_ff = 1.0 / math.sqrt(D_FF)
        return {'x': jax.random.normal(ks[0], (L, B, D_MODEL), dtype=jnp.float32), 'router_w': jax.random.uniform(ks[1], (N_EXPERTS, D_MODEL), minval=-s_in, maxval=s_in), 'W1': jax.random.uniform(ks[2], (N_EXPERTS, D_MODEL, D_FF), minval=-s_in, maxval=s_in), 'b1': jax.random.uniform(ks[3], (N_EXPERTS, D_FF), minval=-s_in, maxval=s_in), 'W2': jax.random.uniform(ks[4], (N_EXPERTS, D_FF, D_MODEL), minval=-s_ff, maxval=s_ff), 'b2': jax.random.uniform(ks[5], (N_EXPERTS, D_MODEL), minval=-s_ff, maxval=s_ff)}
    _L0_ffn_all = _L0_ffn_setup()
    _L0_ffn_in = {k: v for k, v in _L0_ffn_all.items() if k in ('router_w', 'W1', 'b1', 'W2', 'b2')}
    del _L0_ffn_all
    return {'x': x, 'ctx_768': ctx_768, 'L0_xattn_W_d2v': _L0_xattn_in['W_d2v'], 'L0_xattn_b_d2v': _L0_xattn_in['b_d2v'], 'L0_xattn_W_img': _L0_xattn_in['W_img'], 'L0_xattn_b_img': _L0_xattn_in['b_img'], 'L0_xattn_W_txt': _L0_xattn_in['W_txt'], 'L0_xattn_b_txt': _L0_xattn_in['b_txt'], 'L0_xattn_W_att0': _L0_xattn_in['W_att0'], 'L0_xattn_b_att0': _L0_xattn_in['b_att0'], 'L0_xattn_W_att1': _L0_xattn_in['W_att1'], 'L0_xattn_b_att1': _L0_xattn_in['b_att1'], 'L0_xattn_W_f1': _L0_xattn_in['W_f1'], 'L0_xattn_b_f1': _L0_xattn_in['b_f1'], 'L0_xattn_W_f2': _L0_xattn_in['W_f2'], 'L0_xattn_b_f2': _L0_xattn_in['b_f2'], 'L0_ffn_router_w': _L0_ffn_in['router_w'], 'L0_ffn_W1': _L0_ffn_in['W1'], 'L0_ffn_b1': _L0_ffn_in['b1'], 'L0_ffn_W2': _L0_ffn_in['W2'], 'L0_ffn_b2': _L0_ffn_in['b2']}

def reference(x, ctx_768, L0_xattn_W_d2v, L0_xattn_b_d2v, L0_xattn_W_img, L0_xattn_b_img, L0_xattn_W_txt, L0_xattn_b_txt, L0_xattn_W_att0, L0_xattn_b_att0, L0_xattn_W_att1, L0_xattn_b_att1, L0_xattn_W_f1, L0_xattn_b_f1, L0_xattn_W_f2, L0_xattn_b_f2, L0_ffn_router_w, L0_ffn_W1, L0_ffn_b1, L0_ffn_W2, L0_ffn_b2):
    import jax
    import jax.numpy as jnp

    def _L0_xattn_ref(text_embeddings, dinov2_features, W_d2v, b_d2v, W_img, b_img, W_txt, b_txt, W_att0, b_att0, W_att1, b_att1, W_f1, b_f1, W_f2, b_f2):
        import jax, jax.numpy as jnp
        import numpy as np
        import math
        E = 128
        EV = 128
        FFN = 512
        DINO = 96
        B, S, P = (64, 64, 32)

        def bitnet_linear(x, W, b):
            w_scale = jnp.maximum(jnp.mean(jnp.abs(W)), 1e-05)
            qW = jnp.sign(W) * (jnp.abs(W) > 0.5 * w_scale).astype(W.dtype)
            i_scale = jnp.maximum(jnp.max(jnp.abs(x)), 1e-08) / 127.0
            qx = jnp.clip(jnp.round(x / i_scale), -128.0, 127.0)
            out = jnp.einsum('...i,oi->...o', qx, qW) * (w_scale * i_scale)
            return out + b
        b, s, e = text_embeddings.shape
        vis = bitnet_linear(dinov2_features, W_d2v, b_d2v)
        image_embeds = bitnet_linear(vis, W_img, b_img)
        fused = bitnet_linear(text_embeddings, W_txt, b_txt)
        inv_sqrt_e = 1.0 / math.sqrt(e)
        for Wa, ba in ((W_att0, b_att0), (W_att1, b_att1)):
            kv = bitnet_linear(image_embeds, Wa, ba)
            k = jnp.concatenate([kv, kv], axis=-1)
            scores = jnp.einsum('bse,bpe->bsp', fused, k) * inv_sqrt_e
            attn = jax.nn.softmax(scores, axis=-1)
            fused = fused + 0.1 * jnp.einsum('bsp,bpe->bse', attn, k)
        avg_img = jnp.mean(image_embeds, axis=1, keepdims=True)
        concatenated = jnp.concatenate([fused, jnp.broadcast_to(avg_img, (b, s, e))], axis=-1)
        h = jax.nn.relu(bitnet_linear(concatenated, W_f1, b_f1))
        return bitnet_linear(h, W_f2, b_f2)

    def _L0_ffn_ref(x, router_w, W1, b1, W2, b2):
        import math
        import jax, jax.numpy as jnp
        import numpy as np
        D_MODEL = 128
        D_FF = 512
        N_EXPERTS = 8
        CAPACITY_FACTOR = 1.25
        L, B = (64, 8)

        def _route(tokens, router_w):
            T = tokens.shape[0]
            E = router_w.shape[0]
            capacity = int(math.ceil(T / E * CAPACITY_FACTOR))
            logits = tokens @ router_w.T
            probs = jax.nn.softmax(logits, axis=-1)
            top1_idx = jnp.argmax(probs, axis=-1)
            top1_prob = jnp.max(probs, axis=-1)
            order = jnp.lexsort((-top1_prob, top1_idx))
            sorted_e = top1_idx[order]
            counts = jnp.bincount(top1_idx, length=E)
            start = jnp.cumsum(counts) - counts
            pos_in_group = jnp.arange(T) - start[sorted_e]
            keep_sorted = pos_in_group < capacity
            keep = jnp.zeros((T,), bool).at[order].set(keep_sorted)
            return jnp.where(keep, top1_idx, 0).astype(jnp.int32)
        Lx, Bx, D = x.shape
        T = Lx * Bx
        E = router_w.shape[0]
        tokens = x.reshape(T, D)
        final_e = _route(tokens, router_w)
        out = jnp.zeros_like(tokens)
        for e in range(E):
            h = jax.nn.relu(tokens @ W1[e] + b1[e])
            y = h @ W2[e] + b2[e]
            out = out + jnp.where((final_e == e)[:, None], y, 0.0)
        return out.reshape(Lx, Bx, D)
    x = x + _L0_xattn_ref(_layernorm(x, axis=-1), ctx_768, L0_xattn_W_d2v, L0_xattn_b_d2v, L0_xattn_W_img, L0_xattn_b_img, L0_xattn_W_txt, L0_xattn_b_txt, L0_xattn_W_att0, L0_xattn_b_att0, L0_xattn_W_att1, L0_xattn_b_att1, L0_xattn_W_f1, L0_xattn_b_f1, L0_xattn_W_f2, L0_xattn_b_f2)
    x = x + _L0_ffn_ref(_layernorm(x, axis=-1), L0_ffn_router_w, L0_ffn_W1, L0_ffn_b1, L0_ffn_W2, L0_ffn_b2)
    return x

_drawn_inputs = setup_inputs


def setup_inputs(seed=0):
    import zlib

    import numpy as np

    out = dict(_drawn_inputs(seed))
    spreads = {'L0_xattn_b_d2v': (0.0, 0.1),
     'L0_xattn_b_img': (0.0, 0.1),
     'L0_xattn_b_txt': (0.0, 0.1),
     'L0_xattn_b_att0': (0.0, 0.1),
     'L0_xattn_b_att1': (0.0, 0.269),
     'L0_xattn_b_f1': (0.0, 0.1),
     'L0_xattn_b_f2': (0.0, 0.1)}
    factors = {'L0_ffn_b1': 3.039}
    for name, (base, spread) in spreads.items():
        noise = np.random.default_rng([zlib.crc32(name.encode()), seed]).standard_normal(out[name].shape)
        drawn = base * np.exp(spread * noise) if base else spread * noise
        out[name] = jnp.asarray(drawn.astype(out[name].dtype))
    for name, factor in factors.items():
        out[name] = (out[name] * factor).astype(out[name].dtype)
    return out
```

```python
from contextlib import ExitStack

import numpy as np

import concourse.bass as bass
from concourse import mybir

F32 = mybir.dt.float32
BF16 = mybir.dt.bfloat16
I32 = mybir.dt.int32
ALU = mybir.AluOpType
ACT = mybir.ActivationFunctionType
AX = mybir.AxisListType.X

P = 128
B = 64
S = 128
E = 128
CT = 77
DC = 96
KV = 64
FF = 512
NC = FF // P
NX = 8
T = B * S
GB = 4
G = B // GB
GT = GB * S
GC = GB * CT
CP = 112
CJ = B * CT // CP
CAP = int(np.ceil(T / NX * 1.25))
NT = T // P + NX
RING = 8
DEPTH = 4
COPY = 4
LAG = 9
XW = E + 2
MAGIC = 12582912.0
EPS = 1e-5
KEY_BITS = 28
FAR = 32768
WIDTHS = (DC, E, E, E, E, NC * 2 * E, FF)
COUNTS = (E * DC, E * E, E * E, KV * E, KV * E, FF * 2 * E, E * FF)
D2V, IMG, TXT, ATT0, ATT1, F1, F2 = range(7)
Q_CTX, Q_VIS, Q_IMG, Q_X, Q_CAT, Q_H = range(6)


def wait(eng, sem, value):
    if not isinstance(value, int) or value > 0:
        eng.wait_ge(sem, value)


def wait_alone(eng, sem, value, passed):
    if not isinstance(value, int) or value > 0:
        eng.wait_ge(sem, value)
        eng.sem_inc(passed, 1)


class Chain:

    def __init__(self, eng, sem):
        self.eng, self.sem, self.base, self.count = eng, sem, 0, 0

    def link(self, ins):
        ins.then_inc(self.sem, 1)
        self.count += 1

    def join(self):
        self.eng.wait_ge(self.sem, self.base + self.count)

    def loop(self, start, end, per, body):
        first = self.base + self.count
        with self.eng.Fori(start, end) as i:
            self.base, self.count = (i - start) * per + first, 0
            body(i)
            assert self.count == per, self.count
        self.base, self.count = first + (end - start) * per, 0


def xattn_moe(nc, x, ctx_in, weights, biases, router_w, W1, b1, W2, b2, out):
    rows = nc.dram_tensor("token_rows", (T, XW), F32).ap()
    with ExitStack() as stack:
        def sb(name, shape, dtype=F32):
            return stack.enter_context(nc.sbuf_tensor(name, shape, dtype))

        def sem(name):
            return stack.enter_context(nc.semaphore(name))

        psum = stack.enter_context(nc.psum_tensor("psum", [P, 8, 512], F32))

        ident = sb("ident", [P, P])
        ident_b = sb("ident_b", [P, P], BF16)
        ones = sb("ones", [P, P])
        ones_b = sb("ones_b", [P, P], BF16)
        before_b = sb("before_b", [P, P], BF16)
        same_expert = sb("same_expert", [P, P])
        magic = sb("magic", [P, 1])
        inv_counts = sb("inv_counts", [P, 7])
        steps = sb("steps", [P, KEY_BITS])
        tile_no = sb("tile_no", [P, NT])
        tile_no_b = sb("tile_no_b", [P, NT], BF16)
        row_no_b = sb("row_no_b", [P, P], BF16)
        part_no = sb("part_no", [P, 1])
        turn_no = sb("turn_no", [P, B])
        rank8 = sb("rank8", [P, NX])
        seg = sb("seg", [P, NX * B])
        wsum = sb("wsum", [P, 7])
        ws = sb("ws", [P, 7])
        wlim = sb("wlim", [P, 2, 7])
        wT = sb("wT", [P, 3 * P], BF16)
        attT = sb("attT", [P, 2, 2, KV], BF16)
        f1T = sb("f1T", [P, 2, FF], BF16)
        f2T = sb("f2T", [P, NC, E], BF16)
        small_w = sb("small_w", [NX + NX * NC, E])
        small_wT = sb("small_wT", [P, NX + NX * NC])
        rwT = small_wT[:, 0:NX]
        b1col = small_wT[:, NX:].rearrange("p (e c) -> p e c", e=NX)
        bcol = sb("bcol", [P, 5 + NC])
        batt = sb("batt", [P, 2, 2, KV])
        bf2 = sb("bf2", [P, E])
        amax = sb("amax", [P, 6])
        gmax = sb("gmax", [1, 6])
        iscale = sb("iscale", [P, 6])
        inv = sb("inv", [P, 6])
        scale = sb("scale", [P, 7])
        h_scale = sb("h_scale", [P, 1])
        h_bias = sb("h_bias", [P, NC])
        xall = sb("xall", [P, B, XW])
        big = sb("big", [P, T])
        tok_b = sb("tok_b", [P, T], BF16)
        xqT = sb("xqT", [P, T], BF16)
        feat = sb("feat", [P, B * CT])
        qa = sb("qa", [P, B * CT], BF16)
        qb = sb("qb", [P, B * CT], BF16)
        keys = sb("keys", [P, 2 * B * CT])
        stats = sb("stats", [P, B, 6])
        tmp = sb("tmp", [P, 4, B])
        part = sb("part", [P, 4, B])
        avg = sb("avg", [P, B])
        avg_q = sb("avg_q", [P, B], BF16)

        wraw = big[:, 0:sum(WIDTHS)]
        wq = big[:, sum(WIDTHS):sum(WIDTHS) * 3 // 2].bitcast(BF16)
        wneg = big[:, sum(WIDTHS) * 3 // 2:sum(WIDTHS) * 2].bitcast(BF16)
        ctx_raw = keys[:, 0:CJ * DC]
        ctx_q = tok_b[0:CP, 0:CJ * DC]
        kT = keys[:, :].rearrange("p (l n) -> p l n", l=2)
        xn = big[:, :].rearrange("p (t d) -> p t d", d=E)

        fused0 = sb("fused0", [P, GT])
        fused1 = sb("fused1", [P, GT])
        qb_f = qb[:, :].bitcast(F32)
        prob = [qb_f[:, n * GC:(n + 1) * GC].rearrange("p (b c) -> p b c", b=GB) for n in range(2)]
        probT = [sb(f"probT{n}", [CT, GT]) for n in range(2)]
        ktok = [qb_f[0:CT, 2 * GC + n * GB * P:2 * GC + (n + 1) * GB * P].rearrange("p (b k) -> p b k", b=GB)
                for n in range(2)]
        amx = sb("amx", [P, 2, GB])
        asum = sb("asum", [P, 2, GB])
        arec = sb("arec", [P, 2, GB])
        u = feat[:, 0:NC * GT].rearrange("p (c n) -> p c n", c=NC)
        hq = feat[:, NC * GT:NC * GT * 3 // 2].bitcast(BF16).rearrange("p (c n) -> p c n", c=NC)
        xs = fused0[:, :].rearrange("p (t d) -> p t d", d=E)
        xsT = fused1[:, :]
        st2 = stats[:, 0:GB, :]

        def route(n):
            return big[:, n * 512:(n + 1) * 512]

        w1s = keys[:, 0:NX * FF].rearrange("p (e f) -> p e f", e=NX)
        w2s = keys[:, NX * FF:2 * NX * FF].rearrange("p (e c d) -> p e c d", e=NX, c=NC)
        b2bc = keys[:, 2 * NX * FF:2 * NX * FF + NX * E]
        xqT_f = xqT[:, :].bitcast(F32)
        cut = [0]

        def carve(n):
            cut[0] += n
            return xqT_f[:, cut[0] - n:cut[0]]
        xg = [xall[:, n, :] for n in range(RING)]
        y = [xall[:, RING + n, 0:E] for n in range(RING)]
        gn = [carve(E) for _ in range(DEPTH)]
        gT = [carve(E) for _ in range(DEPTH)]
        hT = [carve(FF) for _ in range(DEPTH)]
        w1_now = [feat[:, n * FF:(n + 1) * FF] for n in range(DEPTH)]
        b1_now = [sb(f"b1_now{n}", [P, NC]) for n in range(DEPTH)]
        idx_in = sb("idx_in", [P, RING], I32)
        idx_out = sb("idx_out", [P, RING], I32)
        src_of = sb("src_of", [P, NT], I32)
        dst_of = sb("dst_of", [P, NT], I32)
        expert_of = sb("expert_of", [1, NT], I32)
        cnt = sb("cnt", [P, 1])
        acc = sb("acc", [P, 1])
        thr = sb("thr", [P, 1])
        cand = sb("cand", [P, 1])
        thr8 = sb("thr8", [P, NX])
        n8 = [sb(f"n8_{n}", [P, NX]) for n in range(5)]
        n8i = [sb(f"n8i_{n}", [P, NX], I32) for n in range(2)]
        t64 = [sb(f"t64_{n}", [P, B]) for n in range(8)]
        t64i = [sb(f"t64i_{n}", [P, B], I32) for n in range(3)]
        hot_row = [sb(f"hot_row{n}", [P, P], BF16) for n in range(2)]
        hot_tile = [sb(f"hot_tile{n}", [P, 2, NT], BF16) for n in range(2)]

        s_ctx = sem("ctx_loaded")
        s_w = sem("weights_loaded")
        s_x = [sem(f"x_loaded{n}") for n in range(8)]
        s_small = sem("biases_loaded")
        s_moe = sem("expert_weights_loaded")
        s_const = sem("constants_made")
        s_cc = sem("constants_begun")
        s_amax = sem("amax_ready")
        s_grow = sem("amax_row_ready")
        s_gm = sem("global_max_ready")
        s_gcol = sem("global_max_spread")
        s_inv = sem("inv_ready")
        s_wsum = sem("wsum_ready")
        s_wtot = sem("wsum_spread")
        s_wq = sem("weights_quantised")
        s_wtr = sem("weights_transposed")
        s_wT = sem("weights_in_place")
        s_sc = sem("scales_ready")
        s_cq = sem("ctx_quantised")
        s_tr = sem("transposed")
        s_trc = sem("transposed_copied")
        s_mm = sem("linear_done")
        s_mmc = sem("linear_copied")
        s_vq = sem("vis_quantised")
        s_iq = sem("image_quantised")
        s_var = sem("variance_ready")
        s_std = sem("deviation_ready")
        s_xs = sem("x_scaled")
        s_xq = sem("x_quantised")
        s_f = sem("fused_ready")
        s_fmm = sem("fused_product")
        s_kmm = [sem(f"ktok_product{n}") for n in range(2)]
        s_kev = [sem(f"ktok_scaled{n}") for n in range(2)]
        s_kt = [sem(f"ktok_ready{n}") for n in range(2)]
        s_smm = [sem(f"scores{n}") for n in range(2)]
        s_sub = [sem(f"scores_less_max{n}") for n in range(2)]
        s_e = [sem(f"exp{n}") for n in range(2)]
        s_r = [sem(f"sum_inverted{n}") for n in range(2)]
        s_p = [sem(f"probs{n}") for n in range(2)]
        s_t = [sem(f"probs_transposed{n}") for n in range(2)]
        s_pt = [sem(f"probsT_copied{n}") for n in range(2)]
        s_av = [sem(f"attended{n}") for n in range(2)]
        s_up = [sem(f"fused_updated{n}") for n in range(2)]
        s_res = sem("residual_ready")
        s_cs = sem("cat_scaled")
        s_catq = sem("cat_quantised")
        s_h = sem("hidden_product")
        s_hm = sem("hidden_max_taken")
        s_h2 = sem("hidden_product_again")
        s_relu = sem("relu_done")
        s_hq = sem("hidden_quantised")
        s_f2 = sem("out_product")
        s_var2 = sem("variance2_ready")
        s_std2 = sem("deviation2_ready")
        s_xn2 = sem("xn2_ready")
        s_x2t = sem("xn2_transposed")
        s_x2c = sem("xn2T_copied")
        s_lg = sem("logits_ready")
        s_rows = sem("rows_stored")
        s_d = sem("logits_less_max")
        s_ex = sem("logits_exp")
        s_v = sem("keys_by_expert")
        s_vt = sem("keys_transposed")
        s_cnt = sem("counts_ready")
        s_cnt2 = sem("counts_summed")
        s_thr = sem("threshold_ready")
        s_thr_r = sem("threshold_row")
        s_thr_c = sem("threshold_row_copied")
        s_thr_s = sem("threshold_spread")
        s_ms = sem("masks_ready")
        s_ps = sem("prefixes_ready")
        s_hot = sem("one_hots_ready")
        s_inv_mm = sem("one_hots_used")
        s_idx = sem("indices_ready")
        s_ixi = sem("gather_index_copied")
        s_ixo = sem("scatter_index_copied")
        s_g = [sem(f"gathered{n}") for n in range(RING)]
        s_y = sem("result_ready")
        s_o = [sem(f"scattered{n}") for n in range(RING)]
        s_prep = sem("tile_prepared")
        s_gt = sem("gathered_transposed")
        s_gc = sem("gatheredT_copied")
        s_l1 = sem("layer1_product")
        s_hc = sem("hidden_relu_scalar")
        s_hd = sem("hidden_relu_vector")
        s_l2 = sem("layer2_product")
        s_passed = sem("gpsimd_waits_passed")
        s_passed2 = sem("vector_waits_passed")
        s_dve = sem("vector_chain")
        s_act = sem("scalar_chain")

        WOFF = [sum(WIDTHS[:k]) for k in range(7)]

        def wslice(t, k):
            return t[0:KV if k in (ATT0, ATT1) else P, WOFF[k]:WOFF[k] + WIDTHS[k]]

        def bank(n, width=512, rows_=P):
            return psum[0:rows_, n, 0:width]

        def bank_b(n):
            return psum[:, n, :].bitcast(BF16)

        def c4(i):
            return bass.ds(i * GC, GC)

        def g4(i):
            return bass.ds(i * GT, GT)

        block = stack.enter_context(nc.Block())

        @block.sync
        def _(sp):
            sp.dma_start(ctx_raw[0:CP, 0:CJ * DC],
                         ctx_in.rearrange("b c d -> (b c) d").rearrange("(p j) d -> p (j d)", p=CP)).then_inc(s_ctx, 16)
            for k in range(5):
                sp.dma_start(wslice(wraw, k), weights[k]).then_inc(s_w, 16)
            sp.dma_start(wslice(wraw, F1).rearrange("p (c i) -> p c i", c=NC),
                         weights[F1].rearrange("(c p) i -> p c i", p=P)).then_inc(s_w, 16)
            sp.dma_start(wslice(wraw, F2), weights[F2]).then_inc(s_w, 16)
            xt = x.rearrange("b s e -> s b e")
            for n in range(8):
                sp.dma_start(xall[:, 8 * n:8 * n + 8, 0:E], xt[:, 8 * n:8 * n + 8, :]).then_inc(s_x[n], 16)
            sp.wait_ge(s_smm[1], G)
            sp.dma_start(w1s, W1.rearrange("e d f -> d e f")).then_inc(s_moe, 16)
            for e in range(NX):
                sp.dma_start(w2s[:, e, :, :], W2[e].rearrange("(c p) d -> p c d", p=P)).then_inc(s_moe, 16)
            sp.dma_start(b2bc, b2.rearrange("e d -> (e d)").partition_broadcast(P)).then_inc(s_moe, 16)
            rows_t = rows.rearrange("(t p) w -> p t w", p=P)
            with sp.Fori(0, G) as i:
                sp.wait_ge(s_xn2, i + 1)
                sp.dma_start(rows_t[:, bass.ds(i * GB, GB), :], xall[:, bass.ds(i * GB, GB), :]).then_inc(s_rows, 16)
            sp.wait_ge(s_rows, 16 * G)

        @block.gpsimd
        def _(pool):
            pool.memset(ident[:, :], 0.0).then_inc(s_cc, 1)
            pool.memset(ident_b[:, :], 0.0).then_inc(s_cc, 1)
            pool.memset(before_b[:, :], 1.0).then_inc(s_cc, 1)
            pool.memset(same_expert[:, :], 0.0).then_inc(s_cc, 1)
            pool.memset(seg[:, :], 1.0).then_inc(s_cc, 1)
            pool.memset(ones[:, :], 1.0).then_inc(s_const, 1)
            pool.memset(ones_b[:, :], 1.0).then_inc(s_const, 1)
            pool.memset(magic[:, :], MAGIC).then_inc(s_const, 1)
            pool.memset(wsum[:, :], 0.0).then_inc(s_const, 1)
            pool.memset(amax[:, :], 0.0).then_inc(s_const, 1)
            for k in range(7):
                pool.memset(inv_counts[:, k:k + 1], 1.0 / COUNTS[k]).then_inc(s_const, 1)
            pool.wait_ge(s_cc, 5)
            for m in (ident, ident_b):
                pool.affine_select(out=m[:, :], in_=m[:, :], compare_op=ALU.not_equal, fill=1.0, base=0,
                                   pattern=[[-1, P]], channel_multiplier=1).then_inc(s_const, 1)
            for k in (D2V, IMG, TXT):
                pool.dma_start(bcol[:, k:k + 1], biases[k].rearrange("(p o) -> p o", o=1)).then_inc(s_small, 16)
            for l in range(2):
                for twice in range(2):
                    pool.dma_start(bcol[KV * twice:KV * twice + KV, ATT0 + l:ATT0 + l + 1],
                                   biases[ATT0 + l].rearrange("(p o) -> p o", o=1)).then_inc(s_small, 16)
                    pool.dma_start(batt[:, l, twice, :], biases[ATT0 + l].partition_broadcast(P)).then_inc(s_small, 16)
            for c in range(NC):
                pool.dma_start(bcol[:, 5 + c:6 + c], biases[F1][P * c:P * c + P].rearrange("(p o) -> p o", o=1)
                               ).then_inc(s_small, 16)
            pool.dma_start(bf2[:, :], biases[F2].partition_broadcast(P)).then_inc(s_small, 16)
            pool.dma_start(small_w[0:NX, :], router_w).then_inc(s_small, 16)
            pool.dma_start(small_w[NX:, :], b1.rearrange("e (c p) -> (e c) p", p=P)).then_inc(s_small, 16)
            pool.affine_select(out=before_b[:, :], in_=before_b[:, :], compare_op=ALU.is_gt, fill=0.0, base=0,
                               pattern=[[1, P]], channel_multiplier=-1).then_inc(s_const, 1)
            v = same_expert[:, :].rearrange("p (a e) -> p a e", e=NX)
            for d in range(-(P // NX) + 1, P // NX):
                pool.affine_select(out=same_expert[:, :], in_=same_expert[:, :], compare_op=ALU.not_equal, fill=1.0,
                                   base=NX * d, pattern=[[-1, P]], channel_multiplier=1).then_inc(s_cc, 1)
                pool.wait_ge(s_cc, 5 + d + P // NX)
            segv = seg[:, :].rearrange("p (e t) -> p e t", e=NX)
            pool.memset(segv[:, :, 0:1], 0.0).then_inc(s_const, 1)
            for k in range(KEY_BITS):
                pool.memset(steps[:, k:k + 1], 2.0 ** -k).then_inc(s_const, 1)
            for e in range(NX):
                pool.memset(rank8[:, e:e + 1], float(NX - e)).then_inc(s_const, 1)
            pool.iota(tile_no[:, :], pattern=[[1, NT]], base=0, channel_multiplier=0,
                      allow_small_or_imprecise_dtypes=True).then_inc(s_const, 1)
            pool.iota(tile_no_b[:, :], pattern=[[1, NT]], base=0, channel_multiplier=0,
                      allow_small_or_imprecise_dtypes=True).then_inc(s_const, 1)
            pool.iota(row_no_b[:, :], pattern=[[1, P]], base=0, channel_multiplier=0,
                      allow_small_or_imprecise_dtypes=True).then_inc(s_const, 1)
            pool.iota(part_no[:, :], pattern=[[0, 1]], base=0, channel_multiplier=1,
                      allow_small_or_imprecise_dtypes=True).then_inc(s_const, 1)
            pool.iota(turn_no[:, :], pattern=[[1, B]], base=1, channel_multiplier=0,
                      allow_small_or_imprecise_dtypes=True).then_inc(s_const, 1)

            pool.wait_ge(s_small, 16 * 18)

            def bias(l, i):
                pool.wait_ge(s_kev[l], i + 1)
                pool.tensor_tensor(ktok[l][:, :, :], ktok[l][:, :, :],
                                   batt[0:CT, l, :, :].rearrange("p a k -> p (a k)").unsqueeze(1).to_broadcast([CT, GB, P]),
                                   ALU.add).then_inc(s_kt[l], 1)

            def norm(l, i):
                pool.wait_ge(s_r[l], i + 1)
                pool.tensor_tensor(prob[l][:, :, :], prob[l][:, :, :],
                                   arec[:, l, :].unsqueeze(2).to_broadcast([P, GB, CT]), ALU.mult).then_inc(s_p[l], 1)

            def residual(i):
                pool.tensor_tensor(xall[:, bass.ds(i * GB, GB), 0:E], xall[:, bass.ds(i * GB, GB), 0:E],
                                   bf2[:, :].unsqueeze(1).to_broadcast([P, GB, E]), ALU.add).then_inc(s_res, 1)

            pool.wait_ge(s_xs, 1)
            bias(0, 0)
            norm(0, 0)
            residual(0)
            def both(i):
                bias(1, i - 1)
                bias(0, i)
                norm(1, i - 1)
                norm(0, i)
                residual(i)

            both(1)
            with pool.Fori(2, G) as i:
                both(i)
            bias(1, G - 1)
            norm(1, G - 1)

            out_rows = out.rearrange("b s e -> (b s) e")
            pool.wait_ge(s_idx, 3)
            pool.wait_ge(s_rows, 16 * G)

            def take_indices(r, n, mine, all_, moved, copied):
                for k in range(COPY):
                    wait_alone(pool, moved[n + k], r * 16, s_passed)
                pool.tensor_copy(mine[:, n:n + COPY], all_[:, bass.ds(r * RING + n, COPY)]).then_inc(copied, 1)
                wait_alone(pool, copied, r * (RING // COPY) + (n // COPY + 1), s_passed)

            def gather(r, n):
                if n % COPY == 0:
                    take_indices(r, n, idx_in, src_of, s_g, s_ixi)
                wait_alone(pool, s_prep, (r - 1) * RING + (n + 1), s_passed)
                pool.indirect_dma_start(xg[n], None, rows, bass.IndirectOffsetOnAxis(ap=idx_in[:, n:n + 1], axis=0)
                                        ).then_inc(s_g[n], 16)

            def scatter(r, n):
                if n % COPY == 0:
                    take_indices(r, n, idx_out, dst_of, s_o, s_ixo)
                wait_alone(pool, s_y, r * RING + (n + 1), s_passed)
                pool.indirect_dma_start(out_rows, bass.IndirectOffsetOnAxis(ap=idx_out[:, n:n + 1], axis=0), y[n], None,
                                        bounds_check=T - 1, oob_is_err=False).then_inc(s_o[n], 16)

            def both(r, n):
                gather(r, n)
                scatter(r + (n - LAG) // RING, (n - LAG) % RING)

            for a in range(LAG):
                gather(a // RING, a % RING)
            for a in range(LAG, 3 * RING):
                both(a // RING, a % RING)
            with pool.Fori(3, NT // RING) as r:
                for n in range(RING):
                    both(r, n)
            for a in range(NT - LAG, NT):
                scatter(a // RING, a % RING)
            for n in range(RING):
                pool.wait_ge(s_o[n], 16 * (NT // RING))

        @block.scalar
        def _(act):
            def linear(src_bank, dst, k, b):
                return act.activation(dst, src_bank, ACT.Identity, bias=bcol[:, b:b + 1], scale=scale[:, k:k + 1])

            act.wait_ge(s_wtr, 1)
            act.copy(wT[0:DC, 0:P], bank_b(0)[0:DC, 0:P]).then_inc(s_wT, 1)
            act.copy(wT[:, P:3 * P], bank_b(0)[:, P:3 * P]).then_inc(s_wT, 1)
            act.copy(attT[:, :, :, :], bank_b(0)[:, 3 * P:4 * P].rearrange("p (l k) -> p l k", l=2)
                     .unsqueeze(2).to_broadcast([P, 2, 2, KV])).then_inc(s_wT, 1)
            act.wait_ge(s_wtr, 2)
            act.copy(f1T[:, :, :], bank_b(1).rearrange("p (h f) -> p h f", h=2)).then_inc(s_wT, 1)
            act.wait_ge(s_wtr, 3)
            act.copy(f2T[:, :, :], bank_b(2)[:, 0:FF].rearrange("p (c d) -> p c d", c=NC)).then_inc(s_wT, 1)
            act.wait_ge(s_wtr, 4)
            act.copy(small_wT[:, :], bank(7, NX + NX * NC)).then_inc(s_wT, 1)
            qa_v = qa[0:DC, :].rearrange("d (p j) -> d j p", j=CJ)
            with act.Fori(0, CJ // 4) as r:
                for n in range(2):
                    act.wait_ge(s_tr, r * 2 + n + 1)
                    act.copy(qa_v[:, bass.ds(r * 4 + n * 2, 2), :],
                             bank_b(3 + n)[0:DC, 0:2 * CP].rearrange("d (j p) -> d j p", j=2)).then_inc(s_trc, 1)

            def linears(first, dst, k, b):
                with act.Fori(0, G // 2) as r:
                    for n in range(2):
                        act.wait_ge(s_mm, r * 2 + (first + n + 1))
                        linear(bank(5 + n, GC), dst[:, bass.ds(r * 2 * GC + n * GC, GC)], k, b).then_inc(s_mmc, 1)

            act.wait_ge(s_small, 16 * 18)
            act.wait_ge(s_sc, 1)
            linears(0, feat, D2V, D2V)
            act.wait_ge(s_var, 1)
            act.activation(tmp[:, 3, :], tmp[:, 2, :], ACT.Sqrt).then_inc(s_std, 1)
            act.wait_ge(s_sc, 2)
            act.wait_ge(s_vq, 1)
            linears(G, feat, IMG, IMG)
            act.wait_ge(s_inv, Q_X + 1)
            for n in range(4):
                part_ = big[:, n * T // 4:(n + 1) * T // 4]
                act.activation(part_, part_, ACT.Identity, bias=magic[:, :], scale=inv[:, Q_X:Q_X + 1]).then_inc(s_xs, 1)
            act.wait_ge(s_sc, 4)
            for l in range(2):
                linears((2 + l) * G, kT[:, l, :], ATT0 + l, ATT0 + l)

            def keys_out(l, i):
                act.wait_ge(s_kmm[l], i + 1)
                wait(act, s_av[l], i)
                act.activation(ktok[l][:, :, :], bank(5 + l, 512, CT).rearrange("p (b k) -> p b k", b=GB),
                               ACT.Copy, scale=scale[0:CT, ATT0 + l:ATT0 + l + 1]).then_inc(s_kev[l], 1)

            def fused_out(i):
                act.wait_ge(s_fmm, i + 1)
                wait(act, s_up[0], i)
                linear(bank(0), fused0[:, :], TXT, TXT).then_inc(s_f, 1)

            def exp(l, i):
                act.wait_ge(s_sub[l], i + 1)
                act.activation(prob[l][:, :, :], prob[l][:, :, :], ACT.Exp, scale=float(E) ** -0.5).then_inc(s_e[l], 1)

            def probs_out(l, i):
                act.wait_ge(s_t[l], i + 1)
                wait(act, s_av[l], i)
                act.copy(probT[l][:, :], bank(3 + l, 512, CT)).then_inc(s_pt[l], 1)

            fused_out(0)
            keys_out(0, 0)
            exp(0, 0)
            probs_out(0, 0)
            def both(i):
                fused_out(i)
                keys_out(1, i - 1)
                keys_out(0, i)
                exp(1, i - 1)
                exp(0, i)
                probs_out(1, i - 1)
                probs_out(0, i)

            both(1)
            with act.Fori(2, G) as i:
                both(i)
            keys_out(1, G - 1)
            exp(1, G - 1)
            probs_out(1, G - 1)

            act.wait_ge(s_inv, Q_CAT + 1)
            with act.Fori(0, 8) as r:
                part_ = big[:, bass.ds(r * (T // 8), T // 8)]
                act.activation(part_, part_, ACT.Identity, bias=magic[:, :], scale=inv[:, Q_CAT:Q_CAT + 1]).then_inc(s_cs, 1)

            act.wait_ge(s_sc, 6)

            def relu(i, c):
                act.wait_ge(s_h2, i * 2 + c // 2 + 1)
                act.activation(u[:, c, :], bank(c), ACT.Relu, bias=h_bias[:, c:c + 1],
                               scale=h_scale[:, :]).then_inc(s_relu, 1)

            def sqrt2(i):
                act.wait_ge(s_var2, i + 1)
                act.activation(tmp[:, 3, 0:GB], tmp[:, 2, 0:GB], ACT.Sqrt).then_inc(s_std2, 1)

            def x2T_out(i):
                act.wait_ge(s_x2t, i + 1)
                wait(act, s_lg, i)
                act.copy(xsT, bank(5)).then_inc(s_x2c, 1)

            for c in range(NC):
                relu(0, c)
            def both(i):
                act.wait_ge(s_hq, i)
                relu(i, 0)
                sqrt2(i - 1)
                relu(i, 1)
                relu(i, 2)
                relu(i, 3)
                x2T_out(i - 1)

            both(1)
            with act.Fori(2, G) as i:
                both(i)
            sqrt2(G - 1)
            x2T_out(G - 1)

            act.wait_ge(s_d, 1)
            act.activation(route(0), route(0), ACT.Exp).then_inc(s_ex, 1)

            def gathered_out(a, n):
                act.wait_ge(s_gt, a + 1)
                wait(act, s_l1, a - (DEPTH - 1))
                act.copy(gT[n % DEPTH], bank(n % 2, P)).then_inc(s_gc, 1)

            def hidden_out(a, n):
                act.wait_ge(s_l1, a + 1)
                wait(act, s_l2, a - (DEPTH - 1))
                for c in range(NC - 1):
                    m = act.activation(hT[n % DEPTH][:, P * c:P * c + P], bank(2 + n % 2)[:, P * c:P * c + P],
                                       ACT.Relu, bias=b1_now[n % DEPTH][:, c:c + 1])
                m.then_inc(s_hc, 1)

            gathered_out(0, 0)
            gathered_out(1, 1)
            for a in range(RING):
                gathered_out(a + 2, a + 2)
                hidden_out(a, a)
            with act.Fori(1, NT // RING - 1) as r:
                for n in range(RING):
                    gathered_out(r * RING + (n + 2), n + 2)
                    hidden_out(r * RING + n, n)
            for a in range(NT - RING, NT):
                if a + 2 < NT:
                    gathered_out(a + 2, a + 2)
                hidden_out(a, a)

        @block.tensor
        def _(pe):
            pe.sem_inc(s_trc, 2)
            pe.sem_inc(s_mmc, 2)

            def spread_max(k):
                pe.wait_ge(s_amax, k + 1)
                pe.transpose(psum[0:1, 7, 0:P], amax[:, k:k + 1], ident[:, :]).then_inc(s_grow, 1)
                pe.wait_ge(s_gm, k + 1)
                pe.matmul(psum[:, 7, P + k:P + k + 1], ones[0:1, :], gmax[0:1, k:k + 1],
                          start=True, stop=True).then_inc(s_gcol, 1)

            pe.wait_ge(s_const, 14)
            pe.wait_ge(s_wsum, 7)
            pe.matmul(bank(6, 7), ones[:, :], wsum[:, :], start=True, stop=True).then_inc(s_wtot, 1)
            spread_max(Q_CTX)
            pe.wait_ge(s_wq, 7)
            for k in (D2V, IMG, TXT):
                pe.transpose(bank_b(0)[0:WIDTHS[k], P * k:P * k + P], wslice(wq, k), ident_b[:, :])
            pe.transpose(bank_b(0)[:, 3 * P:3 * P + KV], wslice(wq, ATT0), ident_b[0:KV, 0:KV])
            pe.transpose(bank_b(0)[:, 3 * P + KV:4 * P], wslice(wq, ATT1), ident_b[0:KV, 0:KV]).then_inc(s_wtr, 1)
            f1q = wslice(wq, F1).rearrange("p (c h i) -> p c h i", c=NC, h=2)
            for c in range(NC):
                for h in range(2):
                    m = pe.transpose(bank_b(1)[:, h * FF + c * P:h * FF + c * P + P], f1q[:, c, h, :], ident_b[:, :])
            m.then_inc(s_wtr, 1)
            f2q = wslice(wq, F2).rearrange("p (c i) -> p c i", c=NC)
            for c in range(NC):
                m = pe.transpose(bank_b(2)[:, c * P:c * P + P], f2q[:, c, :], ident_b[:, :])
            m.then_inc(s_wtr, 1)
            pe.wait_ge(s_small, 16 * 18)
            pe.wait_ge(s_inv, 1)
            pe.transpose(bank(7, NX + NX * NC), small_w[:, :], ident[0:NX + NX * NC, 0:NX + NX * NC]).then_inc(s_wtr, 1)

            pe.wait_ge(s_cq, 1)
            cq = ctx_q.rearrange("p (j d) -> p j d", j=CJ)
            with pe.Fori(0, CJ // 4) as r:
                for n in range(2):
                    pe.wait_ge(s_trc, r * 2 + n + 1)
                    for j in range(2):
                        m = pe.transpose(bank_b(3 + n)[0:DC, CP * j:CP * j + CP],
                                         cq[:, bass.ds(r * 4 + (n * 2 + j), 1), :].rearrange("p j d -> p (j d)"),
                                         ident_b[0:CP, 0:CP])
                    m.then_inc(s_tr, 1)
            n_ctx = CJ // 2

            def linears(first, w, src):
                with pe.Fori(0, G // 2) as r:
                    for n in range(2):
                        pe.wait_ge(s_mmc, r * 2 + (first + n + 1))
                        pe.matmul(bank(5 + n, GC), w, src[:, bass.ds(r * 2 * GC + n * GC, GC)],
                                  start=True, stop=True).then_inc(s_mm, 1)

            pe.wait_ge(s_wT, 6)
            pe.wait_ge(s_trc, n_ctx + 2)
            linears(0, wT[0:DC, 0:P], qa[0:DC, :])
            spread_max(Q_VIS)
            pe.wait_ge(s_vq, 1)
            linears(G, wT[:, P:2 * P], qb)
            spread_max(Q_IMG)
            spread_max(Q_X)
            pe.wait_ge(s_iq, 1)
            for l in range(2):
                linears((2 + l) * G, attT[:, l, :, :].rearrange("p a k -> p (a k)"), qa)
            pe.wait_ge(s_xq, 4)
            with pe.Fori(0, G // 2) as r:
                for n in range(2):
                    pe.wait_ge(s_trc, r * 2 + (n_ctx + n + 1))
                    for j in range(GB):
                        m = pe.transpose(bank_b(3 + n)[:, P * j:P * j + P],
                                         tok_b[:, bass.ds(r * 2 * GT + (n * GT + j * P), P)], ident_b[:, :])
                    m.then_inc(s_tr, 1)

            def key_tokens(l, i):
                wait(pe, s_up[l], i)
                for b in range(GB):
                    m = pe.matmul(bank(5 + l, 512, CT)[:, P * b:P * b + P], qa[:, bass.ds(i * GC + b * CT, CT)],
                                  attT[:, l, :, :].rearrange("p a k -> p (a k)"), start=True, stop=True)
                m.then_inc(s_kmm[l], 1)

            def project(i):
                wait(pe, s_f, i)
                pe.matmul(bank(0), wT[:, 2 * P:3 * P], xqT[:, g4(i)], start=True, stop=True).then_inc(s_fmm, 1)

            def scores(l, i):
                wait(pe, s_sub[l], i)
                pe.wait_ge(s_f if l == 0 else s_up[0], i + 1)
                src = fused0 if l == 0 else fused1
                for b in range(GB):
                    m = pe.matmul(bank(1 + l)[:, CT * b:CT * b + CT], src[:, P * b:P * b + P],
                                  kT[:, l, bass.ds(i * GC + b * CT, CT)], start=True, stop=True)
                m.then_inc(s_smm[l], 1)

            def turn(l, i):
                pe.wait_ge(s_p[l], i + 1)
                wait(pe, s_pt[l], i)
                for b in range(GB):
                    m = pe.transpose(bank(3 + l, 512, CT)[:, P * b:P * b + P], prob[l][:, b, :], ident[:, :])
                m.then_inc(s_t[l], 1)

            def attend(l, i):
                pe.wait_ge(s_pt[l], i + 1)
                pe.wait_ge(s_kt[l], i + 1)
                for b in range(GB):
                    m = pe.matmul(bank(5 + l)[:, P * b:P * b + P], ktok[l][:, b, :], probT[l][:, P * b:P * b + P],
                                  start=True, stop=True)
                m.then_inc(s_av[l], 1)

            pe.wait_ge(s_trc, n_ctx + G + 2)
            pe.wait_ge(s_mmc, 4 * G + 2)
            project(0)
            key_tokens(0, 0)
            scores(0, 0)
            turn(0, 0)
            attend(0, 0)
            def both(i):
                project(i)
                scores(1, i - 1)
                key_tokens(1, i - 1)
                key_tokens(0, i)
                scores(0, i)
                turn(1, i - 1)
                attend(1, i - 1)
                turn(0, i)
                attend(0, i)

            both(1)
            with pe.Fori(2, G) as i:
                both(i)
            scores(1, G - 1)
            key_tokens(1, G - 1)
            turn(1, G - 1)
            attend(1, G - 1)

            spread_max(Q_CAT)
            pe.wait_ge(s_catq, 9)

            def hidden(i, c):
                pe.matmul(bank(c), f1T[:, 0, P * c:P * c + P], tok_b[:, g4(i)], start=True, stop=False)
                return pe.matmul(bank(c).rearrange("p (b s) -> p b s", b=GB), f1T[:, 1, P * c:P * c + P],
                                 avg_q[:, bass.ds(i * GB, GB)].unsqueeze(2).to_broadcast([P, GB, S]),
                                 start=False, stop=True)

            with pe.Fori(0, G) as i:
                for pair in range(2):
                    pe.wait_ge(s_hm, i * 2 + pair + 1)
                    hidden(i, 2 * pair)
                    hidden(i, 2 * pair + 1).then_inc(s_h, 1)
            spread_max(Q_H)

            def hidden_again(i):
                for pair in range(2):
                    wait(pe, s_relu, i * 4 + (2 * pair - 2))
                    hidden(i, 2 * pair)
                    hidden(i, 2 * pair + 1).then_inc(s_h2, 1)

            def out_product(i):
                pe.wait_ge(s_hq, i + 1)
                wait(pe, s_var2, i)
                for b in range(GB):
                    for c in range(NC):
                        m = pe.matmul(bank(4)[:, P * b:P * b + P], hq[:, c, P * b:P * b + P], f2T[:, c, :],
                                      start=(c == 0), stop=(c == NC - 1))
                m.then_inc(s_f2, 1)

            def turn_x2(i):
                pe.wait_ge(s_xn2, i + 1)
                wait(pe, s_x2c, i)
                for b in range(GB):
                    m = pe.transpose(bank(5)[:, P * b:P * b + P], xs[:, b, :], ident[:, :])
                m.then_inc(s_x2t, 1)

            def logits(i):
                pe.wait_ge(s_x2c, i + 1)
                for b in range(GB):
                    m = pe.matmul(psum[:, 6, bass.ds(i * GB * NX + b * NX, NX)], xsT[:, P * b:P * b + P], rwT,
                                  start=True, stop=True)
                m.then_inc(s_lg, 1)

            hidden_again(0)
            def both_again(i):
                out_product(i - 1)
                hidden_again(i)
                turn_x2(i - 1)
                logits(i - 1)

            both_again(1)
            with pe.Fori(2, G) as i:
                both_again(i)
            out_product(G - 1)
            turn_x2(G - 1)
            logits(G - 1)

            pe.wait_ge(s_v, 1)
            for n in range(4):
                m = pe.transpose(bank(0)[:, P * n:P * n + P], route(2)[:, P * n:P * n + P], ident[:, :])
            m.then_inc(s_vt, 1)
            with pe.Fori(0, KEY_BITS) as k:
                pe.wait_ge(s_cnt, k + 1)
                pe.matmul(bank(1, 1), same_expert[:, :], cnt[:, :], start=True, stop=True).then_inc(s_cnt2, 1)
            pe.wait_ge(s_thr, 1)
            pe.transpose(psum[0:1, 2, 0:P], thr[:, :], ident[:, :]).then_inc(s_thr_r, 1)
            pe.wait_ge(s_thr_c, 1)
            pe.matmul(bank(3, NX), ones[0:1, :], t64[0][0:1, 0:NX], start=True, stop=True).then_inc(s_thr_s, 1)
            above, ties, final = (tok_b[:, n * 512:(n + 1) * 512] for n in range(3))
            pe.wait_ge(s_ms, 1)
            pe.matmul(bank(4), ones_b[:, :], above, start=True, stop=True)
            pe.matmul(bank(5), ones_b[:, :], ties, start=True, stop=True)
            pe.matmul(bank(6), before_b[:, :], ties, start=True, stop=True).then_inc(s_ps, 1)
            pe.wait_ge(s_ms, 2)
            pe.matmul(bank(0), ones_b[:, :], final, start=True, stop=True)
            pe.matmul(bank(1), before_b[:, :], final, start=True, stop=True).then_inc(s_ps, 1)
            def place(r, n, start=False, stop=False):
                pe.wait_ge(s_hot, r + 1)
                pe.matmul(bank(2, 2 * NT), hot_row[n][:, :], hot_tile[n][:, :, :].rearrange("p a t -> p (a t)"),
                          start=start, stop=stop).then_inc(s_inv_mm, 1)
            place(0, 0, start=True)
            place(1, 1)
            with pe.Fori(1, B // 2 - 1) as r:
                for n in range(2):
                    place(r * 2 + n, n)
            place(B - 2, 0)
            place(B - 1, 1, stop=True)

            pe.wait_ge(s_idx, 3)
            pe.wait_ge(s_moe, 16 * 10)

            def turn_rows(a, n):
                pe.wait_ge(s_prep, a + 1)
                wait(pe, s_gc, a - 1)
                pe.transpose(bank(n % 2, P), gn[n % DEPTH], ident[:, :]).then_inc(s_gt, 1)

            def layer1(a, n):
                pe.wait_ge(s_gc, a + 1)
                wait(pe, s_hc, a - 1)
                wait(pe, s_hd, a - 1)
                for c in range(NC):
                    dst = bank(2 + n % 2)[:, P * c:P * c + P] if c < NC - 1 else bank(6 + n % 2, P)
                    m = pe.matmul(dst, w1_now[n % DEPTH][:, P * c:P * c + P], gT[n % DEPTH], start=True, stop=True)
                m.then_inc(s_l1, 1)

            def layer2(a, n):
                e = pe.value_load(expert_of[0:1, bass.ds(a, 1)], min_val=0, max_val=NX - 1)
                pe.wait_ge(s_hc, a + 1)
                pe.wait_ge(s_hd, a + 1)
                wait(pe, s_y, a - 1)
                for c in range(NC):
                    m = pe.matmul(bank(4 + n % 2, E), hT[n % DEPTH][:, P * c:P * c + P],
                                  w2s[:, bass.ds(e, 1), c, :].rearrange("p e d -> p (e d)"),
                                  start=(c == 0), stop=(c == NC - 1))
                m.then_inc(s_l2, 1)

            turn_rows(0, 0)
            turn_rows(1, 1)
            for a in range(RING):
                turn_rows(a + 2, a + 2)
                layer1(a, a)
                if a >= 2:
                    layer2(a - 2, a - 2)
            with pe.Fori(1, NT // RING - 1) as r:
                for n in range(RING):
                    turn_rows(r * RING + (n + 2), n + 2)
                    layer1(r * RING + n, n)
                    layer2(r * RING + (n - 2), n - 2)
            for a in range(NT - RING, NT + 2):
                if a + 2 < NT:
                    turn_rows(a + 2, a + 2)
                if a < NT:
                    layer1(a, a)
                layer2(a - 2, a - 2)

        @block.vector
        def _(dve):
            ch = Chain(dve, s_dve)

            def do(ins):
                ch.link(ins)
                ch.join()

            def global_scale(k, uses):
                dve.wait_ge(s_grow, k + 1)
                dve.tensor_reduce(gmax[0:1, k:k + 1], psum[0:1, 7, 0:P], AX, ALU.max).then_inc(s_gm, 1)
                dve.wait_ge(s_gcol, k + 1)
                do(dve.tensor_scalar(iscale[:, k:k + 1], psum[:, 7, P + k:P + k + 1], 1e-8, 1.0 / 127.0, ALU.max, ALU.mult))
                dve.reciprocal(inv[:, k:k + 1], iscale[:, k:k + 1]).then_inc(s_inv, 1)
                for w in uses:
                    ins = dve.tensor_tensor(scale[:, w:w + 1], ws[:, w:w + 1], iscale[:, k:k + 1], ALU.mult)
                    if w == uses[-1]:
                        ins.then_inc(s_sc, 1)
                dve.wait_ge(s_inv, k + 1)

            def layer_norm_stats(st, mean, n, done):
                me, m2e, mo, m2o = (st[:, :, j] for j in (1, 2, 4, 5))
                a, b_, v = tmp[:, 0, 0:n], tmp[:, 1, 0:n], tmp[:, 2, 0:n]
                ch.link(dve.tensor_tensor(a, me, mo, ALU.add))
                ch.link(dve.tensor_tensor(b_, me, mo, ALU.subtract))
                ch.link(dve.tensor_tensor(v, m2e, m2o, ALU.add))
                ch.join()
                ch.link(dve.tensor_scalar(mean, a, 0.5, None, ALU.mult))
                do(dve.tensor_tensor(b_, b_, b_, ALU.mult))
                do(dve.scalar_tensor_tensor(v, b_, float(E) / 4, v, ALU.mult, ALU.add))
                dve.tensor_scalar(v, v, 1.0 / E, EPS, ALU.mult, ALU.add).then_inc(done, 1)

            dve.wait_ge(s_const, 12)
            dve.wait_ge(s_w, 16 * 7)
            for k in range(7):
                rows_ = KV if k in (ATT0, ATT1) else P
                dve.tensor_reduce(wsum[0:rows_, k:k + 1], wslice(wraw, k), AX, ALU.add,
                                  apply_absolute_value=True).then_inc(s_wsum, 1)
            dve.wait_ge(s_ctx, 16)
            dve.tensor_reduce(amax[0:CP, Q_CTX:Q_CTX + 1], ctx_raw[0:CP, 0:CJ * DC], AX, ALU.max,
                              apply_absolute_value=True).then_inc(s_amax, 1)
            dve.wait_ge(s_wtot, 1)
            do(dve.tensor_tensor(ws[:, :], bank(6, 7), inv_counts[:, :], ALU.mult))
            do(dve.tensor_scalar(ws[:, :], ws[:, :], 1e-5, None, ALU.max))
            global_scale(Q_CTX, [D2V])
            ch.link(dve.tensor_scalar(wlim[:, 0, :], ws[:, :], 0.5, None, ALU.mult))
            do(dve.tensor_scalar(wlim[:, 1, :], ws[:, :], -0.5, None, ALU.mult))
            do(dve.tensor_scalar(ctx_raw[0:CP, 0:CJ * DC], ctx_raw[0:CP, 0:CJ * DC], inv[0:CP, Q_CTX:Q_CTX + 1], MAGIC,
                                 ALU.mult, ALU.add))
            dve.tensor_scalar(ctx_q, ctx_raw[0:CP, 0:CJ * DC], MAGIC, None, ALU.subtract).then_inc(s_cq, 1)
            for k in range(7):
                rows_ = KV if k in (ATT0, ATT1) else P
                ch.link(dve.tensor_scalar(wslice(wneg, k), wslice(wraw, k), wlim[0:rows_, 1, k:k + 1], None, ALU.is_lt))
            ch.join()
            for k in range(7):
                rows_ = KV if k in (ATT0, ATT1) else P
                dve.scalar_tensor_tensor(wslice(wq, k), wslice(wraw, k), wlim[0:rows_, 0, k:k + 1], wslice(wneg, k),
                                         ALU.is_gt, ALU.subtract).then_inc(s_wq, 1)

            for n in range(8):
                dve.wait_ge(s_x[n], 16)
                with dve.Fori(0, 2) as r:
                    for j in range(4):
                        t = r * 4 + (8 * n + j)
                        m = dve.bn_stats(stats[:, bass.ds(t, 1), :].rearrange("p t s -> p (t s)"),
                                         xall[:, bass.ds(t, 1), 0:E].rearrange("p t d -> p (t d)"))
                        ch.link(m)
                    ch.count -= 4
                ch.count += 8
            ch.join()
            layer_norm_stats(stats[:, :, :], xall[:, :, E], B, s_var)

            def maxima(first, src, p):
                with dve.Fori(0, G) as i:
                    dve.wait_ge(s_mmc, i + (first + 2 + 1))
                    ch.link(dve.tensor_reduce(part[:, p, bass.ds(i, 1)], src[:, c4(i)], AX, ALU.max,
                                              apply_absolute_value=True))
                ch.count += G - 1
                ch.join()

            def quantise(dst, src, k, done):
                do(dve.tensor_scalar(src, src, inv[:, k:k + 1], MAGIC, ALU.mult, ALU.add))
                dve.tensor_scalar(dst, src, MAGIC, None, ALU.subtract).then_inc(done, 1)

            maxima(0, feat, 0)
            dve.tensor_reduce(amax[:, Q_VIS:Q_VIS + 1], part[:, 0, 0:G], AX, ALU.max).then_inc(s_amax, 1)
            global_scale(Q_VIS, [IMG])
            quantise(qb[:, :], feat[:, :], Q_VIS, s_vq)

            dve.wait_ge(s_std, 1)
            do(dve.reciprocal(xall[:, :, E + 1], tmp[:, 3, :]))
            with dve.Fori(0, G) as i:
                for b in range(GB):
                    t = i * GB + b
                    row = xall[:, bass.ds(t, 1), :].rearrange("p t d -> p (t d)")
                    ch.link(dve.tensor_scalar(xn[:, bass.ds(t, 1), :].rearrange("p t d -> p (t d)"), row[:, 0:E],
                                              row[:, E:E + 1], row[:, E + 1:E + 2], ALU.subtract, ALU.mult))
            ch.count += GB * (G - 1)
            ch.join()
            do(dve.tensor_reduce(part[:, 1, 0:1], big[:, :], AX, ALU.max, apply_absolute_value=True))

            maxima(G, feat, 0)
            dve.tensor_reduce(amax[:, Q_IMG:Q_IMG + 1], part[:, 0, 0:G], AX, ALU.max).then_inc(s_amax, 1)
            do(dve.tensor_reduce(avg[:, :], feat[:, :].rearrange("p (b c) -> p b c", c=CT), AX, ALU.add))
            do(dve.tensor_scalar(avg[:, :], avg[:, :], 1.0 / CT, None, ALU.mult))
            global_scale(Q_IMG, [ATT0, ATT1])
            quantise(qa[:, :], feat[:, :], Q_IMG, s_iq)

            dve.tensor_copy(amax[:, Q_X:Q_X + 1], part[:, 1, 0:1]).then_inc(s_amax, 1)
            global_scale(Q_X, [TXT])
            for n in range(4):
                dve.wait_ge(s_xs, n + 1)
                dve.tensor_scalar(tok_b[:, n * T // 4:(n + 1) * T // 4], big[:, n * T // 4:(n + 1) * T // 4], MAGIC, None,
                                  ALU.subtract).then_inc(s_xq, 1)
            n_ctx = CJ // 2
            with dve.Fori(0, G // 2) as r:
                for n in range(2):
                    dve.wait_ge(s_tr, r * 2 + (n_ctx + n + 1))
                    dve.tensor_copy(xqT[:, bass.ds(r * 2 * GT + n * GT, GT)], bank_b(3 + n)[:, 0:GT]).then_inc(s_trc, 1)

            def less_max(l, i):
                dve.wait_ge(s_smm[l], i + 1)
                v = bank(1 + l, GC).rearrange("p (b c) -> p b c", b=GB)
                do(dve.tensor_reduce(amx[:, l, :], v, AX, ALU.max))
                wait(dve, s_t[l], i)
                dve.tensor_tensor(prob[l][:, :, :], v, amx[:, l, :].unsqueeze(2).to_broadcast([P, GB, CT]),
                                  ALU.subtract).then_inc(s_sub[l], 1)

            def inverse_sum(l, i):
                dve.wait_ge(s_e[l], i + 1)
                do(dve.tensor_reduce(asum[:, l, :], prob[l][:, :, :], AX, ALU.add))
                dve.reciprocal(arec[:, l, :], asum[:, l, :]).then_inc(s_r[l], 1)

            def update0(i):
                dve.wait_ge(s_av[0], i + 1)
                dve.scalar_tensor_tensor(fused1[:, :], bank(5), 0.1, fused0[:, :], ALU.mult, ALU.add).then_inc(s_up[0], 1)

            def update1(i):
                dve.wait_ge(s_av[1], i + 1)
                dve.scalar_tensor_tensor(big[:, g4(i)], bank(6), 0.1, fused1[:, :], ALU.mult, ALU.add).then_inc(s_up[1], 1)
                dve.wait_ge(s_up[1], i + 1)
                ch.link(dve.tensor_reduce(part[:, 2, bass.ds(i, 1)], big[:, g4(i)], AX, ALU.max,
                                          apply_absolute_value=True))

            less_max(0, 0)
            inverse_sum(0, 0)
            update0(0)

            def body(i):
                less_max(1, i - 1)
                less_max(0, i)
                inverse_sum(1, i - 1)
                inverse_sum(0, i)
                update1(i - 1)
                update0(i)
            body(1)
            ch.loop(2, G, 5, body)
            less_max(1, G - 1)
            inverse_sum(1, G - 1)
            update1(G - 1)

            ch.link(dve.tensor_reduce(part[:, 3, 0:1], avg[:, :], AX, ALU.max, apply_absolute_value=True))
            ch.join()
            do(dve.tensor_reduce(part[:, 3, 1:2], part[:, 2, 0:G], AX, ALU.max))
            dve.tensor_tensor(amax[:, Q_CAT:Q_CAT + 1], part[:, 3, 0:1], part[:, 3, 1:2], ALU.max).then_inc(s_amax, 1)
            global_scale(Q_CAT, [F1])
            quantise(avg_q[:, :], avg[:, :], Q_CAT, s_catq)
            with dve.Fori(0, 8) as r:
                dve.wait_ge(s_cs, r + 1)
                dve.tensor_scalar(tok_b[:, bass.ds(r * (T // 8), T // 8)], big[:, bass.ds(r * (T // 8), T // 8)], MAGIC,
                                  None, ALU.subtract).then_inc(s_catq, 1)

            dve.sem_inc(s_hm, 2)
            hmax = tmp[:, :, :].rearrange("p a b -> p (a b)")[:, 0:G * NC].rearrange("p (g c) -> p g c", c=NC)
            with dve.Fori(0, G) as i:
                for pair in range(2):
                    dve.wait_ge(s_h, i * 2 + pair + 1)
                    dve.tensor_reduce(hmax[:, bass.ds(i, 1), 2 * pair:2 * pair + 2].rearrange("p g c -> p (g c)"),
                                      psum[:, 2 * pair:2 * pair + 2, :], AX, ALU.max).then_inc(s_hm, 1)
            dve.wait_ge(s_hm, 2 * G + 2)
            do(dve.tensor_reduce(part[:, 0, 0:NC], hmax.rearrange("p g c -> p c g"), AX, ALU.max))
            do(dve.scalar_tensor_tensor(part[:, 1, 0:NC], part[:, 0, 0:NC], scale[:, F1:F1 + 1], bcol[:, 5:5 + NC],
                                        ALU.mult, ALU.add))
            do(dve.tensor_scalar(part[:, 1, 0:NC], part[:, 1, 0:NC], 0.0, None, ALU.max))
            dve.tensor_reduce(amax[:, Q_H:Q_H + 1], part[:, 1, 0:NC], AX, ALU.max).then_inc(s_amax, 1)
            dve.wait_ge(s_grow, Q_H + 1)
            dve.tensor_reduce(gmax[0:1, Q_H:Q_H + 1], psum[0:1, 7, 0:P], AX, ALU.max).then_inc(s_gm, 1)
            dve.wait_ge(s_gcol, Q_H + 1)
            do(dve.tensor_scalar(iscale[:, Q_H:Q_H + 1], psum[:, 7, P + Q_H:P + Q_H + 1], 1e-8, 1.0 / 127.0,
                                 ALU.max, ALU.mult))
            do(dve.reciprocal(inv[:, Q_H:Q_H + 1], iscale[:, Q_H:Q_H + 1]))
            ch.link(dve.tensor_tensor(scale[:, F2:F2 + 1], ws[:, F2:F2 + 1], iscale[:, Q_H:Q_H + 1], ALU.mult))
            ch.link(dve.tensor_scalar(h_bias[:, :], bcol[:, 5:5 + NC], inv[:, Q_H:Q_H + 1], None, ALU.mult))
            ch.join()
            dve.tensor_tensor(h_scale[:, :], scale[:, F1:F1 + 1], inv[:, Q_H:Q_H + 1], ALU.mult).then_inc(s_sc, 1)

            def quantise_hidden(i):
                dve.wait_ge(s_relu, (i + 1) * 4)
                dve.tensor_scalar(hq[:, :, :], u[:, :, :], MAGIC, MAGIC, ALU.add, ALU.subtract).then_inc(s_hq, 1)

            def x1_stats(i):
                xr = xall[:, bass.ds(i * GB, GB), :]
                dve.wait_ge(s_f2, i + 1)
                do(dve.scalar_tensor_tensor(xr[:, :, 0:E], bank(4).rearrange("p (b d) -> p b d", b=GB), scale[:, F2:F2 + 1],
                                            xr[:, :, 0:E], ALU.mult, ALU.add))
                dve.sem_inc(s_passed2, 1)
                for b in range(GB):
                    ch.link(dve.bn_stats(stats[:, b, :],
                                         xall[:, bass.ds(i * GB + b, 1), 0:E].rearrange("p t d -> p (t d)")))
                ch.join()
                layer_norm_stats(st2, xr[:, :, E], GB, s_var2)

            def x2(i):
                xr = xall[:, bass.ds(i * GB, GB), :]
                dve.wait_ge(s_std2, i + 1)
                do(dve.reciprocal(xr[:, :, E + 1], tmp[:, 3, 0:GB]))
                wait(dve, s_x2t, i)
                for b in range(GB):
                    row = xall[:, bass.ds(i * GB + b, 1), :].rearrange("p t d -> p (t d)")
                    m = dve.tensor_scalar(xs[:, b, :], row[:, 0:E], row[:, E:E + 1], row[:, E + 1:E + 2],
                                          ALU.subtract, ALU.mult)
                m.then_inc(s_xn2, 1)

            dve.wait_ge(s_res, G)
            quantise_hidden(0)

            def body(i):
                x1_stats(i - 1)
                quantise_hidden(i)
                x2(i - 1)
            body(1)
            ch.loop(2, G, 12, body)
            x1_stats(G - 1)
            x2(G - 1)

            def v3(ap):
                return ap.rearrange("p (t e) -> p t e", e=NX)

            def over_e(ap):
                return ap.unsqueeze(2).to_broadcast([P, B, NX])

            def over_t(ap):
                return ap.unsqueeze(1).to_broadcast([P, B, NX])

            dve.wait_ge(s_lg, G)
            do(dve.tensor_reduce(t64[1][:, :], v3(bank(6)), AX, ALU.max))
            dve.tensor_tensor(v3(route(0)), v3(bank(6)), over_e(t64[1][:, :]), ALU.subtract).then_inc(s_d, 1)
            dve.wait_ge(s_ex, 1)
            do(dve.tensor_reduce(t64[1][:, :], v3(route(0)), AX, ALU.add))
            do(dve.reciprocal(t64[2][:, :], t64[1][:, :]))
            do(dve.tensor_tensor(v3(route(0)), v3(route(0)), over_e(t64[2][:, :]), ALU.mult))
            top = t64[3][:, :]
            do(dve.tensor_reduce(top, v3(route(0)), AX, ALU.max))
            do(dve.tensor_tensor(v3(route(0)), v3(route(0)), over_e(top), ALU.is_equal))
            do(dve.tensor_tensor(v3(route(0)), v3(route(0)), over_t(rank8[:, :]), ALU.mult))
            do(dve.tensor_reduce(t64[2][:, :], v3(route(0)), AX, ALU.max))
            do(dve.tensor_tensor(v3(route(1)), v3(route(0)), over_e(t64[2][:, :]), ALU.is_equal))
            dve.tensor_tensor(v3(route(2)), v3(route(1)), over_e(top), ALU.mult).then_inc(s_v, 1)
            dve.wait_ge(s_vt, 1)
            ch.link(dve.tensor_copy(route(3), bank(0)))
            ch.link(dve.memset(thr[:, :], 0.0))
            ch.link(dve.memset(cand[:, :], 1.0))
            ch.join()

            def body(k):
                dve.tensor_scalar(route(4), route(3), cand[:, :], None, ALU.is_ge, ALU.add,
                                  accum_out=cnt[:, :]).then_inc(s_cnt, 1)
                dve.wait_ge(s_cnt2, k + 1)
                do(dve.tensor_scalar(acc[:, :], bank(1, 1), float(CAP), steps[:, bass.ds(k, 1)], ALU.is_ge, ALU.mult))
                do(dve.tensor_tensor(thr[:, :], thr[:, :], acc[:, :], ALU.add))
                do(dve.scalar_tensor_tensor(cand[:, :], steps[:, bass.ds(k, 1)], 0.5, thr[:, :], ALU.mult, ALU.add))
            ch.loop(0, KEY_BITS, 3, body)
            dve.tensor_copy(thr[:, :], thr[:, :]).then_inc(s_thr, 1)
            dve.wait_ge(s_thr_r, 1)
            dve.tensor_copy(t64[0][0:1, 0:NX], psum[0:1, 2, 0:NX]).then_inc(s_thr_c, 1)
            dve.wait_ge(s_thr_s, 1)
            do(dve.tensor_copy(thr8[:, :], bank(3, NX)))

            above, ties, final = (tok_b[:, n * 512:(n + 1) * 512] for n in range(3))
            ch.link(dve.tensor_tensor(v3(above), v3(route(2)), over_t(thr8[:, :]), ALU.is_gt))
            do(dve.tensor_tensor(v3(route(0)), v3(route(2)), over_t(thr8[:, :]), ALU.is_equal))
            dve.tensor_tensor(v3(ties), v3(route(0)), v3(route(1)), ALU.mult).then_inc(s_ms, 1)

            def et(ap):
                return ap.rearrange("p (e t) -> p t e", e=NX)

            def te(ap):
                return ap.rearrange("p (t e) -> p e t", e=NX)

            def earlier(columns, rows_, own, full):
                do(dve.tensor_copy(et(own), v3(columns)))
                do(dve.tensor_tensor_scan(full, seg[:, :], own, 0.0, ALU.mult, ALU.add))
                do(dve.tensor_tensor(own, full, own, ALU.subtract))
                do(dve.tensor_tensor(v3(route(7)), et(own), v3(rows_), ALU.add))

            dve.wait_ge(s_ps, 1)
            do(dve.tensor_reduce(n8[0][:, :], te(bank(4)), AX, ALU.add))
            do(dve.tensor_scalar(n8[1][:, :], n8[0][:, :], -1.0, float(CAP), ALU.mult, ALU.add))
            earlier(bank(5), bank(6), route(5), route(6))
            do(dve.tensor_tensor(v3(route(7)), v3(route(7)), over_t(n8[1][:, :]), ALU.is_lt))
            do(dve.tensor_tensor(route(7), route(7), ties, ALU.mult))
            do(dve.tensor_tensor(route(7), route(7), above, ALU.add))
            do(dve.tensor_reduce(t64[1][:, :], v3(route(7)), AX, ALU.add))
            do(dve.tensor_scalar(t64[1][:, :], t64[1][:, :], -1.0, 1.0, ALU.mult, ALU.add))
            do(dve.tensor_tensor(v3(route(7))[:, :, 0], v3(route(7))[:, :, 0], t64[1][:, :], ALU.add))
            do(dve.tensor_copy(route(8), route(7)))
            dve.tensor_copy(final, route(7)).then_inc(s_ms, 1)

            dve.wait_ge(s_ps, 2)
            earlier(bank(0), bank(1), route(5), route(6))
            do(dve.tensor_copy(n8[0][:, :], route(6).rearrange("p (e t) -> p e t", e=NX)[:, :, B - 1]))
            do(dve.tensor_scalar(n8i[0][:, :], n8[0][:, :], float(P - 1), None, ALU.add))
            do(dve.tensor_scalar(n8i[1][:, :], n8i[0][:, :], 7, None, ALU.arith_shift_right))
            do(dve.tensor_copy(n8[1][:, :], n8i[1][:, :]))
            do(dve.tensor_tensor_scan(n8[2][:, :], ones[:, 0:NX], n8[1][:, :], 0.0, ALU.mult, ALU.add))
            do(dve.tensor_tensor(n8[3][:, :], n8[2][:, :], n8[1][:, :], ALU.subtract))
            do(dve.tensor_scalar(n8[3][:, :], n8[3][:, :], float(P), None, ALU.mult))
            do(dve.tensor_tensor(v3(route(7)), v3(route(7)), over_t(n8[3][:, :]), ALU.add))
            do(dve.tensor_tensor(route(7), route(7), route(8), ALU.mult))
            do(dve.tensor_reduce(t64[1][:, :], v3(route(7)), AX, ALU.add))
            do(dve.tensor_copy(t64i[0][:, :], t64[1][:, :]))
            ch.link(dve.tensor_scalar(t64i[1][:, :], t64i[0][:, :], 7, None, ALU.arith_shift_right))
            ch.link(dve.tensor_scalar(t64i[2][:, :], t64i[0][:, :], P - 1, None, ALU.bitwise_and))
            ch.join()
            ch.link(dve.tensor_copy(t64[4][:, :], t64i[1][:, :]))
            ch.link(dve.tensor_copy(t64[5][:, :], t64i[2][:, :]))
            ch.join()

            def one_hots(t, n):
                wait(dve, s_inv_mm, t - 1)
                tile_ = t64[4][:, bass.ds(t, 1)]
                ch.link(dve.tensor_scalar(hot_row[n][:, :], row_no_b[:, :], t64[5][:, bass.ds(t, 1)], None, ALU.is_equal))
                ch.link(dve.tensor_scalar(hot_tile[n][:, 0, :], tile_no_b[:, :], tile_, part_no[:, :],
                                          ALU.is_equal, ALU.mult))
                ch.join()
                dve.tensor_scalar(hot_tile[n][:, 1, :], tile_no_b[:, :], tile_, turn_no[:, bass.ds(t, 1)],
                                  ALU.is_equal, ALU.mult).then_inc(s_hot, 1)

            one_hots(0, 0)
            one_hots(1, 1)

            def body(r):
                for n in range(2):
                    one_hots(r * 2 + n, n)
            ch.loop(1, B // 2, 4, body)

            m = big[0:1, 10 * 512:10 * 512 + NT * NX].rearrange("p (a e) -> p a e", e=NX)
            do(dve.tensor_tensor(m, tile_no[0:1, :].unsqueeze(2).to_broadcast([1, NT, NX]),
                                 n8[2][0:1, :].unsqueeze(1).to_broadcast([1, NT, NX]), ALU.is_ge))
            m2 = big[0:1, 12 * 512:12 * 512 + NT]
            do(dve.tensor_reduce(m2, m, AX, ALU.add))
            dve.tensor_scalar(expert_of[:, :], m2, float(NX - 1), None, ALU.min).then_inc(s_idx, 1)
            dve.wait_ge(s_inv_mm, B)
            w = [big[:, (13 + j) * 512:(13 + j) * 512 + NT] for j in range(3)]
            do(dve.tensor_scalar(w[0], bank(2)[:, NT:2 * NT], float(P), -float(P), ALU.mult, ALU.add))
            do(dve.tensor_tensor(w[0], bank(2)[:, 0:NT], w[0], ALU.add))
            dve.tensor_scalar(src_of[:, :], w[0], 0.0, None, ALU.max).then_inc(s_idx, 1)
            do(dve.tensor_scalar(w[1], w[0], 0.0, float(FAR + P), ALU.is_lt, ALU.mult))
            dve.tensor_tensor(dst_of[:, :], w[0], w[1], ALU.add).then_inc(s_idx, 1)

            dve.wait_ge(s_moe, 16 * 10)
            dve.wait_ge(s_idx, 3)

            def prepare(a, n, turn_):
                e = dve.value_load(expert_of[0:1, bass.ds(a, 1)], min_val=0, max_val=NX - 1)
                k, m = n % RING, n % DEPTH
                wait(dve, s_l1, a - (DEPTH - 1))
                ch.link(dve.tensor_copy(w1_now[m], w1s[:, bass.ds(e, 1), :].rearrange("p e f -> p (e f)")))
                wait(dve, s_hc, a - (DEPTH - 1))
                wait(dve, s_hd, a - (DEPTH - 1))
                ch.link(dve.tensor_copy(b1_now[m][:, :], b1col[:, bass.ds(e, 1), :].rearrange("p e c -> p (e c)")))
                dve.wait_ge(s_g[k], turn_)
                wait(dve, s_o[k], turn_ - 16)
                ch.link(dve.tensor_tensor(y[k], xg[k][:, 0:E], b2bc[:, bass.ds(e * E, E)], ALU.add))
                dve.tensor_scalar(gn[m], xg[k][:, 0:E], xg[k][:, E:E + 1], xg[k][:, E + 1:E + 2],
                                  ALU.subtract, ALU.mult).then_inc(s_prep, 1)
                ch.join()

            def hidden_out(a, n):
                dve.wait_ge(s_l1, a + 1)
                wait(dve, s_l2, a - (DEPTH - 1))
                c = NC - 1
                dve.tensor_scalar(hT[n % DEPTH][:, P * c:P * c + P], bank(6 + n % 2, P),
                                  b1_now[n % DEPTH][:, c:c + 1], 0.0, ALU.add, ALU.max).then_inc(s_hd, 1)

            def result(a, n):
                dve.wait_ge(s_l2, a + 1)
                dve.tensor_tensor(y[n % RING], bank(4 + n % 2, E), y[n % RING], ALU.add).then_inc(s_y, 1)

            for a in range(3):
                prepare(a, a, 16)
            for a in range(RING):
                prepare(a + 3, a + 3, 16 * ((a + 3) // RING + 1))
                hidden_out(a, a)
                if a >= 2:
                    result(a - 2, a - 2)

            def body(r):
                for n in range(RING):
                    prepare(r * RING + (n + 3), n + 3, (r + ((n + 3) // RING + 1)) * 16)
                    hidden_out(r * RING + n, n)
                    result(r * RING + (n - 2), n - 2)
            ch.loop(1, NT // RING - 1, 3 * RING, body)
            for a in range(NT - RING, NT + 2):
                if a + 3 < NT:
                    prepare(a + 3, a + 3, 16 * ((a + 3) // RING + 1))
                if a < NT:
                    hidden_out(a, a)
                result(a - 2, a - 2)


_WEIGHTS = ["d2v", "img", "txt", "att0", "att1", "f1", "f2"]


def kernel(**inputs):
    import concourse.bacc as _bacc
    from concourse.bass_utils import run_bass_kernel_spmd as _run

    nc = _bacc.Bacc("TRN2", target_bir_lowering=False, num_devices=1)
    arrays = {}

    def given(name):
        a = np.ascontiguousarray(inputs[name])
        arrays[f"in_{name}"] = a
        return nc.dram_tensor(f"in_{name}", a.shape, mybir.dt.from_np(a.dtype), kind="ExternalInput").ap()

    args = [given("x"), given("ctx_768"), [given(f"L0_xattn_W_{w}") for w in _WEIGHTS],
            [given(f"L0_xattn_b_{w}") for w in _WEIGHTS], given("L0_ffn_router_w"), given("L0_ffn_W1"),
            given("L0_ffn_b1"), given("L0_ffn_W2"), given("L0_ffn_b2")]
    out = nc.dram_tensor("out_0", (B, S, E), F32, kind="ExternalOutput").ap()
    xattn_moe(nc, *args, out)
    r = _run(nc, [arrays], core_ids=[0])
    return r.results[0]["out_0"]
```

```python
from contextlib import ExitStack

import numpy as np

import concourse.bass as bass
from concourse import mybir

F32 = mybir.dt.float32
BF16 = mybir.dt.bfloat16
I32 = mybir.dt.int32
ALU = mybir.AluOpType
ACT = mybir.ActivationFunctionType
AX = mybir.AxisListType.X

P = 128
B = 64
S = 128
E = 128
CT = 77
DC = 96
KV = 64
FF = 512
NC = FF // P
NX = 8
T = B * S
GB = 4
G = B // GB
GT = GB * S
GC = GB * CT
CP = 112
CJ = B * CT // CP
CAP = int(np.ceil(T / NX * 1.25))
NT = T // P + NX
RING = 8
DEPTH = 4
COPY = 4
LAG = 9
NQ = CJ // 4
QC = 4 * CP
NP = 4
PC = B * CT // NP
XP = 8
OWN = (0, 3, 6)
VG = 10
GR = 4
XW = E + 2
MAGIC = 12582912.0
EPS = 1e-5
LEVELS = 14
HT = 16
FAR = 32768
WIDTHS = (DC, E, E, E, E, NC * 2 * E, FF)
COUNTS = (E * DC, E * E, E * E, KV * E, KV * E, FF * 2 * E, E * FF)
D2V, IMG, TXT, ATT0, ATT1, F1, F2 = range(7)
NSMALL = 7 + NC + 3
Q_CTX, Q_VIS, Q_IMG, Q_X, Q_CAT, Q_H = range(6)


def wait(eng, sem, value):
    if not isinstance(value, int) or value > 0:
        eng.wait_ge(sem, value)


def wait_alone(eng, sem, value, passed):
    if not isinstance(value, int) or value > 0:
        eng.wait_ge(sem, value)
        eng.sem_inc(passed, 1)


def for_loop(eng, start, end, body):
    with eng.Fori(start, end) as i:
        body(i)


class Chain:

    def __init__(self, eng, sem):
        self.eng, self.sem, self.base, self.count = eng, sem, 0, 0

    def link(self, ins):
        ins.then_inc(self.sem, 1)
        self.count += 1

    def join(self):
        self.eng.wait_ge(self.sem, self.base + self.count)

    def loop(self, start, end, per, body):
        first = self.base + self.count
        with self.eng.Fori(start, end) as i:
            self.base, self.count = (i - start) * per + first, 0
            body(i)
            assert self.count == per, self.count
        self.base, self.count = first + (end - start) * per, 0


def xattn_moe(nc, x, ctx_in, weights, biases, router_w, W1, b1, W2, b2, out):
    rows = nc.dram_tensor("token_rows", (T, XW), F32).ap()
    with ExitStack() as stack:
        def sb(name, shape, dtype=F32):
            return stack.enter_context(nc.sbuf_tensor(name, shape, dtype))

        def sem(name):
            return stack.enter_context(nc.semaphore(name))

        psum = stack.enter_context(nc.psum_tensor("psum", [P, 8, 512], F32))

        ident = sb("ident", [P, P])
        ident_b = sb("ident_b", [P, P], BF16)
        ones = sb("ones", [P, P])
        ones_b = sb("ones_b", [P, P], BF16)
        before_b = sb("before_b", [P, P], BF16)
        same_expert = sb("same_expert", [P, P])
        magic = sb("magic", [P, 1])
        warm = sb("warm", [1, 1])
        inv_counts = sb("inv_counts", [P, 7])
        steps = sb("steps", [P, LEVELS, 3])
        tile_no = sb("tile_no", [P, NT])
        tile_no_b = sb("tile_no_b", [P, NT], BF16)
        row_no_b = sb("row_no_b", [P, P], BF16)
        part_no = sb("part_no", [P, 1])
        turn_no = sb("turn_no", [P, B])
        rank8 = sb("rank8", [P, NX])
        seg = sb("seg", [P, NX * B])
        wsum = sb("wsum", [P, 7])
        ws = sb("ws", [P, 7])
        wlim = sb("wlim", [P, 2, 7])
        wT = sb("wT", [P, 3 * P], BF16)
        attT = sb("attT", [P, 2, 2, KV], BF16)
        f1T = sb("f1T", [P, 2, FF], BF16)
        f2T = sb("f2T", [P, NC, E], BF16)
        small_w = sb("small_w", [NX + NX * NC, E])
        small_wT = sb("small_wT", [P, NX + NX * NC])
        rwT = small_wT[:, 0:NX]
        b1col = small_wT[:, NX:].rearrange("p (e c) -> p e c", e=NX)
        bcol = sb("bcol", [P, 5 + NC])
        bf2 = sb("bf2", [P, E])
        amax = sb("amax", [P, 6])
        gmax = sb("gmax", [1, 6])
        iscale = sb("iscale", [P, 6])
        inv = sb("inv", [P, 6])
        scale = sb("scale", [P, 7])
        h_scale = sb("h_scale", [P, 1])
        h_bias = sb("h_bias", [P, NC])
        xall = sb("xall", [P, B, XW])
        big = sb("big", [P, T])
        tok_b = sb("tok_b", [P, T], BF16)
        xqT = sb("xqT", [P, T], BF16)
        feat = sb("feat", [P, B * CT])
        qa = sb("qa", [P, B * CT], BF16)
        qb = sb("qb", [P, B * CT], BF16)
        keys = sb("keys", [P, 2 * B * CT])
        stats = sb("stats", [P, B, 6])
        tmp = sb("tmp", [P, 4, B])
        part = sb("part", [P, 4, B])
        avg = sb("avg", [P, B])
        avg_q = sb("avg_q", [P, B], BF16)

        wraw = big[:, 0:sum(WIDTHS)]
        wq = big[:, sum(WIDTHS):sum(WIDTHS) * 3 // 2].bitcast(BF16)
        wneg = big[:, sum(WIDTHS) * 3 // 2:sum(WIDTHS) * 2].bitcast(BF16)
        ctx_raw = keys[:, 0:CJ * DC]
        scaled = keys[:, 0:B * CT]
        ctx_q = tok_b[0:CP, 0:CJ * DC]
        xn = big[:, :].rearrange("p (t d) -> p t d", d=E)

        at = [0]

        def take(n):
            at[0] += n
            return keys[:, at[0] - n:at[0]]
        fused0 = [take(GT) for _ in range(GR)]
        fused1 = [take(GT) for _ in range(GR)]
        kT = [[take(GC) for _ in range(GR)] for _ in range(2)]
        ktok = [[take(GB * P)[0:CT, :] for _ in range(n)] for n in (2, GR)]
        qb_f = qb[:, :].bitcast(F32)
        prob = [[qb_f[:, (2 * l + n) * GC:(2 * l + n + 1) * GC].rearrange("p (b c) -> p b c", b=GB)
                 for n in range(2)] for l in range(2)]
        probT = [sb(f"probT{l}", [CT, GT]) for l in range(2)]
        amx = sb("amx", [P, 2, GB])
        asum = sb("asum", [P, 2, GB])
        arec = sb("arec", [P, 2, GB])
        u = feat[:, 0:NC * GT].rearrange("p (c n) -> p c n", c=NC)
        hq = feat[:, NC * GT:NC * GT * 3 // 2].bitcast(BF16).rearrange("p (c n) -> p c n", c=NC)
        xs = sb("xs", [P, GB, E])
        xsT = sb("xsT", [P, GT])[:, :]
        st2 = stats[:, 0:GB, :]

        def route(n):
            return big[:, n * 512:(n + 1) * 512]

        w1s = keys[:, 0:NX * FF].rearrange("p (e f) -> p e f", e=NX)
        w2s = keys[:, NX * FF:2 * NX * FF].rearrange("p (e c d) -> p e c d", e=NX, c=NC)
        b2bc = keys[:, 2 * NX * FF:2 * NX * FF + NX * E]
        xqT_f = xqT[:, :].bitcast(F32)
        cut = [0]

        def carve(n):
            cut[0] += n
            return xqT_f[:, cut[0] - n:cut[0]]
        xg = [xall[:, n, :] for n in range(RING)]
        y = [xall[:, RING + n, 0:E] for n in range(RING)]
        gn = [carve(E) for _ in range(DEPTH)]
        gT = [carve(E) for _ in range(DEPTH)]
        hT = [carve(FF) for _ in range(DEPTH)]
        w1_now = [feat[:, n * FF:(n + 1) * FF] for n in range(DEPTH)]
        b1_now = [sb(f"b1_now{n}", [P, NC]) for n in range(DEPTH)]
        idx_in = sb("idx_in", [P, RING], I32)
        idx_out = sb("idx_out", [P, RING], I32)
        src_of = sb("src_of", [P, NT], I32)
        dst_of = sb("dst_of", [P, NT], I32)
        expert_of = sb("expert_of", [1, NT], I32)
        cnt = sb("cnt", [P, 3])
        reached = sb("reached", [P, 3])
        met = sb("met", [P, 1])
        thr = sb("thr", [P, 1])
        cand = sb("cand", [P, 3])
        thr8 = sb("thr8", [P, NX])
        n8 = [sb(f"n8_{n}", [P, NX]) for n in range(5)]
        n8i = [sb(f"n8i_{n}", [P, NX], I32) for n in range(2)]
        t64 = [sb(f"t64_{n}", [P, B]) for n in range(8)]
        t64i = [sb(f"t64i_{n}", [P, B], I32) for n in range(3)]
        hot_row = xqT[:, :].rearrange("p (t r) -> p t r", t=B)
        hot_tile = feat[:, :].bitcast(BF16)[:, 0:B * 2 * NT].rearrange("p (t a c) -> p t a c", t=B, a=2)
        hot = qb[:, 0:B * NT].rearrange("p (t c) -> p t c", t=B)

        s_ctx = [sem(f"ctx_loaded{n}") for n in range(NP)]
        s_w = sem("weights_loaded")
        s_x = [sem(f"x_loaded{n}") for n in range(XP)]
        s_small = sem("biases_loaded")
        s_moe = sem("expert_weights_loaded")
        s_const = sem("constants_made")
        s_cc = sem("constants_begun")
        s_amax = sem("amax_ready")
        s_grow = sem("amax_row_ready")
        s_gm = sem("global_max_ready")
        s_gcol = sem("global_max_spread")
        s_inv = sem("inv_ready")
        s_wsum = sem("wsum_ready")
        s_wtot = sem("wsum_spread")
        s_wq = sem("weights_quantised")
        s_wtr = sem("weights_transposed")
        s_wT = sem("weights_in_place")
        s_sc = sem("scales_ready")
        s_fs = sem("ctx_or_features_scaled")
        s_cq = sem("ctx_quantised")
        s_tr = sem("transposed")
        s_trc = sem("transposed_copied")
        s_trd = sem("transposed_copied_vector")
        s_mm = sem("linear_done")
        s_mmc = sem("linear_copied")
        s_vq = sem("vis_quantised")
        s_iq = sem("image_quantised")
        s_bn0 = sem("half_statistics")
        s_mean = sem("mean_ready")
        s_var = sem("variance_ready")
        s_std = sem("deviation_ready")
        s_lm = sem("x_less_mean_vector")
        s_rs0 = sem("inverse_deviation")
        s_xd = sem("x_less_mean")
        s_xn = sem("xn_from_gpsimd")
        s_avg = sem("image_sums")
        s_xs = sem("x_scaled")
        s_xq = sem("x_quantised")
        s_fmm = sem("fused_product")
        s_f = sem("fused_ready")
        s_kmm = [sem(f"keys_product{n}") for n in range(2)]
        s_k = [sem(f"keys_ready{n}") for n in range(2)]
        s_kt = sem("attention_keys_turned")
        s_ktc = sem("key_tokens_ready")
        s_smm = [sem(f"scores{n}") for n in range(2)]
        s_mx = [sem(f"scores_max{n}") for n in range(2)]
        s_sub = [sem(f"scores_less_max{n}") for n in range(2)]
        s_e = [sem(f"exp{n}") for n in range(2)]
        s_sum = [sem(f"exp_sum{n}") for n in range(2)]
        s_r = [sem(f"sum_inverted{n}") for n in range(2)]
        s_p = [sem(f"probs{n}") for n in range(2)]
        s_t = [sem(f"probs_transposed{n}") for n in range(2)]
        s_pt = [sem(f"probsT_copied{n}") for n in range(2)]
        s_av = [sem(f"attended{n}") for n in range(2)]
        s_up = [sem(f"fused_updated{n}") for n in range(2)]
        s_fm = sem("fused_max")
        s_res = sem("residual_ready")
        s_cs = sem("cat_scaled")
        s_catq = sem("cat_quantised")
        s_h = sem("hidden_product")
        s_hm = sem("hidden_max_taken")
        s_h2 = sem("hidden_product_again")
        s_relu = sem("relu_done")
        s_hq = sem("hidden_quantised")
        s_f2 = sem("out_product")
        s_x1 = sem("x1_ready")
        s_bn = sem("half_statistics2")
        s_rs = sem("inverse_deviation2")
        s_var2 = sem("variance2_ready")
        s_std2 = sem("deviation2_ready")
        s_xn2 = sem("xn2_ready")
        s_x2t = sem("xn2_transposed")
        s_x2c = sem("xn2T_copied")
        s_lg = sem("logits_ready")
        s_rows = sem("rows_stored")
        s_d = sem("logits_less_max")
        s_ex = sem("logits_exp")
        s_v = sem("keys_by_expert")
        s_vt = sem("keys_transposed")
        s_cnt = sem("counts_ready")
        s_cnt2 = sem("counts_summed")
        s_thr = sem("threshold_ready")
        s_thr_r = sem("threshold_row")
        s_thr_c = sem("threshold_row_copied")
        s_thr_s = sem("threshold_spread")
        s_ms = sem("masks_ready")
        s_ps = sem("prefixes_ready")
        s_ht = sem("one_hot_tiles_ready")
        s_hr = sem("one_hot_rows_ready")
        s_hp = sem("tiles_times_row")
        s_hu = sem("tiles_times_turn")
        s_inv_mm = sem("one_hots_used")
        s_idx = sem("indices_ready")
        s_ixi = sem("gather_index_copied")
        s_ixo = sem("scatter_index_copied")
        s_g = [sem(f"gathered{n}") for n in range(RING)]
        s_y = sem("result_ready")
        s_o = [sem(f"scattered{n}") for n in range(RING)]
        s_prep = sem("tile_prepared")
        s_gt = sem("gathered_transposed")
        s_gc = sem("gatheredT_copied")
        s_l1 = sem("layer1_product")
        s_hc = sem("hidden_relu_scalar")
        s_hd = sem("hidden_relu_vector")
        s_l2 = sem("layer2_product")
        s_passed = sem("gpsimd_waits_passed")
        s_passed3 = sem("tensor_waits_passed")
        s_passed2 = sem("vector_waits_passed")
        s_dve = sem("vector_chain")
        s_act = sem("scalar_chain")

        WOFF = [sum(WIDTHS[:k]) for k in range(7)]

        def wslice(t, k):
            return t[0:KV if k in (ATT0, ATT1) else P, WOFF[k]:WOFF[k] + WIDTHS[k]]

        def bank(n, width=512, rows_=P):
            return psum[0:rows_, n, 0:width]

        def bank_b(n):
            return psum[:, n, :].bitcast(BF16)

        def c4(i):
            return bass.ds(i * GC, GC)

        def g4(i):
            return bass.ds(i * GT, GT)

        def attention_steps(loop, step):
            for t in range(GR - 1):
                step(t, t, t)
            loop(1, G // GR, lambda r: [step(r * GR + (n - 1), (n - 1) % GR, G - 2) for n in range(GR)])
            for t in range(G - 1, G + 3):
                step(t, t % GR, t)

        def hidden_steps(loop, step):
            for t in range(-1, 4):
                step(t, t)
            loop(4, G - 1, lambda t: step(t, G - 2))
            for t in range(G - 1, G + 3):
                step(t, t)

        block = stack.enter_context(nc.Block())

        @block.sync
        def _(sp):
            ctx_rows = ctx_in.rearrange("b c d -> (b c) d").rearrange("(p j) d -> p (j d)", p=CP)
            w = CJ * DC // NP
            for n in range(NP):
                sp.dma_start(ctx_raw[0:CP, w * n:w * n + w], ctx_rows[:, w * n:w * n + w]).then_inc(s_ctx[n], 16)
            for k in (D2V, IMG, TXT):
                sp.dma_start(bcol[:, k:k + 1], biases[k].rearrange("(p o) -> p o", o=1)).then_inc(s_small, 16)
            for l in range(2):
                for twice in range(2):
                    sp.dma_start(bcol[KV * twice:KV * twice + KV, ATT0 + l:ATT0 + l + 1],
                                 biases[ATT0 + l].rearrange("(p o) -> p o", o=1)).then_inc(s_small, 16)
            for c in range(NC):
                sp.dma_start(bcol[:, 5 + c:6 + c], biases[F1][P * c:P * c + P].rearrange("(p o) -> p o", o=1)
                             ).then_inc(s_small, 16)
            sp.dma_start(bf2[:, :], biases[F2].partition_broadcast(P)).then_inc(s_small, 16)
            sp.dma_start(small_w[0:NX, :], router_w).then_inc(s_small, 16)
            sp.dma_start(small_w[NX:, :], b1.rearrange("e (c p) -> (e c) p", p=P)).then_inc(s_small, 16)
            xt = x.rearrange("b s e -> s b e")
            w = B // XP
            for n in range(XP):
                sp.dma_start(xall[:, w * n:w * n + w, 0:E], xt[:, w * n:w * n + w, :]).then_inc(s_x[n], 16)
            sp.wait_ge(s_up[1], G + 1)
            sp.dma_start(w1s, W1.rearrange("e d f -> d e f")).then_inc(s_moe, 16)
            for e in range(NX):
                sp.dma_start(w2s[:, e, :, :], W2[e].rearrange("(c p) d -> p c d", p=P)).then_inc(s_moe, 16)
            sp.dma_start(b2bc, b2.rearrange("e d -> (e d)").partition_broadcast(P)).then_inc(s_moe, 16)
            rows_t = rows.rearrange("(t p) w -> p t w", p=P)
            with sp.Fori(0, G) as i:
                sp.wait_ge(s_xn2, i + 1)
                sp.dma_start(rows_t[:, bass.ds(i * GB, GB), :], xall[:, bass.ds(i * GB, GB), :]).then_inc(s_rows, 16)
            sp.wait_ge(s_rows, 16 * G)

        @block.gpsimd
        def _(pool):
            pool.memset(ident[:, :], 0.0).then_inc(s_cc, 1)
            pool.memset(ident_b[:, :], 0.0).then_inc(s_cc, 1)
            pool.memset(before_b[:, :], 1.0).then_inc(s_cc, 1)
            pool.memset(same_expert[:, :], 0.0).then_inc(s_cc, 1)
            pool.memset(seg[:, :], 1.0).then_inc(s_cc, 1)
            pool.memset(ones[:, :], 1.0).then_inc(s_const, 1)
            pool.memset(ones_b[:, :], 1.0).then_inc(s_const, 1)
            pool.memset(magic[:, :], MAGIC).then_inc(s_const, 1)
            pool.memset(wsum[:, :], 0.0).then_inc(s_const, 1)
            pool.memset(amax[:, :], 0.0).then_inc(s_const, 1)
            for k in range(7):
                pool.memset(inv_counts[:, k:k + 1], 1.0 / COUNTS[k]).then_inc(s_const, 1)
            pool.wait_ge(s_cc, 5)
            for m in (ident, ident_b):
                pool.affine_select(out=m[:, :], in_=m[:, :], compare_op=ALU.not_equal, fill=1.0, base=0,
                                   pattern=[[-1, P]], channel_multiplier=1).then_inc(s_const, 1)
            pool.affine_select(out=before_b[:, :], in_=before_b[:, :], compare_op=ALU.is_gt, fill=0.0, base=0,
                               pattern=[[1, P]], channel_multiplier=-1).then_inc(s_const, 1)
            v = same_expert[:, :].rearrange("p (a e) -> p a e", e=NX)
            for d in range(-(P // NX) + 1, P // NX):
                pool.affine_select(out=same_expert[:, :], in_=same_expert[:, :], compare_op=ALU.not_equal, fill=1.0,
                                   base=NX * d, pattern=[[-1, P]], channel_multiplier=1).then_inc(s_cc, 1)
                pool.wait_ge(s_cc, 5 + d + P // NX)
            segv = seg[:, :].rearrange("p (e t) -> p e t", e=NX)
            pool.memset(segv[:, :, 0:1], 0.0).then_inc(s_const, 1)
            for k in range(LEVELS):
                for j in range(3):
                    pool.memset(steps[:, k, j:j + 1], (j + 1) * 4.0 ** -(k + 1)).then_inc(s_const, 1)
            for e in range(NX):
                pool.memset(rank8[:, e:e + 1], float(NX - e)).then_inc(s_const, 1)
            pool.iota(tile_no[:, :], pattern=[[1, NT]], base=0, channel_multiplier=0,
                      allow_small_or_imprecise_dtypes=True).then_inc(s_const, 1)
            pool.iota(tile_no_b[:, :], pattern=[[1, NT]], base=0, channel_multiplier=0,
                      allow_small_or_imprecise_dtypes=True).then_inc(s_const, 1)
            pool.iota(row_no_b[:, :], pattern=[[1, P]], base=0, channel_multiplier=0,
                      allow_small_or_imprecise_dtypes=True).then_inc(s_const, 1)
            pool.iota(part_no[:, :], pattern=[[0, 1]], base=0, channel_multiplier=1,
                      allow_small_or_imprecise_dtypes=True).then_inc(s_const, 1)
            pool.iota(turn_no[:, :], pattern=[[1, B]], base=1, channel_multiplier=0,
                      allow_small_or_imprecise_dtypes=True).then_inc(s_const, 1)

            pool.wait_ge(s_mean, 1)
            pool.wait_ge(s_rs0, 1)
            for n, i in enumerate(range(VG, G, 2)):
                xr, xo = xall[:, i * GB:(i + 2) * GB, :], xn[:, i * GB:(i + 2) * GB, :]
                pool.tensor_tensor(xo, xr[:, :, 0:E], xr[:, :, E:E + 1].to_broadcast([P, 2 * GB, E]), ALU.subtract
                                   ).then_inc(s_xd, 1)
                pool.wait_ge(s_xd, n + 1)
                pool.tensor_tensor(xo, xo, xr[:, :, E + 1:E + 2].to_broadcast([P, 2 * GB, E]), ALU.mult
                                   ).then_inc(s_xn, 1)
            pool.wait_ge(s_mmc, 2 * NQ + 2)
            v = feat[:, :].rearrange("p (b a c) -> p b a c", b=B, a=CT // 11)
            so_far = qb_f[:, 4 * GC:4 * GC + B * 11].rearrange("p (b c) -> p b c", b=B)
            parts = [v[:, :, a, :] for a in range(CT // 11)] + [so_far[:, :, c] for c in range(1, 11)]
            for n, new in enumerate(parts[1:]):
                wide = n + 2 <= CT // 11
                dst, old = (so_far, so_far if n else parts[0]) if wide else (
                    avg[:, :], avg[:, :] if n + 2 > CT // 11 + 1 else so_far[:, :, 0])
                pool.tensor_tensor(dst, old, new, ALU.add).then_inc(s_avg, 1)
                pool.wait_ge(s_avg, n + 1)

            def norm(l, i, n):
                pool.wait_ge(s_r[l], i + 1)
                pr = prob[l][n % 2]
                pool.tensor_tensor(pr, pr, arec[:, l, :].unsqueeze(2).to_broadcast([P, GB, CT]), ALU.mult
                                   ).then_inc(s_p[l], 1)

            def residual(i):
                xr = xall[:, bass.ds(i * GB, GB), 0:E]
                pool.tensor_tensor(xr, xr, bf2[:, :].unsqueeze(1).to_broadcast([P, GB, E]), ALU.add).then_inc(s_res, 1)

            def step(t, n, last):
                if last < G:
                    norm(0, t, n)
                if 2 <= last < G + 2:
                    norm(1, t - 2, n + 2)
                if last < G:
                    residual(t)
            pool.wait_ge(s_small, 16 * NSMALL)
            pool.wait_ge(s_amax, Q_X + 1)
            attention_steps(lambda a, b, body: for_loop(pool, a, b, body), step)

            for i in range(B // HT):
                pool.wait_ge(s_ht, i + 1)
                t = slice(i * HT, (i + 1) * HT)
                pool.tensor_tensor(hot_tile[:, t, 1, :], hot[:, t, :], turn_no[:, t].unsqueeze(2).to_broadcast([P, HT, NT]),
                                   ALU.mult).then_inc(s_hu, 1)

            out_rows = out.rearrange("b s e -> (b s) e")
            pool.wait_ge(s_idx, 3)
            pool.wait_ge(s_rows, 16 * G)

            def take_indices(r, n, mine, all_, moved, copied):
                for k in range(COPY):
                    wait_alone(pool, moved[n + k], r * 16, s_passed)
                pool.tensor_copy(mine[:, n:n + COPY], all_[:, bass.ds(r * RING + n, COPY)]).then_inc(copied, 1)
                wait_alone(pool, copied, r * (RING // COPY) + (n // COPY + 1), s_passed)

            def gather(r, n):
                if n % COPY == 0:
                    take_indices(r, n, idx_in, src_of, s_g, s_ixi)
                wait_alone(pool, s_prep, (r - 1) * RING + (n + 1), s_passed)
                pool.indirect_dma_start(xg[n], None, rows, bass.IndirectOffsetOnAxis(ap=idx_in[:, n:n + 1], axis=0)
                                        ).then_inc(s_g[n], 16)

            def scatter(r, n):
                if n % COPY == 0:
                    take_indices(r, n, idx_out, dst_of, s_o, s_ixo)
                wait_alone(pool, s_y, r * RING + (n + 1), s_passed)
                pool.indirect_dma_start(out_rows, bass.IndirectOffsetOnAxis(ap=idx_out[:, n:n + 1], axis=0), y[n], None,
                                        bounds_check=T - 1, oob_is_err=False).then_inc(s_o[n], 16)

            def both(r, n):
                gather(r, n)
                scatter(r + (n - LAG) // RING, (n - LAG) % RING)

            for a in range(LAG):
                gather(a // RING, a % RING)
            for a in range(LAG, 3 * RING):
                both(a // RING, a % RING)
            with pool.Fori(3, NT // RING) as r:
                for n in range(RING):
                    both(r, n)
            for a in range(NT - LAG, NT):
                scatter(a // RING, a % RING)
            for n in range(RING):
                pool.wait_ge(s_o[n], 16 * (NT // RING))

        @block.scalar
        def _(act):
            def linear(src_bank, dst, k, b):
                return act.activation(dst, src_bank, ACT.Identity, bias=bcol[:, b:b + 1], scale=scale[:, k:k + 1])

            for k in range(5):
                act.dma_start(wslice(wraw, k), weights[k]).then_inc(s_w, 16)
            act.dma_start(wslice(wraw, F1).rearrange("p (c i) -> p c i", c=NC),
                          weights[F1].rearrange("(c p) i -> p c i", p=P)).then_inc(s_w, 16)
            act.dma_start(wslice(wraw, F2), weights[F2]).then_inc(s_w, 16)

            def scale_up(dst, src, k, n, done):
                act.activation(dst, src, ACT.Identity, bias=magic[0:dst.shape[0], :],
                               scale=inv[0:dst.shape[0], k:k + 1]).then_inc(done, 1)

            act.wait_ge(s_const, 14)
            act.wait_ge(s_inv, Q_CTX + 1)
            w = CJ * DC // NP
            for n in range(NP):
                v = ctx_raw[0:CP, w * n:w * n + w]
                scale_up(v, v, Q_CTX, n, s_fs)
            act.wait_ge(s_wtr, 1)
            act.copy(wT[0:DC, 0:P], bank_b(0)[0:DC, 0:P]).then_inc(s_wT, 1)
            act.copy(wT[:, P:3 * P], bank_b(0)[:, P:3 * P]).then_inc(s_wT, 1)
            act.copy(attT[:, :, :, :], bank_b(0)[:, 3 * P:4 * P].rearrange("p (l k) -> p l k", l=2)
                     .unsqueeze(2).to_broadcast([P, 2, 2, KV])).then_inc(s_wT, 1)
            act.wait_ge(s_wtr, 2)
            act.copy(f1T[:, :, :], bank_b(1).rearrange("p (h f) -> p h f", h=2)).then_inc(s_wT, 1)
            act.wait_ge(s_wtr, 3)
            act.copy(f2T[:, :, :], bank_b(2)[:, 0:FF].rearrange("p (c d) -> p c d", c=NC)).then_inc(s_wT, 1)
            act.wait_ge(s_wtr, 4)
            act.copy(small_wT[:, :], bank(7, NX + NX * NC)).then_inc(s_wT, 1)
            qa_v = qa[0:DC, :].rearrange("d (p j) -> d j p", j=CJ)
            for k in range(NQ):
                act.wait_ge(s_tr, k + 1)
                act.copy(qa_v[:, 4 * k:4 * k + 4, :], bank_b(3 + k % 2)[0:DC, 0:QC].rearrange("d (j p) -> d j p", j=4)
                         ).then_inc(s_trc, 1)

            def linears(first, k):
                for n in range(NQ):
                    act.wait_ge(s_mm, first + n + 1)
                    linear(bank(5 + (first + n) % 2, QC), feat[:, QC * n:QC * n + QC], k, k).then_inc(s_mmc, 1)

            act.wait_ge(s_small, 16 * NSMALL)
            act.wait_ge(s_sc, 1)
            linears(0, D2V)
            act.wait_ge(s_var, 1)
            act.activation(tmp[:, 3, :], tmp[:, 2, :], ACT.Sqrt).then_inc(s_std, 1)
            act.wait_ge(s_inv, Q_VIS + 1)
            for n in range(NP):
                scale_up(scaled[:, PC * n:PC * n + PC], feat[:, PC * n:PC * n + PC], Q_VIS, n, s_fs)
            act.wait_ge(s_sc, 2)
            linears(NQ, IMG)
            act.wait_ge(s_inv, Q_IMG + 1)
            for n in range(NP):
                scale_up(scaled[:, PC * n:PC * n + PC], feat[:, PC * n:PC * n + PC], Q_IMG, n, s_fs)

            def scale_tokens(k, done):
                act.wait_ge(s_inv, k + 1)
                w = T // XP
                for n in range(XP):
                    if n not in OWN:
                        scale_up(big[:, w * n:w * n + w], big[:, w * n:w * n + w], k, n, done)
            act.activation(warm[:, :], magic[0:1, :], ACT.Exp, scale=0.0)
            scale_tokens(Q_X, s_xs)
            w = T // XP
            for n in range(XP // 2):
                act.wait_ge(s_tr, NQ + n + 1)
                act.copy(xqT[:, w * n:w * n + w], bank_b(n)).then_inc(s_trc, 1)

            act.sem_inc(s_pt[0], 1)
            act.sem_inc(s_pt[1], 1)

            def operands(i, n):
                act.wait_ge(s_fmm, i + 1)
                wait(act, s_up[0], i - (GR - 2))
                linear(bank(0), fused0[n % GR], TXT, TXT).then_inc(s_f, 1)
                for l in range(2):
                    act.wait_ge(s_kmm[l], i + 1)
                    wait(act, s_smm[l], i - (GR - 1))
                    linear(bank(1 + l, GC), kT[l][n % GR], ATT0 + l, ATT0 + l).then_inc(s_k[l], 1)

            def key_tokens(i, n):
                act.wait_ge(s_kt, i + 1)
                for l in range(2):
                    wait(act, s_av[l], i - (GR - 2) if l else i)
                    v = bank(7, GB * P, CT).rearrange("p (b l k) -> p b l k", b=GB, l=2)[:, :, l:l + 1, :]
                    m = act.copy(ktok[l][n % (GR if l else 2)].rearrange("p (b a k) -> p b a k", b=GB, a=2),
                                 v.to_broadcast([CT, GB, 2, KV]))
                m.then_inc(s_ktc, 1)

            def exp(l, i, n):
                act.wait_ge(s_sub[l], i + 2)
                pr = prob[l][n % 2]
                act.activation(pr, pr, ACT.Exp, scale=float(E) ** -0.5).then_inc(s_e[l], 1)

            def probs_out(l, i):
                act.wait_ge(s_t[l], i + 1)
                act.wait_ge(s_av[l], i + 1)
                act.copy(probT[l][:, :], bank(3 + l, 512, CT)).then_inc(s_pt[l], 1)

            def step(t, n, last):
                if 1 <= last < G + 1:
                    probs_out(0, t - 1)
                if last < G:
                    exp(0, t, n)
                if 3 <= last:
                    probs_out(1, t - 3)
                if 2 <= last < G + 2:
                    exp(1, t - 2, n + 2)
                if last < G - 1:
                    operands(t + 1, n + 1)
                if last < G:
                    key_tokens(t, n)

            act.wait_ge(s_sc, 4)
            operands(0, 0)
            attention_steps(lambda a, b, body: for_loop(act, a, b, body), step)

            scale_tokens(Q_CAT, s_cs)

            act.wait_ge(s_sc, 6)

            def relu(i, c):
                act.wait_ge(s_h2, i * 2 + c // 2 + 1)
                act.activation(u[:, c, :], bank(c), ACT.Relu, bias=h_bias[:, c:c + 1],
                               scale=h_scale[:, :]).then_inc(s_relu, 1)

            def sqrt2(i):
                act.wait_ge(s_var2, i + 1)
                act.activation(tmp[:, 3, 0:GB], tmp[:, 2, 0:GB], ACT.Sqrt).then_inc(s_std2, 1)

            def x2T_out(i):
                act.wait_ge(s_x2t, i + 1)
                wait(act, s_lg, i)
                act.copy(xsT, bank(5)).then_inc(s_x2c, 1)

            def step(t, last):
                if 2 <= last < G + 2:
                    sqrt2(t - 2)
                if 3 <= last:
                    x2T_out(t - 3)
                if last < G - 1:
                    wait(act, s_hq, t + 1)
                    for c in range(NC):
                        relu(t + 1, c)
            hidden_steps(lambda a, b, body: for_loop(act, a, b, body), step)

            act.wait_ge(s_d, 1)
            act.activation(route(0), route(0), ACT.Exp).then_inc(s_ex, 1)

            for i in range(B // HT):
                act.wait_ge(s_ht, i + 1)
                act.activation(hot_tile[:, i * HT:(i + 1) * HT, 0, :], hot[:, i * HT:(i + 1) * HT, :], ACT.Copy,
                               scale=part_no[:, :]).then_inc(s_hp, 1)

            def gathered_out(a, n):
                act.wait_ge(s_gt, a + 1)
                wait(act, s_l1, a - (DEPTH - 1))
                act.copy(gT[n % DEPTH], bank(n % 2, P)).then_inc(s_gc, 1)

            def hidden_out(a, n):
                act.wait_ge(s_l1, a + 1)
                wait(act, s_l2, a - (DEPTH - 1))
                for c in range(NC - 1):
                    m = act.activation(hT[n % DEPTH][:, P * c:P * c + P], bank(2 + n % 2)[:, P * c:P * c + P],
                                       ACT.Relu, bias=b1_now[n % DEPTH][:, c:c + 1])
                m.then_inc(s_hc, 1)

            gathered_out(0, 0)
            gathered_out(1, 1)
            for a in range(RING):
                gathered_out(a + 2, a + 2)
                hidden_out(a, a)
            with act.Fori(1, NT // RING - 1) as r:
                for n in range(RING):
                    gathered_out(r * RING + (n + 2), n + 2)
                    hidden_out(r * RING + n, n)
            for a in range(NT - RING, NT):
                if a + 2 < NT:
                    gathered_out(a + 2, a + 2)
                hidden_out(a, a)

        @block.tensor
        def _(pe):
            pe.sem_inc(s_trc, 2)
            pe.sem_inc(s_mmc, 2)

            def spread_max(k):
                pe.wait_ge(s_amax, k + 1)
                pe.transpose(psum[0:1, 7, 0:P], amax[:, k:k + 1], ident[:, :]).then_inc(s_grow, 1)
                pe.wait_ge(s_gm, k + 1)
                pe.matmul(psum[:, 7, P + k:P + k + 1], ones[0:1, :], gmax[0:1, k:k + 1],
                          start=True, stop=True).then_inc(s_gcol, 1)

            pe.wait_ge(s_const, 14)
            spread_max(Q_CTX)
            pe.wait_ge(s_wsum, 7)
            pe.matmul(bank(6, 7), ones[:, :], wsum[:, :], start=True, stop=True).then_inc(s_wtot, 1)
            pe.wait_ge(s_wq, 7)
            for k in (D2V, IMG, TXT):
                pe.transpose(bank_b(0)[0:WIDTHS[k], P * k:P * k + P], wslice(wq, k), ident_b[:, :])
            pe.transpose(bank_b(0)[:, 3 * P:3 * P + KV], wslice(wq, ATT0), ident_b[0:KV, 0:KV])
            pe.transpose(bank_b(0)[:, 3 * P + KV:4 * P], wslice(wq, ATT1), ident_b[0:KV, 0:KV]).then_inc(s_wtr, 1)
            f1q = wslice(wq, F1).rearrange("p (c h i) -> p c h i", c=NC, h=2)
            for c in range(NC):
                for h in range(2):
                    m = pe.transpose(bank_b(1)[:, h * FF + c * P:h * FF + c * P + P], f1q[:, c, h, :], ident_b[:, :])
            m.then_inc(s_wtr, 1)
            f2q = wslice(wq, F2).rearrange("p (c i) -> p c i", c=NC)
            for c in range(NC):
                m = pe.transpose(bank_b(2)[:, c * P:c * P + P], f2q[:, c, :], ident_b[:, :])
            m.then_inc(s_wtr, 1)
            pe.wait_ge(s_small, 16 * NSMALL)
            pe.wait_ge(s_inv, 1)
            pe.transpose(bank(7, NX + NX * NC), small_w[:, :], ident[0:NX + NX * NC, 0:NX + NX * NC]).then_inc(s_wtr, 1)

            cq = ctx_q.rearrange("p (j d) -> p j d", j=CJ)
            for k in range(NQ):
                pe.wait_ge(s_trc, k + 1)
                pe.wait_ge(s_cq, (4 * k + 3) * NP // CJ + 1)
                for j in range(4):
                    m = pe.transpose(bank_b(3 + k % 2)[0:DC, CP * j:CP * j + CP], cq[:, 4 * k + j, :],
                                     ident_b[0:CP, 0:CP])
                m.then_inc(s_tr, 1)

            def linears(first, w, src, pieces=None):
                for n in range(NQ):
                    pe.wait_ge(s_mmc, first + n + 1)
                    if pieces is not None:
                        pe.wait_ge(pieces, (QC * n + QC - 1) // PC + 1)
                    pe.matmul(bank(5 + (first + n) % 2, QC), w, src[:, QC * n:QC * n + QC],
                              start=True, stop=True).then_inc(s_mm, 1)

            pe.wait_ge(s_wT, 6)
            pe.wait_ge(s_trc, NQ + 2)
            linears(0, wT[0:DC, 0:P], qa[0:DC, :])
            spread_max(Q_VIS)
            linears(NQ, wT[:, P:2 * P], qb, s_vq)
            spread_max(Q_IMG)
            spread_max(Q_X)
            pe.wait_ge(s_trc, NQ + 2)
            pe.wait_ge(s_mmc, 2 * NQ + 2)
            w = T // XP
            for n in range(XP):
                pe.wait_ge(s_xq, n + 1)
                for j in range(B // XP):
                    m = pe.transpose(bank_b(n)[:, P * j:P * j + P], tok_b[:, w * n + P * j:w * n + P * j + P],
                                     ident_b[:, :])
                m.then_inc(s_tr, 1)

            pe.sem_inc(s_av[0], 1)
            pe.sem_inc(s_av[1], 1)

            def project(i):
                wait(pe, s_f, i)
                pe.matmul(bank(0), wT[:, 2 * P:3 * P], xqT[:, g4(i)], start=True, stop=True).then_inc(s_fmm, 1)

            def keys_product(l, i):
                wait(pe, s_sub[l], i + 1 if l == 0 else i - 1)
                wait(pe, s_k[l], i)
                pe.matmul(bank(1 + l, GC), attT[:, l, :, :].rearrange("p a k -> p (a k)"), qa[:, c4(i)],
                          start=True, stop=True).then_inc(s_kmm[l], 1)

            def turn_keys(i, n):
                pe.wait_ge(s_k[0], i + 1)
                pe.wait_ge(s_k[1], i + 1)
                wait(pe, s_ktc, i)
                pe.sem_inc(s_passed3, 1)
                for b in range(GB):
                    for l in range(2):
                        m = pe.transpose(bank(7, GB * P, CT)[:, P * b + KV * l:P * b + KV * l + KV],
                                         kT[l][n % GR][0:KV, CT * b:CT * b + CT], ident[0:KV, 0:KV])
                m.then_inc(s_kt, 1)

            def scores(l, i, n, keys_read):
                pe.wait_ge(s_f if l == 0 else s_up[0], i + 1 + l)
                pe.wait_ge(s_k[l], keys_read)
                src = fused1 if l else fused0
                for b in range(GB):
                    m = pe.matmul(bank(1 + l)[:, CT * b:CT * b + CT], src[n % GR][:, P * b:P * b + P],
                                  kT[l][n % GR][:, CT * b:CT * b + CT], start=True, stop=True)
                m.then_inc(s_smm[l], 1)

            def turn(l, i, n):
                pe.wait_ge(s_p[l], i + 1)
                pe.wait_ge(s_pt[l], i + 1)
                for b in range(GB):
                    m = pe.transpose(bank(3 + l, 512, CT)[:, P * b:P * b + P], prob[l][n % 2][:, b, :], ident[:, :])
                m.then_inc(s_t[l], 1)

            def attend(l, i, n):
                pe.wait_ge(s_pt[l], i + 2)
                pe.wait_ge(s_ktc, i + 1)
                pe.wait_ge(s_up[l], i + 1)
                for b in range(GB):
                    m = pe.matmul(bank(5 + l)[:, P * b:P * b + P],
                                  ktok[l][n % (GR if l else 2)][:, P * b:P * b + P],
                                  probT[l][:, P * b:P * b + P], start=True, stop=True)
                m.then_inc(s_av[l], 1)

            def step(t, n, last):
                if last < G:
                    scores(0, t, n, t + 1)
                if 2 <= last < G + 2:
                    scores(1, t - 2, n + 2, t + 1 if last < G else G)
                if 1 <= last < G + 1:
                    turn(0, t - 1, n + 1)
                if 3 <= last:
                    turn(1, t - 3, n + 1)
                if last < G - 1:
                    project(t + 1)
                    keys_product(0, t + 1)
                if 1 <= last < G + 1:
                    attend(0, t - 1, n - 1)
                if last < G - 1:
                    keys_product(1, t + 1)
                if 3 <= last:
                    attend(1, t - 3, n - 3)
                if last < G:
                    turn_keys(t, n)

            pe.wait_ge(s_trd, XP // 2)
            pe.wait_ge(s_trc, NQ + 2 + XP // 2)
            pe.wait_ge(s_iq, NP)
            keys_product(0, 0)
            keys_product(1, 0)
            project(0)
            attention_steps(lambda a, b, body: for_loop(pe, a, b, body), step)

            spread_max(Q_CAT)
            pe.wait_ge(s_catq, XP + 1)

            def hidden(i, c):
                pe.matmul(bank(c), f1T[:, 0, P * c:P * c + P], tok_b[:, g4(i)], start=True, stop=False)
                return pe.matmul(bank(c).rearrange("p (b s) -> p b s", b=GB), f1T[:, 1, P * c:P * c + P],
                                 avg_q[:, bass.ds(i * GB, GB)].unsqueeze(2).to_broadcast([P, GB, S]),
                                 start=False, stop=True)

            with pe.Fori(0, G) as i:
                for pair in range(2):
                    pe.wait_ge(s_hm, i * 2 + pair + 1)
                    hidden(i, 2 * pair)
                    hidden(i, 2 * pair + 1).then_inc(s_h, 1)
            spread_max(Q_H)

            def hidden_again(i):
                for pair in range(2):
                    wait(pe, s_relu, i * 4 + (2 * pair - 2))
                    hidden(i, 2 * pair)
                    hidden(i, 2 * pair + 1).then_inc(s_h2, 1)

            def out_product(i):
                pe.wait_ge(s_hq, i + 1)
                wait(pe, s_x1, i)
                for b in range(GB):
                    for c in range(NC):
                        m = pe.matmul(bank(4)[:, P * b:P * b + P], hq[:, c, P * b:P * b + P], f2T[:, c, :],
                                      start=(c == 0), stop=(c == NC - 1))
                m.then_inc(s_f2, 1)

            def turn_x2(i):
                pe.wait_ge(s_xn2, i + 1)
                wait(pe, s_x2c, i)
                for b in range(GB):
                    m = pe.transpose(bank(5)[:, P * b:P * b + P], xs[:, b, :], ident[:, :])
                m.then_inc(s_x2t, 1)

            def logits(i):
                pe.wait_ge(s_x2c, i + 1)
                for b in range(GB):
                    m = pe.matmul(psum[:, 6, bass.ds(i * GB * NX + b * NX, NX)], xsT[:, P * b:P * b + P], rwT,
                                  start=True, stop=True)
                m.then_inc(s_lg, 1)

            def step(t, last):
                if 3 <= last:
                    turn_x2(t - 3)
                if last < G - 1:
                    hidden_again(t + 1)
                if 0 <= last < G:
                    out_product(t)
                if 3 <= last:
                    logits(t - 3)
            hidden_steps(lambda a, b, body: for_loop(pe, a, b, body), step)

            pe.wait_ge(s_v, 1)
            for n in range(4):
                m = pe.transpose(bank(0)[:, P * n:P * n + P], route(2)[:, P * n:P * n + P], ident[:, :])
            m.then_inc(s_vt, 1)
            with pe.Fori(0, LEVELS) as k:
                pe.wait_ge(s_cnt, k + 1)
                pe.matmul(bank(1, 3), same_expert[:, :], cnt[:, :], start=True, stop=True).then_inc(s_cnt2, 1)
            pe.wait_ge(s_thr, 1)
            pe.transpose(psum[0:1, 2, 0:P], thr[:, :], ident[:, :]).then_inc(s_thr_r, 1)
            pe.wait_ge(s_thr_c, 1)
            pe.matmul(bank(3, NX), ones[0:1, :], t64[0][0:1, 0:NX], start=True, stop=True).then_inc(s_thr_s, 1)
            above, ties, final = (tok_b[:, n * 512:(n + 1) * 512] for n in range(3))
            pe.wait_ge(s_ms, 1)
            pe.matmul(bank(4), ones_b[:, :], above, start=True, stop=True)
            pe.matmul(bank(5), ones_b[:, :], ties, start=True, stop=True)
            pe.matmul(bank(6), before_b[:, :], ties, start=True, stop=True).then_inc(s_ps, 1)
            pe.wait_ge(s_ms, 2)
            pe.matmul(bank(0), ones_b[:, :], final, start=True, stop=True)
            pe.matmul(bank(1), before_b[:, :], final, start=True, stop=True).then_inc(s_ps, 1)
            def place(i, first=False, last=False):
                pe.wait_ge(s_hr, i + 1)
                pe.wait_ge(s_hp, i + 1)
                pe.wait_ge(s_hu, i + 1)
                rows_, tiles = hot_row[:, bass.ds(i * HT, HT), :], hot_tile[:, bass.ds(i * HT, HT), :, :]
                for t in range(HT):
                    m = pe.matmul(bank(2, 2 * NT), rows_[:, t, :], tiles[:, t, :, :].rearrange("p a c -> p (a c)"),
                                  start=first and t == 0, stop=last and t == HT - 1)
                m.then_inc(s_inv_mm, 1)
            for i in range(B // HT):
                place(i, first=i == 0, last=i == B // HT - 1)

            pe.wait_ge(s_idx, 3)
            pe.wait_ge(s_moe, 16 * 10)

            def turn_rows(a, n):
                pe.wait_ge(s_prep, a + 1)
                wait(pe, s_gc, a - 1)
                pe.transpose(bank(n % 2, P), gn[n % DEPTH], ident[:, :]).then_inc(s_gt, 1)

            def layer1(a, n):
                pe.wait_ge(s_gc, a + 1)
                wait(pe, s_hc, a - 1)
                wait(pe, s_hd, a - 1)
                for c in range(NC):
                    dst = bank(2 + n % 2)[:, P * c:P * c + P] if c < NC - 1 else bank(6 + n % 2, P)
                    m = pe.matmul(dst, w1_now[n % DEPTH][:, P * c:P * c + P], gT[n % DEPTH], start=True, stop=True)
                m.then_inc(s_l1, 1)

            def layer2(a, n):
                e = pe.value_load(expert_of[0:1, bass.ds(a, 1)], min_val=0, max_val=NX - 1)
                pe.wait_ge(s_hc, a + 1)
                pe.wait_ge(s_hd, a + 1)
                wait(pe, s_y, a - 1)
                for c in range(NC):
                    m = pe.matmul(bank(4 + n % 2, E), hT[n % DEPTH][:, P * c:P * c + P],
                                  w2s[:, bass.ds(e, 1), c, :].rearrange("p e d -> p (e d)"),
                                  start=(c == 0), stop=(c == NC - 1))
                m.then_inc(s_l2, 1)

            turn_rows(0, 0)
            turn_rows(1, 1)
            for a in range(RING):
                turn_rows(a + 2, a + 2)
                layer1(a, a)
                if a >= 2:
                    layer2(a - 2, a - 2)
            with pe.Fori(1, NT // RING - 1) as r:
                for n in range(RING):
                    turn_rows(r * RING + (n + 2), n + 2)
                    layer1(r * RING + n, n)
                    layer2(r * RING + (n - 2), n - 2)
            for a in range(NT - RING, NT + 2):
                if a + 2 < NT:
                    turn_rows(a + 2, a + 2)
                if a < NT:
                    layer1(a, a)
                layer2(a - 2, a - 2)

        @block.vector
        def _(dve):
            ch = Chain(dve, s_dve)

            def do(ins):
                ch.link(ins)
                ch.join()

            def global_scale(k, uses, meanwhile=(None, None)):
                if meanwhile[0]:
                    meanwhile[0]()
                dve.wait_ge(s_grow, k + 1)
                dve.tensor_reduce(gmax[0:1, k:k + 1], psum[0:1, 7, 0:P], AX, ALU.max).then_inc(s_gm, 1)
                if meanwhile[1]:
                    meanwhile[1]()
                dve.wait_ge(s_gcol, k + 1)
                do(dve.tensor_scalar(iscale[:, k:k + 1], psum[:, 7, P + k:P + k + 1], 1e-8, 1.0 / 127.0, ALU.max, ALU.mult))
                dve.reciprocal(inv[:, k:k + 1], iscale[:, k:k + 1]).then_inc(s_inv, 1)
                for w in uses:
                    ins = dve.tensor_tensor(scale[:, w:w + 1], ws[:, w:w + 1], iscale[:, k:k + 1], ALU.mult)
                    if w == uses[-1]:
                        ins.then_inc(s_sc, 1)

            def layer_norm_steps(st, mean, n, ready, count, done):
                me, m2e, mo, m2o = (st[:, :, j] for j in (1, 2, 4, 5))
                a, b_, v = tmp[:, 0, 0:n], tmp[:, 1, 0:n], tmp[:, 2, 0:n]

                def sums():
                    dve.wait_ge(ready, count)
                    ch.link(dve.tensor_tensor(a, me, mo, ALU.add))
                    ch.link(dve.tensor_tensor(b_, me, mo, ALU.subtract))
                    ch.link(dve.tensor_tensor(v, m2e, m2o, ALU.add))

                def square():
                    ch.join()
                    dve.tensor_scalar(mean, a, 0.5, None, ALU.mult).then_inc(s_mean, 1)
                    ch.link(dve.tensor_tensor(b_, b_, b_, ALU.mult))

                def combine():
                    ch.join()
                    ch.link(dve.scalar_tensor_tensor(v, b_, float(E) / 4, v, ALU.mult, ALU.add))

                def finish():
                    ch.join()
                    dve.tensor_scalar(v, v, 1.0 / E, EPS, ALU.mult, ALU.add).then_inc(done, 1)
                return sums, square, combine, finish

            w = CJ * DC // NP
            dve.wait_ge(s_const, 12)
            for n in range(NP):
                dve.wait_ge(s_ctx[n], 16)
                ch.link(dve.tensor_reduce(part[0:CP, 0, n:n + 1], ctx_raw[0:CP, w * n:w * n + w], AX, ALU.max,
                                          apply_absolute_value=True))
            ch.join()
            dve.tensor_reduce(amax[0:CP, Q_CTX:Q_CTX + 1], part[0:CP, 0, 0:NP], AX, ALU.max).then_inc(s_amax, 1)

            def weight_sums():
                dve.wait_ge(s_w, 16 * 7)
                for k in range(7):
                    rows_ = KV if k in (ATT0, ATT1) else P
                    dve.tensor_reduce(wsum[0:rows_, k:k + 1], wslice(wraw, k), AX, ALU.add,
                                      apply_absolute_value=True).then_inc(s_wsum, 1)

            global_scale(Q_CTX, [], (None, weight_sums))
            dve.wait_ge(s_wtot, 1)
            do(dve.tensor_tensor(ws[:, :], bank(6, 7), inv_counts[:, :], ALU.mult))
            do(dve.tensor_scalar(ws[:, :], ws[:, :], 1e-5, None, ALU.max))
            dve.tensor_tensor(scale[:, D2V:D2V + 1], ws[:, D2V:D2V + 1], iscale[:, Q_CTX:Q_CTX + 1], ALU.mult
                              ).then_inc(s_sc, 1)
            ch.link(dve.tensor_scalar(wlim[:, 0, :], ws[:, :], 0.5, None, ALU.mult))
            do(dve.tensor_scalar(wlim[:, 1, :], ws[:, :], -0.5, None, ALU.mult))
            for k in range(7):
                rows_ = KV if k in (ATT0, ATT1) else P
                ch.link(dve.tensor_scalar(wslice(wneg, k), wslice(wraw, k), wlim[0:rows_, 1, k:k + 1], None, ALU.is_lt))
            ch.join()
            for k in range(7):
                rows_ = KV if k in (ATT0, ATT1) else P
                dve.scalar_tensor_tensor(wslice(wq, k), wslice(wraw, k), wlim[0:rows_, 0, k:k + 1], wslice(wneg, k),
                                         ALU.is_gt, ALU.subtract).then_inc(s_wq, 1)
            for n in range(NP):
                dve.wait_ge(s_fs, n + 1)
                dve.tensor_scalar(ctx_q[:, w * n:w * n + w], ctx_raw[0:CP, w * n:w * n + w], MAGIC, None, ALU.subtract
                                  ).then_inc(s_cq, 1)

            for n in range(XP):
                dve.wait_ge(s_x[n], 16)
                for t in range(B // XP * n, B // XP * (n + 1)):
                    m = dve.bn_stats(stats[:, t, :], xall[:, t, 0:E])
            m.then_inc(s_bn0, 1)
            for small in layer_norm_steps(stats[:, :, :], xall[:, :, E], B, s_bn0, 1, s_var):
                small()

            def less_mean(n):
                t = slice(n * 2 * GB, (n + 1) * 2 * GB)
                dve.tensor_tensor(xn[:, t, :], xall[:, t, 0:E], xall[:, t, E:E + 1].to_broadcast([P, 2 * GB, E]),
                                  ALU.subtract).then_inc(s_lm, 1)

            def over_deviation(n):
                t = slice(n * 2 * GB, (n + 1) * 2 * GB)
                dve.wait_ge(s_lm, n + 1)
                ch.link(dve.tensor_tensor(xn[:, t, :], xn[:, t, :],
                                          xall[:, t, E + 1:E + 2].to_broadcast([P, 2 * GB, E]), ALU.mult))

            def maxima(first):
                for n in range(NP):
                    dve.wait_ge(s_mmc, first + 2 + -(-PC * (n + 1) // QC))
                    ch.link(dve.tensor_reduce(part[:, 0, n:n + 1], feat[:, PC * n:PC * n + PC], AX, ALU.max,
                                              apply_absolute_value=True))
                ch.join()

            def take_magic_off(dst, first, done, meanwhile=()):
                for n in range(NP):
                    if n < len(meanwhile):
                        meanwhile[n]()
                    dve.wait_ge(s_fs, first + n + 1)
                    dve.tensor_scalar(dst[:, PC * n:PC * n + PC], scaled[:, PC * n:PC * n + PC], MAGIC, None,
                                      ALU.subtract).then_inc(done, 1)

            maxima(0)
            dve.tensor_reduce(amax[:, Q_VIS:Q_VIS + 1], part[:, 0, 0:NP], AX, ALU.max).then_inc(s_amax, 1)
            dve.wait_ge(s_std, 1)
            dve.wait_ge(s_mean, 1)
            dve.reciprocal(xall[:, :, E + 1], tmp[:, 3, :]).then_inc(s_rs0, 1)
            dve.wait_ge(s_wtr, 3)
            global_scale(Q_VIS, [IMG], (lambda: less_mean(0), lambda: less_mean(1)))
            dve.wait_ge(s_rs0, 1)
            over_deviation(0)
            less_mean(2)
            take_magic_off(qb, NP, s_vq, [lambda n=n: (over_deviation(n), less_mean(n + 2))
                                          for n in range(1, VG // 2 - 2)])
            over_deviation(VG // 2 - 2)
            over_deviation(VG // 2 - 1)

            def ln_max(n):
                lo, hi = (n * VG * GT // (NP - 1), (n + 1) * VG * GT // (NP - 1)) if n < NP - 1 else (VG * GT, T)
                ch.link(dve.tensor_reduce(part[:, 1, n:n + 1], big[:, lo:hi], AX, ALU.max, apply_absolute_value=True))

            ch.join()
            ln_max(0)
            maxima(NQ)
            dve.tensor_reduce(amax[:, Q_IMG:Q_IMG + 1], part[:, 0, 0:NP], AX, ALU.max).then_inc(s_amax, 1)
            global_scale(Q_IMG, [ATT0, ATT1], (None, lambda: ln_max(1)))
            ln_max(2)
            dve.wait_ge(s_xn, (G - VG) // 2)
            ln_max(3)
            ch.join()
            dve.tensor_reduce(amax[:, Q_X:Q_X + 1], part[:, 1, 0:NP], AX, ALU.max).then_inc(s_amax, 1)
            global_scale(Q_X, [TXT], (lambda: take_magic_off(qa, 2 * NP, s_iq), None))

            def quantise_tokens(k, scaled_, done):
                w, waits = T // XP, 0
                for n in range(XP):
                    v = big[:, w * n:w * n + w]
                    if n in OWN:
                        dve.wait_ge(s_inv, k + 1)
                        do(dve.tensor_scalar(v, v, inv[:, k:k + 1], MAGIC, ALU.mult, ALU.add))
                    else:
                        waits += 1
                        dve.wait_ge(scaled_, waits)
                    dve.tensor_scalar(tok_b[:, w * n:w * n + w], v, MAGIC, None, ALU.subtract).then_inc(done, 1)
            quantise_tokens(Q_X, s_xs, s_xq)
            w = T // XP
            for n in range(XP // 2, XP):
                dve.wait_ge(s_tr, NQ + n + 1)
                dve.tensor_copy(xqT[:, w * n:w * n + w], bank_b(n)).then_inc(s_trd, 1)

            for l in range(2):
                dve.sem_inc(s_sub[l], 1)
                dve.sem_inc(s_up[l], 1)

            def scores_in(l):
                return bank(1 + l, GC).rearrange("p (b c) -> p b c", b=GB)

            def maximum(l, i):
                dve.wait_ge(s_smm[l], i + 1)
                dve.tensor_reduce(amx[:, l, :], scores_in(l), AX, ALU.max).then_inc(s_mx[l], 1)

            def less_max(l, i, n):
                dve.wait_ge(s_mx[l], i + 1)
                wait(dve, s_t[l], i - 1)
                dve.tensor_tensor(prob[l][n % 2], scores_in(l), amx[:, l, :].unsqueeze(2).to_broadcast([P, GB, CT]),
                                  ALU.subtract).then_inc(s_sub[l], 1)

            def total(l, i, n):
                dve.wait_ge(s_e[l], i + 1)
                dve.tensor_reduce(asum[:, l, :], prob[l][n % 2], AX, ALU.add).then_inc(s_sum[l], 1)

            def invert(l, i):
                dve.wait_ge(s_sum[l], i + 1)
                wait(dve, s_p[l], i)
                dve.reciprocal(arec[:, l, :], asum[:, l, :]).then_inc(s_r[l], 1)

            def update(l, i, n):
                dve.wait_ge(s_av[l], i + 2)
                dst, src = (big[:, g4(i)], fused1[n % GR]) if l else (fused1[n % GR], fused0[n % GR])
                dve.scalar_tensor_tensor(dst, bank(5 + l), 0.1, src, ALU.mult, ALU.add).then_inc(s_up[l], 1)

            def maximum_fused(i):
                dve.wait_ge(s_up[1], i + 2)
                dve.tensor_reduce(part[:, 2, bass.ds(i, 1)], big[:, g4(i)], AX, ALU.max,
                                  apply_absolute_value=True).then_inc(s_fm, 1)

            def step(t, n, last):
                first, second = last < G, 2 <= last < G + 2
                if first:
                    maximum(0, t)
                if second:
                    maximum(1, t - 2)
                if first:
                    less_max(0, t, n)
                if second:
                    less_max(1, t - 2, n + 2)
                if first:
                    total(0, t, n)
                if second:
                    total(1, t - 2, n + 2)
                if first:
                    invert(0, t)
                if second:
                    invert(1, t - 2)
                if 1 <= last < G + 1:
                    update(0, t - 1, n - 1)
                if 3 <= last:
                    update(1, t - 3, n - 3)
                    maximum_fused(t - 3)
            attention_steps(lambda a, b, body: for_loop(dve, a, b, body), step)

            dve.wait_ge(s_avg, CT // 11 - 1 + 10)
            do(dve.tensor_scalar(avg[:, :], avg[:, :], 1.0 / CT, None, ALU.mult))
            ch.link(dve.tensor_reduce(part[:, 3, 0:1], avg[:, :], AX, ALU.max, apply_absolute_value=True))
            dve.wait_ge(s_fm, G)
            ch.join()
            do(dve.tensor_reduce(part[:, 3, 1:2], part[:, 2, 0:G], AX, ALU.max))
            dve.tensor_tensor(amax[:, Q_CAT:Q_CAT + 1], part[:, 3, 0:1], part[:, 3, 1:2], ALU.max).then_inc(s_amax, 1)
            global_scale(Q_CAT, [F1])
            dve.wait_ge(s_inv, Q_CAT + 1)
            do(dve.tensor_scalar(avg[:, :], avg[:, :], inv[:, Q_CAT:Q_CAT + 1], MAGIC, ALU.mult, ALU.add))
            dve.tensor_scalar(avg_q[:, :], avg[:, :], MAGIC, None, ALU.subtract).then_inc(s_catq, 1)
            quantise_tokens(Q_CAT, s_cs, s_catq)

            dve.sem_inc(s_hm, 2)
            hmax = tmp[:, :, :].rearrange("p a b -> p (a b)")[:, 0:G * NC].rearrange("p (g c) -> p g c", c=NC)
            with dve.Fori(0, G) as i:
                for pair in range(2):
                    dve.wait_ge(s_h, i * 2 + pair + 1)
                    dve.tensor_reduce(hmax[:, bass.ds(i, 1), 2 * pair:2 * pair + 2].rearrange("p g c -> p (g c)"),
                                      psum[:, 2 * pair:2 * pair + 2, :], AX, ALU.max).then_inc(s_hm, 1)
            dve.wait_ge(s_hm, 2 * G + 2)
            do(dve.tensor_reduce(part[:, 0, 0:NC], hmax.rearrange("p g c -> p c g"), AX, ALU.max))
            do(dve.scalar_tensor_tensor(part[:, 1, 0:NC], part[:, 0, 0:NC], scale[:, F1:F1 + 1], bcol[:, 5:5 + NC],
                                        ALU.mult, ALU.add))
            do(dve.tensor_scalar(part[:, 1, 0:NC], part[:, 1, 0:NC], 0.0, None, ALU.max))
            dve.tensor_reduce(amax[:, Q_H:Q_H + 1], part[:, 1, 0:NC], AX, ALU.max).then_inc(s_amax, 1)
            dve.wait_ge(s_grow, Q_H + 1)
            dve.tensor_reduce(gmax[0:1, Q_H:Q_H + 1], psum[0:1, 7, 0:P], AX, ALU.max).then_inc(s_gm, 1)
            dve.wait_ge(s_gcol, Q_H + 1)
            do(dve.tensor_scalar(iscale[:, Q_H:Q_H + 1], psum[:, 7, P + Q_H:P + Q_H + 1], 1e-8, 1.0 / 127.0,
                                 ALU.max, ALU.mult))
            do(dve.reciprocal(inv[:, Q_H:Q_H + 1], iscale[:, Q_H:Q_H + 1]))
            ch.link(dve.tensor_tensor(scale[:, F2:F2 + 1], ws[:, F2:F2 + 1], iscale[:, Q_H:Q_H + 1], ALU.mult))
            ch.link(dve.tensor_scalar(h_bias[:, :], bcol[:, 5:5 + NC], inv[:, Q_H:Q_H + 1], None, ALU.mult))
            ch.join()
            dve.tensor_tensor(h_scale[:, :], scale[:, F1:F1 + 1], inv[:, Q_H:Q_H + 1], ALU.mult).then_inc(s_sc, 1)

            def quantise_hidden(i):
                dve.wait_ge(s_relu, (i + 1) * 4)
                wait(dve, s_f2, i)
                dve.tensor_scalar(hq[:, :, :], u[:, :, :], MAGIC, MAGIC, ALU.add, ALU.subtract).then_inc(s_hq, 1)

            def x1(i):
                xr = xall[:, bass.ds(i * GB, GB), 0:E]
                dve.wait_ge(s_f2, i + 1)
                dve.scalar_tensor_tensor(xr, bank(4).rearrange("p (b d) -> p b d", b=GB), scale[:, F2:F2 + 1],
                                         xr, ALU.mult, ALU.add).then_inc(s_x1, 1)

            def x1_stats(i):
                dve.wait_ge(s_x1, i + 1)
                dve.sem_inc(s_passed2, 1)
                for b in range(GB):
                    m = dve.bn_stats(stats[:, b, :], xall[:, bass.ds(i * GB + b, 1), 0:E].rearrange("p t d -> p (t d)"))
                m.then_inc(s_bn, 1)

            def inverse_deviation(i):
                dve.wait_ge(s_std2, i + 1)
                dve.reciprocal(xall[:, bass.ds(i * GB, GB), E + 1], tmp[:, 3, 0:GB]).then_inc(s_rs, 1)

            def normalise(i, b):
                if b == 0:
                    dve.wait_ge(s_rs, i + 1)
                    dve.wait_ge(s_mean, i + 2)
                    wait(dve, s_x2t, i)
                row = xall[:, bass.ds(i * GB + b, 1), :].rearrange("p t d -> p (t d)")
                m = dve.tensor_scalar(xs[:, b, :], row[:, 0:E], row[:, E:E + 1], row[:, E + 1:E + 2],
                                      ALU.subtract, ALU.mult)
                if b == GB - 1:
                    m.then_inc(s_xn2, 1)

            def step(t, last):
                ahead, behind = 1 <= last < G + 1, 2 <= last < G + 2
                if 0 <= last < G:
                    quantise_hidden(t)
                if ahead:
                    x1(t - 1)
                if behind:
                    inverse_deviation(t - 2)
                if ahead:
                    x1_stats(t - 1)
                    small = layer_norm_steps(st2, xall[:, bass.ds((t - 1) * GB, GB), E], GB, s_bn, t, s_var2)
                for b in range(GB):
                    if ahead:
                        small[b]()
                    if behind:
                        normalise(t - 2, b)

            dve.wait_ge(s_res, G)
            hidden_steps(lambda a, b, body: ch.loop(a, b, 5, body), step)

            def v3(ap):
                return ap.rearrange("p (t e) -> p t e", e=NX)

            def over_e(ap):
                return ap.unsqueeze(2).to_broadcast([P, B, NX])

            def over_t(ap):
                return ap.unsqueeze(1).to_broadcast([P, B, NX])

            dve.wait_ge(s_lg, G)
            do(dve.tensor_reduce(t64[1][:, :], v3(bank(6)), AX, ALU.max))
            dve.tensor_tensor(v3(route(0)), v3(bank(6)), over_e(t64[1][:, :]), ALU.subtract).then_inc(s_d, 1)
            dve.wait_ge(s_ex, 1)
            do(dve.tensor_reduce(t64[1][:, :], v3(route(0)), AX, ALU.add))
            do(dve.reciprocal(t64[2][:, :], t64[1][:, :]))
            do(dve.tensor_tensor(v3(route(0)), v3(route(0)), over_e(t64[2][:, :]), ALU.mult))
            top = t64[3][:, :]
            do(dve.tensor_reduce(top, v3(route(0)), AX, ALU.max))
            do(dve.tensor_tensor(v3(route(0)), v3(route(0)), over_e(top), ALU.is_equal))
            do(dve.tensor_tensor(v3(route(0)), v3(route(0)), over_t(rank8[:, :]), ALU.mult))
            do(dve.tensor_reduce(t64[2][:, :], v3(route(0)), AX, ALU.max))
            do(dve.tensor_tensor(v3(route(1)), v3(route(0)), over_e(t64[2][:, :]), ALU.is_equal))
            dve.tensor_tensor(v3(route(2)), v3(route(1)), over_e(top), ALU.mult).then_inc(s_v, 1)
            dve.wait_ge(s_vt, 1)
            ch.link(dve.tensor_copy(route(3), bank(0)))
            ch.link(dve.memset(thr[:, :], 0.0))
            ch.link(dve.tensor_copy(cand[:, :], steps[:, 0, :]))
            ch.join()

            def level(k, following):
                for j in range(3):
                    m = dve.tensor_scalar(route(4 + j), route(3), cand[:, j:j + 1], None, ALU.is_ge, ALU.add,
                                          accum_out=cnt[:, j:j + 1])
                m.then_inc(s_cnt, 1)
                dve.wait_ge(s_cnt2, k + 1)
                do(dve.tensor_scalar(reached[:, :], bank(1, 3), float(CAP), None, ALU.is_ge, ALU.add,
                                     accum_out=met[:, :]))
                at_k = steps[:, bass.ds(k, 1), 0:1].rearrange("p a b -> p (a b)")
                do(dve.scalar_tensor_tensor(thr[:, :], met[:, :], at_k, thr[:, :], ALU.mult, ALU.add))
                if following:
                    do(dve.tensor_scalar(cand[:, :], steps[:, bass.ds(k + 1, 1), :].rearrange("p a b -> p (a b)"),
                                         thr[:, :], None, ALU.add))

            def body(r):
                for n in range(2):
                    level(r * 2 + n, True)
            ch.loop(0, LEVELS // 2 - 1, 6, body)
            level(LEVELS - 2, True)
            level(LEVELS - 1, False)
            dve.tensor_copy(thr[:, :], thr[:, :]).then_inc(s_thr, 1)
            dve.wait_ge(s_thr_r, 1)
            dve.tensor_copy(t64[0][0:1, 0:NX], psum[0:1, 2, 0:NX]).then_inc(s_thr_c, 1)
            dve.wait_ge(s_thr_s, 1)
            do(dve.tensor_copy(thr8[:, :], bank(3, NX)))

            above, ties, final = (tok_b[:, n * 512:(n + 1) * 512] for n in range(3))
            ch.link(dve.tensor_tensor(v3(above), v3(route(2)), over_t(thr8[:, :]), ALU.is_gt))
            do(dve.tensor_tensor(v3(route(0)), v3(route(2)), over_t(thr8[:, :]), ALU.is_equal))
            dve.tensor_tensor(v3(ties), v3(route(0)), v3(route(1)), ALU.mult).then_inc(s_ms, 1)

            def et(ap):
                return ap.rearrange("p (e t) -> p t e", e=NX)

            def te(ap):
                return ap.rearrange("p (t e) -> p e t", e=NX)

            def earlier(columns, rows_, own, full):
                do(dve.tensor_copy(et(own), v3(columns)))
                do(dve.tensor_tensor_scan(full, seg[:, :], own, 0.0, ALU.mult, ALU.add))
                do(dve.tensor_tensor(own, full, own, ALU.subtract))
                do(dve.tensor_tensor(v3(route(7)), et(own), v3(rows_), ALU.add))

            dve.wait_ge(s_ps, 1)
            do(dve.tensor_reduce(n8[0][:, :], te(bank(4)), AX, ALU.add))
            do(dve.tensor_scalar(n8[1][:, :], n8[0][:, :], -1.0, float(CAP), ALU.mult, ALU.add))
            earlier(bank(5), bank(6), route(5), route(6))
            do(dve.tensor_tensor(v3(route(7)), v3(route(7)), over_t(n8[1][:, :]), ALU.is_lt))
            do(dve.tensor_tensor(route(7), route(7), ties, ALU.mult))
            do(dve.tensor_tensor(route(7), route(7), above, ALU.add))
            do(dve.tensor_reduce(t64[1][:, :], v3(route(7)), AX, ALU.add))
            do(dve.tensor_scalar(t64[1][:, :], t64[1][:, :], -1.0, 1.0, ALU.mult, ALU.add))
            do(dve.tensor_tensor(v3(route(7))[:, :, 0], v3(route(7))[:, :, 0], t64[1][:, :], ALU.add))
            do(dve.tensor_copy(route(8), route(7)))
            dve.tensor_copy(final, route(7)).then_inc(s_ms, 1)

            dve.wait_ge(s_ps, 2)
            earlier(bank(0), bank(1), route(5), route(6))
            do(dve.tensor_copy(n8[0][:, :], route(6).rearrange("p (e t) -> p e t", e=NX)[:, :, B - 1]))
            do(dve.tensor_scalar(n8i[0][:, :], n8[0][:, :], float(P - 1), None, ALU.add))
            do(dve.tensor_scalar(n8i[1][:, :], n8i[0][:, :], 7, None, ALU.arith_shift_right))
            do(dve.tensor_copy(n8[1][:, :], n8i[1][:, :]))
            do(dve.tensor_tensor_scan(n8[2][:, :], ones[:, 0:NX], n8[1][:, :], 0.0, ALU.mult, ALU.add))
            do(dve.tensor_tensor(n8[3][:, :], n8[2][:, :], n8[1][:, :], ALU.subtract))
            do(dve.tensor_scalar(n8[3][:, :], n8[3][:, :], float(P), None, ALU.mult))
            do(dve.tensor_tensor(v3(route(7)), v3(route(7)), over_t(n8[3][:, :]), ALU.add))
            do(dve.tensor_tensor(route(7), route(7), route(8), ALU.mult))
            do(dve.tensor_reduce(t64[1][:, :], v3(route(7)), AX, ALU.add))
            do(dve.tensor_copy(t64i[0][:, :], t64[1][:, :]))
            ch.link(dve.tensor_scalar(t64i[1][:, :], t64i[0][:, :], 7, None, ALU.arith_shift_right))
            ch.link(dve.tensor_scalar(t64i[2][:, :], t64i[0][:, :], P - 1, None, ALU.bitwise_and))
            ch.join()
            ch.link(dve.tensor_copy(t64[4][:, :], t64i[1][:, :]))
            ch.link(dve.tensor_copy(t64[5][:, :], t64i[2][:, :]))
            ch.join()

            def one_hots(i):
                t = bass.ds(i * HT, HT)
                dve.tensor_tensor(hot[:, t, :], tile_no_b[:, :].unsqueeze(1).to_broadcast([P, HT, NT]),
                                  t64[4][:, t].unsqueeze(2).to_broadcast([P, HT, NT]), ALU.is_equal).then_inc(s_ht, 1)
                dve.tensor_tensor(hot_row[:, t, :], row_no_b[:, :].unsqueeze(1).to_broadcast([P, HT, P]),
                                  t64[5][:, t].unsqueeze(2).to_broadcast([P, HT, P]), ALU.is_equal).then_inc(s_hr, 1)
            for i in range(B // HT):
                one_hots(i)

            m = big[0:1, 10 * 512:10 * 512 + NT * NX].rearrange("p (a e) -> p a e", e=NX)
            do(dve.tensor_tensor(m, tile_no[0:1, :].unsqueeze(2).to_broadcast([1, NT, NX]),
                                 n8[2][0:1, :].unsqueeze(1).to_broadcast([1, NT, NX]), ALU.is_ge))
            m2 = big[0:1, 12 * 512:12 * 512 + NT]
            do(dve.tensor_reduce(m2, m, AX, ALU.add))
            dve.tensor_scalar(expert_of[:, :], m2, float(NX - 1), None, ALU.min).then_inc(s_idx, 1)
            dve.wait_ge(s_inv_mm, B // HT)
            w = [big[:, (13 + j) * 512:(13 + j) * 512 + NT] for j in range(3)]
            do(dve.tensor_scalar(w[0], bank(2)[:, NT:2 * NT], float(P), -float(P), ALU.mult, ALU.add))
            do(dve.tensor_tensor(w[0], bank(2)[:, 0:NT], w[0], ALU.add))
            dve.tensor_scalar(src_of[:, :], w[0], 0.0, None, ALU.max).then_inc(s_idx, 1)
            do(dve.tensor_scalar(w[1], w[0], 0.0, float(FAR + P), ALU.is_lt, ALU.mult))
            dve.tensor_tensor(dst_of[:, :], w[0], w[1], ALU.add).then_inc(s_idx, 1)

            dve.wait_ge(s_moe, 16 * 10)
            dve.wait_ge(s_idx, 3)

            def prepare(a, n, turn_):
                e = dve.value_load(expert_of[0:1, bass.ds(a, 1)], min_val=0, max_val=NX - 1)
                k, m = n % RING, n % DEPTH
                wait(dve, s_l1, a - (DEPTH - 1))
                ch.link(dve.tensor_copy(w1_now[m], w1s[:, bass.ds(e, 1), :].rearrange("p e f -> p (e f)")))
                wait(dve, s_hc, a - (DEPTH - 1))
                wait(dve, s_hd, a - (DEPTH - 1))
                ch.link(dve.tensor_copy(b1_now[m][:, :], b1col[:, bass.ds(e, 1), :].rearrange("p e c -> p (e c)")))
                dve.wait_ge(s_g[k], turn_)
                wait(dve, s_o[k], turn_ - 16)
                ch.link(dve.tensor_tensor(y[k], xg[k][:, 0:E], b2bc[:, bass.ds(e * E, E)], ALU.add))
                dve.tensor_scalar(gn[m], xg[k][:, 0:E], xg[k][:, E:E + 1], xg[k][:, E + 1:E + 2],
                                  ALU.subtract, ALU.mult).then_inc(s_prep, 1)
                ch.join()

            def hidden_out(a, n):
                dve.wait_ge(s_l1, a + 1)
                wait(dve, s_l2, a - (DEPTH - 1))
                c = NC - 1
                dve.tensor_scalar(hT[n % DEPTH][:, P * c:P * c + P], bank(6 + n % 2, P),
                                  b1_now[n % DEPTH][:, c:c + 1], 0.0, ALU.add, ALU.max).then_inc(s_hd, 1)

            def result(a, n):
                dve.wait_ge(s_l2, a + 1)
                dve.tensor_tensor(y[n % RING], bank(4 + n % 2, E), y[n % RING], ALU.add).then_inc(s_y, 1)

            for a in range(3):
                prepare(a, a, 16)
            for a in range(RING):
                prepare(a + 3, a + 3, 16 * ((a + 3) // RING + 1))
                hidden_out(a, a)
                if a >= 2:
                    result(a - 2, a - 2)

            def body(r):
                for n in range(RING):
                    prepare(r * RING + (n + 3), n + 3, (r + ((n + 3) // RING + 1)) * 16)
                    hidden_out(r * RING + n, n)
                    result(r * RING + (n - 2), n - 2)
            ch.loop(1, NT // RING - 1, 3 * RING, body)
            for a in range(NT - RING, NT + 2):
                if a + 3 < NT:
                    prepare(a + 3, a + 3, 16 * ((a + 3) // RING + 1))
                if a < NT:
                    hidden_out(a, a)
                result(a - 2, a - 2)


_WEIGHTS = ["d2v", "img", "txt", "att0", "att1", "f1", "f2"]


def kernel(**inputs):
    import concourse.bacc as _bacc
    from concourse.bass_utils import run_bass_kernel_spmd as _run

    nc = _bacc.Bacc("TRN2", target_bir_lowering=False, num_devices=1)
    arrays = {}

    def given(name):
        a = np.ascontiguousarray(inputs[name])
        arrays[f"in_{name}"] = a
        return nc.dram_tensor(f"in_{name}", a.shape, mybir.dt.from_np(a.dtype), kind="ExternalInput").ap()

    args = [given("x"), given("ctx_768"), [given(f"L0_xattn_W_{w}") for w in _WEIGHTS],
            [given(f"L0_xattn_b_{w}") for w in _WEIGHTS], given("L0_ffn_router_w"), given("L0_ffn_W1"),
            given("L0_ffn_b1"), given("L0_ffn_W2"), given("L0_ffn_b2")]
    out = nc.dram_tensor("out_0", (B, S, E), F32, kind="ExternalOutput").ap()
    xattn_moe(nc, *args, out)
    r = _run(nc, [arrays], core_ids=[0])
    return r.results[0]["out_0"]
```

```python
from contextlib import ExitStack

import numpy as np

import concourse.bass as bass
from concourse import mybir

F32 = mybir.dt.float32
BF16 = mybir.dt.bfloat16
I32 = mybir.dt.int32
I16 = mybir.dt.int16
ALU = mybir.AluOpType
ACT = mybir.ActivationFunctionType
AX = mybir.AxisListType.X

P = 128
B = 64
S = 128
E = 128
CT = 77
DC = 96
KV = 64
FF = 512
NC = FF // P
NX = 8
T = B * S
GB = 4
G = B // GB
GT = GB * S
GC = GB * CT
CP = 112
CJ = B * CT // CP
CAP = int(np.ceil(T / NX * 1.25))
NT = T // P + NX
USED = NT - 1
RING = 12
DEPTH = 4
COPY = 6
LAG = 10
NQ = CJ // 4
QC = 4 * CP
NP = 4
PC = B * CT // NP
XP = 8
OWN = (0, 3, 6)
VG = 10
GR = 4
XW = E + 2
MAGIC = 12582912.0
EPS = 1e-5
LEVELS = 7
HALF = 4 ** LEVELS
HT = 16
FAR = 32768
WIDTHS = (DC, E, E, E, E, NC * 2 * E, FF)
COUNTS = (E * DC, E * E, E * E, KV * E, KV * E, FF * 2 * E, E * FF)
D2V, IMG, TXT, ATT0, ATT1, F1, F2 = range(7)
NSMALL = 7 + NC + 3
Q_CTX, Q_VIS, Q_IMG, Q_X, Q_CAT, Q_H = range(6)


def wait(eng, sem, value):
    if not isinstance(value, int) or value > 0:
        eng.wait_ge(sem, value)


def wait_alone(eng, sem, value, passed):
    if not isinstance(value, int) or value > 0:
        eng.wait_ge(sem, value)
        eng.sem_inc(passed, 1)


def for_loop(eng, start, end, body):
    with eng.Fori(start, end) as i:
        body(i)


class Chain:

    def __init__(self, eng, sem):
        self.eng, self.sem, self.base, self.count = eng, sem, 0, 0

    def link(self, ins):
        ins.then_inc(self.sem, 1)
        self.count += 1

    def join(self):
        self.eng.wait_ge(self.sem, self.base + self.count)

    def loop(self, start, end, per, body):
        first = self.base + self.count
        with self.eng.Fori(start, end) as i:
            self.base, self.count = (i - start) * per + first, 0
            body(i)
            assert self.count == per, self.count
        self.base, self.count = first + (end - start) * per, 0


def xattn_moe(nc, x, ctx_in, weights, biases, router_w, W1, b1, W2, b2, out):
    rows = nc.dram_tensor("token_rows", (T, XW), F32).ap()
    with ExitStack() as stack:
        def sb(name, shape, dtype=F32):
            return stack.enter_context(nc.sbuf_tensor(name, shape, dtype))

        def sem(name):
            return stack.enter_context(nc.semaphore(name))

        psum = stack.enter_context(nc.psum_tensor("psum", [P, 8, 512], F32))

        ident = sb("ident", [P, P])
        ident_b = sb("ident_b", [P, P], BF16)
        ones = sb("ones", [P, P])
        ones_b = sb("ones_b", [P, P], BF16)
        not_before_b = sb("not_before_b", [P, P], BF16)
        same_expert = sb("same_expert", [P, P])
        magic = sb("magic", [P, 1])
        warm = sb("warm", [1, 1])
        inv_counts = sb("inv_counts", [P, 7])
        steps = sb("steps", [P, LEVELS + 1, 6])
        tile_no = sb("tile_no", [P, NT])
        tile_no_b = sb("tile_no_b", [P, NT], BF16)
        row_no_b = sb("row_no_b", [P, P], BF16)
        part_no = sb("part_no", [P, 1])
        turn_no = sb("turn_no", [P, B])
        rank8 = sb("rank8", [P, NX])
        seg = sb("seg", [P, NX * B])
        wsum = sb("wsum", [P, 7])
        ws = sb("ws", [P, 7])
        wlim = sb("wlim", [P, 2, 7])
        wT = sb("wT", [P, 3 * P], BF16)
        attT = sb("attT", [P, 2, 2, KV], BF16)
        f1T = sb("f1T", [P, 2, FF], BF16)
        f2T = sb("f2T", [P, NC, E], BF16)
        small_w = sb("small_w", [NX + NX * NC, E])
        small_wT = sb("small_wT", [P, NX + NX * NC])
        rwT = small_wT[:, 0:NX]
        b1col = small_wT[:, NX:].rearrange("p (e c) -> p e c", e=NX)
        bcol = sb("bcol", [P, 5 + NC])
        bf2 = sb("bf2", [P, E])
        amax = sb("amax", [P, 6])
        gmax = sb("gmax", [1, 6])
        iscale = sb("iscale", [P, 6])
        inv = sb("inv", [P, 6])
        scale = sb("scale", [P, 7])
        h_scale = sb("h_scale", [P, 1])
        h_bias = sb("h_bias", [P, NC])
        xall = sb("xall", [P, B, XW])
        big = sb("big", [P, T])
        tok_b = sb("tok_b", [P, T], BF16)
        xqT = sb("xqT", [P, T], BF16)
        feat = sb("feat", [P, B * CT])
        qa = sb("qa", [P, B * CT], BF16)
        qb = sb("qb", [P, B * CT], BF16)
        keys = sb("keys", [P, 2 * B * CT])
        stats = sb("stats", [P, B, 6])
        tmp = sb("tmp", [P, 4, B])
        part = sb("part", [P, 4, B])
        avg = sb("avg", [P, B])
        avg_q = sb("avg_q", [P, B], BF16)

        wraw = big[:, 0:sum(WIDTHS)]
        wq = big[:, sum(WIDTHS):sum(WIDTHS) * 3 // 2].bitcast(BF16)
        wneg = big[:, sum(WIDTHS) * 3 // 2:sum(WIDTHS) * 2].bitcast(BF16)
        ctx_raw = keys[:, 0:CJ * DC]
        scaled = keys[:, 0:B * CT]
        ctx_q = tok_b[0:CP, 0:CJ * DC]
        xn = big[:, :].rearrange("p (t d) -> p t d", d=E)

        at = [0]

        def take(n):
            at[0] += n
            return keys[:, at[0] - n:at[0]]
        fused0 = [take(GT) for _ in range(GR)]
        fused1 = [take(GT) for _ in range(GR)]
        kT = [[take(GC) for _ in range(GR)] for _ in range(2)]
        ktok = [[take(GB * P)[0:CT, :] for _ in range(n)] for n in (2, GR)]
        qb_f = qb[:, :].bitcast(F32)
        prob = [[qb_f[:, (2 * l + n) * GC:(2 * l + n + 1) * GC].rearrange("p (b c) -> p b c", b=GB)
                 for n in range(2)] for l in range(2)]
        probT = [sb(f"probT{l}", [CT, GT]) for l in range(2)]
        amx = sb("amx", [P, 2, GB])
        asum = sb("asum", [P, 2, GB])
        arec = sb("arec", [P, 2, GB])
        u = [feat[:, n * NC * GT:(n + 1) * NC * GT].rearrange("p (c n) -> p c n", c=NC) for n in range(2)]
        hq = [qb[:, n * NC * GT:(n + 1) * NC * GT].rearrange("p (c n) -> p c n", c=NC) for n in range(2)]
        xs = sb("xs", [P, GB, E])
        xsT = sb("xsT", [P, GT])[:, :]
        hint = [v[:, 0:G * GT].bitcast(I16).rearrange("p (g c n) -> p g c n", g=G, c=2) for v in (keys, big)]
        hrun = [feat[:, n * GT:(n + 1) * GT].bitcast(I16).rearrange("p (c n) -> p c n", c=2) for n in range(2)]
        st2 = stats[:, 0:GB, :]

        def route(n):
            return big[:, n * 512:(n + 1) * 512]

        w1s = keys[:, 0:NX * FF].rearrange("p (e f) -> p e f", e=NX)
        w2s = keys[:, NX * FF:2 * NX * FF].rearrange("p (e c d) -> p e c d", e=NX, c=NC)
        b2bc = keys[:, 2 * NX * FF:2 * NX * FF + NX * E]
        xqT_f = xqT[:, :].bitcast(F32)
        cut = [0]

        def take_f(n):
            cut[0] += n
            return xqT_f[:, cut[0] - n:cut[0]]
        xg = [xall[:, n, :] for n in range(RING)]
        y = [xall[:, RING + n, 0:E] for n in range(RING)]
        gn = [take_f(E) for _ in range(DEPTH)]
        gT = [take_f(E) for _ in range(DEPTH)]
        hT = [take_f(FF) for _ in range(DEPTH)]
        w1_now = [feat[:, n * FF:(n + 1) * FF] for n in range(DEPTH)]
        b1_now = [sb(f"b1_now{n}", [P, NC]) for n in range(DEPTH)]
        idx_in = sb("idx_in", [P, RING], I32)
        idx_out = sb("idx_out", [P, RING], I32)
        src_of = sb("src_of", [P, NT], I32)
        dst_of = sb("dst_of", [P, NT], I32)
        expert_of = sb("expert_of", [1, NT], I32)
        cnt = sb("cnt", [P, 3])
        reached = sb("reached", [P, 3])
        met = sb("met", [P, 1])
        base = sb("base", [P, 3])
        thr = sb("thr", [P, 1])
        half = sb("half", [P, 2])
        cand = sb("cand", [P, 3])
        thr8 = sb("thr8", [P, NX])
        n8 = [sb(f"n8_{n}", [P, NX]) for n in range(4)]
        n8i = [sb(f"n8i_{n}", [P, NX], I32) for n in range(2)]
        t64 = [sb(f"t64_{n}", [P, B]) for n in range(6)]
        t64i = [sb(f"t64i_{n}", [P, B], I32) for n in range(3)]
        hot_row = xqT[:, :].rearrange("p (t r) -> p t r", t=B)
        hot_tile = feat[:, :].bitcast(BF16)[:, 0:B * 2 * NT].rearrange("p (t a c) -> p t a c", t=B, a=2)
        hot = qb[:, 0:B * NT].rearrange("p (t c) -> p t c", t=B)

        s_ctx = [sem(f"ctx_loaded{n}") for n in range(NP)]
        s_w = sem("weights_loaded")
        s_x = [sem(f"x_loaded{n}") for n in range(XP)]
        s_small = sem("biases_loaded")
        s_moe = sem("expert_weights_loaded")
        s_const = sem("constants_made")
        s_cc = sem("constants_begun")
        s_amax = sem("amax_ready")
        s_grow = sem("amax_row_ready")
        s_gm = sem("global_max_ready")
        s_gcol = sem("global_max_spread")
        s_inv = sem("inv_ready")
        s_wsum = sem("wsum_ready")
        s_wtot = sem("wsum_spread")
        s_wq = sem("weights_quantised")
        s_wtr = sem("weights_transposed")
        s_wT = sem("weights_in_place")
        s_sc = sem("scales_ready")
        s_fs = sem("ctx_or_features_scaled")
        s_cq = sem("ctx_quantised")
        s_tr = sem("transposed")
        s_trc = sem("transposed_copied")
        s_trd = sem("transposed_copied_vector")
        s_mm = sem("linear_done")
        s_mmc = sem("linear_copied")
        s_vq = sem("vis_quantised")
        s_iq = sem("image_quantised")
        s_bn0 = sem("half_statistics")
        s_mean = sem("mean_ready")
        s_var = sem("variance_ready")
        s_std = sem("deviation_ready")
        s_lm = sem("x_less_mean_vector")
        s_rs0 = sem("inverse_deviation")
        s_xd = sem("x_less_mean")
        s_xn = sem("xn_from_gpsimd")
        s_avg = sem("image_sums")
        s_xs = sem("x_scaled")
        s_xq = sem("x_quantised")
        s_fmm = sem("fused_product")
        s_f = sem("fused_ready")
        s_kmm = [sem(f"keys_product{n}") for n in range(2)]
        s_k = [sem(f"keys_ready{n}") for n in range(2)]
        s_kt = sem("attention_keys_turned")
        s_ktc = sem("key_tokens_ready")
        s_smm = [sem(f"scores{n}") for n in range(2)]
        s_mx = [sem(f"scores_max{n}") for n in range(2)]
        s_sub = [sem(f"scores_less_max{n}") for n in range(2)]
        s_e = [sem(f"exp{n}") for n in range(2)]
        s_sum = [sem(f"exp_sum{n}") for n in range(2)]
        s_r = [sem(f"sum_inverted{n}") for n in range(2)]
        s_p = [sem(f"probs{n}") for n in range(2)]
        s_t = [sem(f"probs_transposed{n}") for n in range(2)]
        s_pt = [sem(f"probsT_copied{n}") for n in range(2)]
        s_av = [sem(f"attended{n}") for n in range(2)]
        s_up = [sem(f"fused_updated{n}") for n in range(2)]
        s_fm = sem("fused_max")
        s_res = sem("residual_ready")
        s_cs = sem("cat_scaled")
        s_catq = sem("cat_quantised")
        s_h = sem("hidden_product")
        s_hcp = sem("hidden_copied")
        s_hrm = sem("hidden_running_max_taken")
        s_relu = sem("relu_done")
        s_hq = sem("hidden_quantised")
        s_f2 = sem("out_product")
        s_xm2 = sem("x1_less_mean")
        s_x1 = sem("x1_ready")
        s_bn = sem("half_statistics2")
        s_rs = sem("inverse_deviation2")
        s_var2 = sem("variance2_ready")
        s_std2 = sem("deviation2_ready")
        s_xn2 = sem("xn2_ready")
        s_x2t = sem("xn2_transposed")
        s_x2c = sem("xn2T_copied")
        s_lg = sem("logits_ready")
        s_rows = sem("rows_stored")
        s_d = sem("logits_less_max")
        s_ex = sem("logits_exp")
        s_v = sem("keys_by_expert")
        s_vt = sem("keys_transposed")
        s_cnt = sem("counts_ready")
        s_cnt2 = sem("counts_summed")
        s_thr = sem("threshold_ready")
        s_thr_r = sem("threshold_row")
        s_thr_c = sem("threshold_row_copied")
        s_thr_s = sem("threshold_spread")
        s_ms = sem("masks_ready")
        s_ps = sem("prefixes_ready")
        s_ht = sem("one_hot_tiles_ready")
        s_hr = sem("one_hot_rows_ready")
        s_hp = sem("tiles_times_row")
        s_hu = sem("tiles_times_turn")
        s_inv_mm = sem("one_hots_used")
        s_idx = sem("indices_ready")
        s_ixi = sem("gather_index_copied")
        s_ixo = sem("scatter_index_copied")
        s_g = [sem(f"gathered{n}") for n in range(RING)]
        s_y = sem("result_ready")
        s_o = [sem(f"scattered{n}") for n in range(RING)]
        s_prep = sem("tile_prepared")
        s_gt = sem("gathered_transposed")
        s_gc = sem("gatheredT_copied")
        s_l1 = sem("layer1_product")
        s_hc = sem("hidden_relu_scalar")
        s_hd = sem("hidden_relu_vector")
        s_l2 = sem("layer2_product")
        s_passed = sem("gpsimd_waits_passed")
        s_passed2 = sem("vector_waits_passed")
        s_passed3 = sem("tensor_waits_passed")
        s_dve = sem("vector_chain")

        WOFF = [sum(WIDTHS[:k]) for k in range(7)]

        def wslice(t, k):
            return t[0:KV if k in (ATT0, ATT1) else P, WOFF[k]:WOFF[k] + WIDTHS[k]]

        def bank(n, width=512, rows_=P):
            return psum[0:rows_, n, 0:width]

        def bank_b(n):
            return psum[:, n, :].bitcast(BF16)

        def c4(i):
            return bass.ds(i * GC, GC)

        def g4(i):
            return bass.ds(i * GT, GT)

        def attention_steps(loop, step):
            for t in range(GR - 1):
                step(t, t, t)
            loop(1, G // GR, lambda r: [step(r * GR + (n - 1), (n - 1) % GR, G - 2) for n in range(GR)])
            for t in range(G - 1, G + 3):
                step(t, t % GR, t)

        def hidden_steps(loop, step):
            for t in range(-1, 5):
                step(t, t % 2, t)
            loop(0, (G - 6) // 2, lambda r: [step(r * 2 + (5 + n), (5 + n) % 2, G - 2) for n in range(2)])
            for t in range(G - 1, G + 4):
                step(t, t % 2, t)

        block = stack.enter_context(nc.Block())

        @block.sync
        def _(sp):
            ctx_rows = ctx_in.rearrange("b c d -> (b c) d").rearrange("(p j) d -> p (j d)", p=CP)
            w = CJ * DC // NP
            for n in range(NP):
                sp.dma_start(ctx_raw[0:CP, w * n:w * n + w], ctx_rows[:, w * n:w * n + w]).then_inc(s_ctx[n], 16)
            for k in (D2V, IMG, TXT):
                sp.dma_start(bcol[:, k:k + 1], biases[k].rearrange("(p o) -> p o", o=1)).then_inc(s_small, 16)
            for l in range(2):
                for twice in range(2):
                    sp.dma_start(bcol[KV * twice:KV * twice + KV, ATT0 + l:ATT0 + l + 1],
                                 biases[ATT0 + l].rearrange("(p o) -> p o", o=1)).then_inc(s_small, 16)
            for c in range(NC):
                sp.dma_start(bcol[:, 5 + c:6 + c], biases[F1][P * c:P * c + P].rearrange("(p o) -> p o", o=1)
                             ).then_inc(s_small, 16)
            sp.dma_start(bf2[:, :], biases[F2].partition_broadcast(P)).then_inc(s_small, 16)
            sp.dma_start(small_w[0:NX, :], router_w).then_inc(s_small, 16)
            sp.dma_start(small_w[NX:, :], b1.rearrange("e (c p) -> (e c) p", p=P)).then_inc(s_small, 16)
            xt = x.rearrange("b s e -> s b e")
            w = B // XP
            for n in range(XP):
                sp.dma_start(xall[:, w * n:w * n + w, 0:E], xt[:, w * n:w * n + w, :]).then_inc(s_x[n], 16)
            rows_t = rows.rearrange("(t p) w -> p t w", p=P)
            with sp.Fori(0, G) as i:
                sp.wait_ge(s_xn2, i + 1)
                sp.dma_start(rows_t[:, bass.ds(i * GB, GB), :], xall[:, bass.ds(i * GB, GB), :]).then_inc(s_rows, 16)
            sp.wait_ge(s_relu, NC * G)
            sp.dma_start(w1s, W1.rearrange("e d f -> d e f")).then_inc(s_moe, 16)
            for e in range(NX):
                sp.dma_start(w2s[:, e, :, :], W2[e].rearrange("(c p) d -> p c d", p=P)).then_inc(s_moe, 16)
            sp.dma_start(b2bc, b2.rearrange("e d -> (e d)").partition_broadcast(P)).then_inc(s_moe, 16)
            sp.wait_ge(s_rows, 16 * G)

        @block.gpsimd
        def _(pool):
            pool.memset(ident[:, :], 0.0).then_inc(s_cc, 1)
            pool.memset(ident_b[:, :], 0.0).then_inc(s_cc, 1)
            pool.memset(not_before_b[:, :], 0.0).then_inc(s_cc, 1)
            pool.memset(same_expert[:, :], 0.0).then_inc(s_cc, 1)
            pool.memset(seg[:, :], 1.0).then_inc(s_cc, 1)
            pool.memset(ones[:, :], 1.0).then_inc(s_const, 1)
            pool.memset(ones_b[:, :], 1.0).then_inc(s_const, 1)
            pool.memset(magic[:, :], MAGIC).then_inc(s_const, 1)
            pool.memset(wsum[:, :], 0.0).then_inc(s_const, 1)
            pool.memset(amax[:, :], 0.0).then_inc(s_const, 1)
            for k in range(7):
                pool.memset(inv_counts[:, k:k + 1], 1.0 / COUNTS[k]).then_inc(s_const, 1)
            pool.wait_ge(s_cc, 5)
            for m in (ident, ident_b):
                pool.affine_select(out=m[:, :], in_=m[:, :], compare_op=ALU.not_equal, fill=1.0, base=0,
                                   pattern=[[-1, P]], channel_multiplier=1).then_inc(s_const, 1)
            pool.affine_select(out=not_before_b[:, :], in_=not_before_b[:, :], compare_op=ALU.is_gt, fill=-1.0, base=0,
                               pattern=[[1, P]], channel_multiplier=-1).then_inc(s_const, 1)
            for d in range(-(P // NX) + 1, P // NX):
                pool.affine_select(out=same_expert[:, :], in_=same_expert[:, :], compare_op=ALU.not_equal, fill=1.0,
                                   base=NX * d, pattern=[[-1, P]], channel_multiplier=1).then_inc(s_cc, 1)
                pool.wait_ge(s_cc, 5 + d + P // NX)
            segv = seg[:, :].rearrange("p (e t) -> p e t", e=NX)
            pool.memset(segv[:, :, 0:1], 0.0).then_inc(s_const, 1)
            pool.memset(steps[:, LEVELS, :], 0.0).then_inc(s_const, 1)
            for k in range(LEVELS):
                w = float(HALF // 4 ** (k + 1))
                pool.memset(steps[:, k, 0:4], w).then_inc(s_const, 1)
                for j in (2, 3):
                    pool.memset(steps[:, k, 2 + j:3 + j], j * w).then_inc(s_const, 1)
            for e in range(NX):
                pool.memset(rank8[:, e:e + 1], float(NX - e)).then_inc(s_const, 1)
            pool.iota(tile_no[:, :], pattern=[[1, NT]], base=0, channel_multiplier=0,
                      allow_small_or_imprecise_dtypes=True).then_inc(s_const, 1)
            pool.iota(tile_no_b[:, :], pattern=[[1, NT]], base=0, channel_multiplier=0,
                      allow_small_or_imprecise_dtypes=True).then_inc(s_const, 1)
            pool.iota(row_no_b[:, :], pattern=[[1, P]], base=0, channel_multiplier=0,
                      allow_small_or_imprecise_dtypes=True).then_inc(s_const, 1)
            pool.iota(part_no[:, :], pattern=[[0, 1]], base=0, channel_multiplier=1,
                      allow_small_or_imprecise_dtypes=True).then_inc(s_const, 1)
            pool.iota(turn_no[:, :], pattern=[[1, B]], base=1, channel_multiplier=0,
                      allow_small_or_imprecise_dtypes=True).then_inc(s_const, 1)

            pool.wait_ge(s_mean, 1)
            pool.wait_ge(s_rs0, 1)
            for n, i in enumerate(range(VG, G, 2)):
                xr, xo = xall[:, i * GB:(i + 2) * GB, :], xn[:, i * GB:(i + 2) * GB, :]
                pool.tensor_tensor(xo, xr[:, :, 0:E], xr[:, :, E:E + 1].to_broadcast([P, 2 * GB, E]), ALU.subtract
                                   ).then_inc(s_xd, 1)
                pool.wait_ge(s_xd, n + 1)
                pool.tensor_tensor(xo, xo, xr[:, :, E + 1:E + 2].to_broadcast([P, 2 * GB, E]), ALU.mult
                                   ).then_inc(s_xn, 1)
            pool.wait_ge(s_mmc, 2 * NQ + 2)
            v = feat[:, :].rearrange("p (b a c) -> p b a c", b=B, a=CT // 11)
            so_far = qb_f[:, 4 * GC:4 * GC + B * 11].rearrange("p (b c) -> p b c", b=B)
            parts = [v[:, :, a, :] for a in range(CT // 11)] + [so_far[:, :, c] for c in range(1, 11)]
            for n, new in enumerate(parts[1:]):
                wide = n + 2 <= CT // 11
                dst, old = (so_far, so_far if n else parts[0]) if wide else (
                    avg[:, :], avg[:, :] if n + 2 > CT // 11 + 1 else so_far[:, :, 0])
                pool.tensor_tensor(dst, old, new, ALU.add).then_inc(s_avg, 1)
                pool.wait_ge(s_avg, n + 1)

            def norm(l, i, n):
                pool.wait_ge(s_r[l], i + 1)
                pr = prob[l][n % 2]
                pool.tensor_tensor(pr, pr, arec[:, l, :].unsqueeze(2).to_broadcast([P, GB, CT]), ALU.mult
                                   ).then_inc(s_p[l], 1)

            def residual(i):
                xr = xall[:, bass.ds(i * GB, GB), 0:E]
                pool.tensor_tensor(xr, xr, bf2[:, :].unsqueeze(1).to_broadcast([P, GB, E]), ALU.add).then_inc(s_res, 1)

            def step(t, n, last):
                if last < G:
                    norm(0, t, n)
                if 2 <= last < G + 2:
                    norm(1, t - 2, n + 2)
                if last < G:
                    residual(t)
            pool.wait_ge(s_small, 16 * NSMALL)
            pool.wait_ge(s_amax, Q_X + 1)
            attention_steps(lambda a, b, body: for_loop(pool, a, b, body), step)

            def normalise(i):
                xr = xall[:, bass.ds(i * GB, GB), :]
                wait_alone(pool, s_rs, i + 1, s_passed)
                wait_alone(pool, s_x2t, i, s_passed)
                pool.tensor_tensor(xs[:, :, :], xr[:, :, 0:E], xr[:, :, E:E + 1].to_broadcast([P, GB, E]), ALU.subtract
                                   ).then_inc(s_xm2, 1)
                wait_alone(pool, s_xm2, i + 1, s_passed)
                pool.tensor_tensor(xs[:, :, :], xs[:, :, :], xr[:, :, E + 1:E + 2].to_broadcast([P, GB, E]), ALU.mult
                                   ).then_inc(s_xn2, 1)

            def step(t, n, last):
                if 3 <= last < G + 3:
                    normalise(t - 3)
            hidden_steps(lambda a, b, body: for_loop(pool, a, b, body), step)

            for i in range(B // HT):
                pool.wait_ge(s_ht, i + 1)
                t = slice(i * HT, (i + 1) * HT)
                pool.tensor_tensor(hot_tile[:, t, 1, :], hot[:, t, :],
                                   turn_no[:, t].unsqueeze(2).to_broadcast([P, HT, NT]), ALU.mult).then_inc(s_hu, 1)

            out_rows = out.rearrange("b s e -> (b s) e")
            pool.wait_ge(s_idx, 3)
            pool.wait_ge(s_rows, 16 * G)

            def take_indices(r, n, mine, all_, moved, copied):
                for k in range(COPY):
                    wait_alone(pool, moved[n + k], r * 16, s_passed)
                pool.tensor_copy(mine[:, n:n + COPY], all_[:, bass.ds(r * RING + n, COPY)]).then_inc(copied, 1)
                wait_alone(pool, copied, r * (RING // COPY) + (n // COPY + 1), s_passed)

            def gather(r, n):
                if n % COPY == 0:
                    take_indices(r, n, idx_in, src_of, s_g, s_ixi)
                wait_alone(pool, s_prep, (r - 1) * RING + (n + 1), s_passed)
                pool.indirect_dma_start(xg[n], None, rows, bass.IndirectOffsetOnAxis(ap=idx_in[:, n:n + 1], axis=0)
                                        ).then_inc(s_g[n], 16)

            def scatter(r, n):
                if n % COPY == 0:
                    take_indices(r, n, idx_out, dst_of, s_o, s_ixo)
                wait_alone(pool, s_y, r * RING + (n + 1), s_passed)
                pool.indirect_dma_start(out_rows, bass.IndirectOffsetOnAxis(ap=idx_out[:, n:n + 1], axis=0), y[n], None,
                                        bounds_check=T - 1, oob_is_err=False).then_inc(s_o[n], 16)

            def both(r, n):
                gather(r, n)
                scatter(r + (n - LAG) // RING, (n - LAG) % RING)

            for a in range(LAG):
                gather(a // RING, a % RING)
            for a in range(LAG, 2 * RING):
                both(a // RING, a % RING)
            with pool.Fori(2, NT // RING - 1) as r:
                for n in range(RING):
                    both(r, n)
            for a in range(NT - RING, USED):
                both(a // RING, a % RING)
            for a in range(USED - LAG, USED):
                scatter(a // RING, a % RING)
            for n in range(RING):
                pool.wait_ge(s_o[n], 16 * ((USED - 1 - n) // RING + 1))

        @block.scalar
        def _(act):
            def linear(src_bank, dst, k, b):
                return act.activation(dst, src_bank, ACT.Identity, bias=bcol[:, b:b + 1], scale=scale[:, k:k + 1])

            for k in range(5):
                act.dma_start(wslice(wraw, k), weights[k]).then_inc(s_w, 16)
            act.dma_start(wslice(wraw, F1).rearrange("p (c i) -> p c i", c=NC),
                          weights[F1].rearrange("(c p) i -> p c i", p=P)).then_inc(s_w, 16)
            act.dma_start(wslice(wraw, F2), weights[F2]).then_inc(s_w, 16)

            def scale_up(dst, src, k, done):
                act.activation(dst, src, ACT.Identity, bias=magic[0:dst.shape[0], :],
                               scale=inv[0:dst.shape[0], k:k + 1]).then_inc(done, 1)

            act.wait_ge(s_const, 14)
            act.wait_ge(s_inv, Q_CTX + 1)
            w = CJ * DC // NP
            for n in range(NP):
                v = ctx_raw[0:CP, w * n:w * n + w]
                scale_up(v, v, Q_CTX, s_fs)
            act.wait_ge(s_wtr, 1)
            act.copy(wT[0:DC, 0:P], bank_b(0)[0:DC, 0:P]).then_inc(s_wT, 1)
            act.copy(wT[:, P:3 * P], bank_b(0)[:, P:3 * P]).then_inc(s_wT, 1)
            act.copy(attT[:, :, :, :], bank_b(0)[:, 3 * P:4 * P].rearrange("p (l k) -> p l k", l=2)
                     .unsqueeze(2).to_broadcast([P, 2, 2, KV])).then_inc(s_wT, 1)
            act.wait_ge(s_wtr, 2)
            act.copy(f1T[:, :, :], bank_b(1).rearrange("p (h f) -> p h f", h=2)).then_inc(s_wT, 1)
            act.wait_ge(s_wtr, 3)
            act.copy(f2T[:, :, :], bank_b(2)[:, 0:FF].rearrange("p (c d) -> p c d", c=NC)).then_inc(s_wT, 1)
            act.wait_ge(s_wtr, 4)
            act.copy(small_wT[:, :], bank(7, NX + NX * NC)).then_inc(s_wT, 1)
            qa_v = qa[0:DC, :].rearrange("d (p j) -> d j p", j=CJ)
            for k in range(NQ):
                act.wait_ge(s_tr, k + 1)
                act.copy(qa_v[:, 4 * k:4 * k + 4, :], bank_b(3 + k % 2)[0:DC, 0:QC].rearrange("d (j p) -> d j p", j=4)
                         ).then_inc(s_trc, 1)

            def linears(first, k):
                for n in range(NQ):
                    act.wait_ge(s_mm, first + n + 1)
                    linear(bank(5 + (first + n) % 2, QC), feat[:, QC * n:QC * n + QC], k, k).then_inc(s_mmc, 1)

            act.wait_ge(s_small, 16 * NSMALL)
            act.wait_ge(s_sc, 1)
            linears(0, D2V)
            act.wait_ge(s_var, 1)
            act.activation(tmp[:, 3, :], tmp[:, 2, :], ACT.Sqrt).then_inc(s_std, 1)
            act.wait_ge(s_inv, Q_VIS + 1)
            for n in range(NP):
                scale_up(scaled[:, PC * n:PC * n + PC], feat[:, PC * n:PC * n + PC], Q_VIS, s_fs)
            act.wait_ge(s_sc, 2)
            linears(NQ, IMG)
            act.wait_ge(s_inv, Q_IMG + 1)
            for n in range(NP):
                scale_up(scaled[:, PC * n:PC * n + PC], feat[:, PC * n:PC * n + PC], Q_IMG, s_fs)

            def scale_tokens(k, done):
                act.wait_ge(s_inv, k + 1)
                w = T // XP
                for n in range(XP):
                    if n not in OWN:
                        scale_up(big[:, w * n:w * n + w], big[:, w * n:w * n + w], k, done)
            act.activation(warm[:, :], magic[0:1, :], ACT.Exp, scale=0.0)
            scale_tokens(Q_X, s_xs)
            w = T // XP
            for n in range(XP // 2):
                act.wait_ge(s_tr, NQ + n + 1)
                act.copy(xqT[:, w * n:w * n + w], bank_b(n)).then_inc(s_trc, 1)

            act.sem_inc(s_pt[0], 1)
            act.sem_inc(s_pt[1], 1)

            def operands(i, n):
                act.wait_ge(s_fmm, i + 1)
                wait(act, s_up[0], i - (GR - 2))
                linear(bank(0), fused0[n % GR], TXT, TXT).then_inc(s_f, 1)
                for l in range(2):
                    act.wait_ge(s_kmm[l], i + 1)
                    wait(act, s_smm[l], i - (GR - 1))
                    linear(bank(1 + l, GC), kT[l][n % GR], ATT0 + l, ATT0 + l).then_inc(s_k[l], 1)

            def key_tokens(i, n):
                act.wait_ge(s_kt, i + 1)
                for l in range(2):
                    wait(act, s_av[l], i - (GR - 2) if l else i)
                    v = bank(7, GB * P, CT).rearrange("p (b l k) -> p b l k", b=GB, l=2)[:, :, l:l + 1, :]
                    m = act.copy(ktok[l][n % (GR if l else 2)].rearrange("p (b a k) -> p b a k", b=GB, a=2),
                                 v.to_broadcast([CT, GB, 2, KV]))
                m.then_inc(s_ktc, 1)

            def exp(l, i, n):
                act.wait_ge(s_sub[l], i + 2)
                pr = prob[l][n % 2]
                act.activation(pr, pr, ACT.Exp, scale=float(E) ** -0.5).then_inc(s_e[l], 1)

            def probs_out(l, i):
                act.wait_ge(s_t[l], i + 2)
                act.wait_ge(s_av[l], i + 1)
                act.copy(probT[l][:, :], bank(3 + l, 512, CT)).then_inc(s_pt[l], 1)

            def step(t, n, last):
                if 1 <= last < G + 1:
                    probs_out(0, t - 1)
                if last < G:
                    exp(0, t, n)
                if 3 <= last:
                    probs_out(1, t - 3)
                if 2 <= last < G + 2:
                    exp(1, t - 2, n + 2)
                if last < G - 1:
                    operands(t + 1, n + 1)
                if last < G:
                    key_tokens(t, n)

            act.wait_ge(s_sc, 4)
            operands(0, 0)
            attention_steps(lambda a, b, body: for_loop(act, a, b, body), step)

            scale_tokens(Q_CAT, s_cs)

            with act.Fori(0, G // 2) as r:
                for n in range(2):
                    for pair in range(2):
                        act.wait_ge(s_h, (r * 2 + n) * 2 + (pair + 1))
                        act.copy(hint[pair][:, bass.ds(r * 2 + n, 1), :, :].rearrange("p g c n -> p (g c) n"),
                                 psum[:, 4 * n + 2 * pair:4 * n + 2 * pair + 2, :]).then_inc(s_hcp, 1)

            act.wait_ge(s_sc, 6)

            def relu(i, n, c):
                products = hint[c // 2][:, bass.ds(i, 1), c % 2, :].rearrange("p g n -> p (g n)")
                act.activation(u[n][:, c, :], products, ACT.Relu, bias=h_bias[:, c:c + 1], scale=h_scale[:, :]
                               ).then_inc(s_relu, 1)

            def sqrt2(i):
                act.wait_ge(s_var2, i + 1)
                act.activation(tmp[:, 3, 0:GB], tmp[:, 2, 0:GB], ACT.Sqrt).then_inc(s_std2, 1)

            def x2T_out(i):
                act.wait_ge(s_x2t, i + 1)
                wait(act, s_lg, i)
                act.copy(xsT, bank(5)).then_inc(s_x2c, 1)

            def step(t, n, last):
                if 3 <= last < G + 3:
                    sqrt2(t - 3)
                if last < G - 1:
                    wait(act, s_hq, t)
                    for c in range(NC // 2):
                        relu(t + 1, 1 - n, c)
                if 4 <= last:
                    x2T_out(t - 4)
                if last < G - 1:
                    for c in range(NC // 2, NC):
                        relu(t + 1, 1 - n, c)
            hidden_steps(lambda a, b, body: for_loop(act, a, b, body), step)

            act.wait_ge(s_d, 1)
            act.activation(route(0), route(0), ACT.Exp).then_inc(s_ex, 1)

            for i in range(B // HT):
                act.wait_ge(s_ht, i + 1)
                act.activation(hot_tile[:, i * HT:(i + 1) * HT, 0, :], hot[:, i * HT:(i + 1) * HT, :], ACT.Copy,
                               scale=part_no[:, :]).then_inc(s_hp, 1)

            def gathered_out(a, n):
                act.wait_ge(s_gt, a + 1)
                wait(act, s_l1, a - (DEPTH - 1))
                act.copy(gT[n % DEPTH], bank(n % 2, P)).then_inc(s_gc, 1)

            def hidden_out(a, n):
                act.wait_ge(s_l1, a + 1)
                wait(act, s_l2, a - (DEPTH - 1))
                for c in range(NC - 1):
                    m = act.activation(hT[n % DEPTH][:, P * c:P * c + P], bank(2 + n % 2)[:, P * c:P * c + P],
                                       ACT.Relu, bias=b1_now[n % DEPTH][:, c:c + 1])
                m.then_inc(s_hc, 1)

            gathered_out(0, 0)
            gathered_out(1, 1)
            for a in range(RING):
                gathered_out(a + 2, a + 2)
                hidden_out(a, a)
            with act.Fori(1, NT // RING - 1) as r:
                for n in range(RING):
                    gathered_out(r * RING + (n + 2), n + 2)
                    hidden_out(r * RING + n, n)
            for a in range(NT - RING, USED):
                if a + 2 < USED:
                    gathered_out(a + 2, a + 2)
                hidden_out(a, a)

        @block.tensor
        def _(pe):
            pe.sem_inc(s_trc, 2)
            pe.sem_inc(s_mmc, 2)

            def spread_max(k):
                pe.wait_ge(s_amax, k + 1)
                pe.transpose(psum[0:1, 7, 0:P], amax[:, k:k + 1], ident[:, :]).then_inc(s_grow, 1)
                pe.wait_ge(s_gm, k + 1)
                pe.matmul(psum[:, 7, P + k:P + k + 1], ones[0:1, :], gmax[0:1, k:k + 1],
                          start=True, stop=True).then_inc(s_gcol, 1)

            pe.wait_ge(s_const, 14)
            spread_max(Q_CTX)
            pe.wait_ge(s_wsum, 7)
            pe.matmul(bank(6, 7), ones[:, :], wsum[:, :], start=True, stop=True).then_inc(s_wtot, 1)
            pe.wait_ge(s_wq, 7)
            for k in (D2V, IMG, TXT):
                pe.transpose(bank_b(0)[0:WIDTHS[k], P * k:P * k + P], wslice(wq, k), ident_b[:, :])
            pe.transpose(bank_b(0)[:, 3 * P:3 * P + KV], wslice(wq, ATT0), ident_b[0:KV, 0:KV])
            pe.transpose(bank_b(0)[:, 3 * P + KV:4 * P], wslice(wq, ATT1), ident_b[0:KV, 0:KV]).then_inc(s_wtr, 1)
            f1q = wslice(wq, F1).rearrange("p (c h i) -> p c h i", c=NC, h=2)
            for c in range(NC):
                for h in range(2):
                    m = pe.transpose(bank_b(1)[:, h * FF + c * P:h * FF + c * P + P], f1q[:, c, h, :], ident_b[:, :])
            m.then_inc(s_wtr, 1)
            f2q = wslice(wq, F2).rearrange("p (c i) -> p c i", c=NC)
            for c in range(NC):
                m = pe.transpose(bank_b(2)[:, c * P:c * P + P], f2q[:, c, :], ident_b[:, :])
            m.then_inc(s_wtr, 1)
            pe.wait_ge(s_small, 16 * NSMALL)
            pe.wait_ge(s_inv, Q_CTX + 1)
            pe.transpose(bank(7, NX + NX * NC), small_w[:, :], ident[0:NX + NX * NC, 0:NX + NX * NC]).then_inc(s_wtr, 1)

            cq = ctx_q.rearrange("p (j d) -> p j d", j=CJ)
            for k in range(NQ):
                pe.wait_ge(s_trc, k + 1)
                pe.wait_ge(s_cq, (4 * k + 3) * NP // CJ + 1)
                for j in range(4):
                    m = pe.transpose(bank_b(3 + k % 2)[0:DC, CP * j:CP * j + CP], cq[:, 4 * k + j, :],
                                     ident_b[0:CP, 0:CP])
                m.then_inc(s_tr, 1)

            def linears(first, w, src, pieces=None):
                for n in range(NQ):
                    pe.wait_ge(s_mmc, first + n + 1)
                    if pieces is not None:
                        pe.wait_ge(pieces, (QC * n + QC - 1) // PC + 1)
                    pe.matmul(bank(5 + (first + n) % 2, QC), w, src[:, QC * n:QC * n + QC],
                              start=True, stop=True).then_inc(s_mm, 1)

            pe.wait_ge(s_wT, 6)
            pe.wait_ge(s_trc, NQ + 2)
            linears(0, wT[0:DC, 0:P], qa[0:DC, :])
            spread_max(Q_VIS)
            linears(NQ, wT[:, P:2 * P], qb, s_vq)
            spread_max(Q_IMG)
            spread_max(Q_X)
            pe.wait_ge(s_trc, NQ + 2)
            pe.wait_ge(s_mmc, 2 * NQ + 2)
            w = T // XP
            for n in range(XP):
                pe.wait_ge(s_xq, n + 1)
                for j in range(B // XP):
                    m = pe.transpose(bank_b(n)[:, P * j:P * j + P], tok_b[:, w * n + P * j:w * n + P * j + P],
                                     ident_b[:, :])
                m.then_inc(s_tr, 1)

            for l in range(2):
                pe.sem_inc(s_av[l], 1)
                pe.sem_inc(s_t[l], 1)

            def project(i):
                wait(pe, s_f, i)
                pe.matmul(bank(0), wT[:, 2 * P:3 * P], xqT[:, g4(i)], start=True, stop=True).then_inc(s_fmm, 1)

            def keys_product(l, i):
                wait(pe, s_sub[l], i + 1 if l == 0 else i - 1)
                wait(pe, s_k[l], i)
                pe.matmul(bank(1 + l, GC), attT[:, l, :, :].rearrange("p a k -> p (a k)"), qa[:, c4(i)],
                          start=True, stop=True).then_inc(s_kmm[l], 1)

            def turn_keys(i, n):
                pe.wait_ge(s_k[0], i + 1)
                pe.wait_ge(s_k[1], i + 1)
                wait(pe, s_ktc, i)
                pe.sem_inc(s_passed3, 1)
                for b in range(GB):
                    for l in range(2):
                        m = pe.transpose(bank(7, GB * P, CT)[:, P * b + KV * l:P * b + KV * l + KV],
                                         kT[l][n % GR][0:KV, CT * b:CT * b + CT], ident[0:KV, 0:KV])
                m.then_inc(s_kt, 1)

            def scores(l, i, n, keys_read):
                pe.wait_ge(s_f if l == 0 else s_up[0], i + 1 + l)
                pe.wait_ge(s_k[l], keys_read)
                src = fused1 if l else fused0
                for b in range(GB):
                    m = pe.matmul(bank(1 + l)[:, CT * b:CT * b + CT], src[n % GR][:, P * b:P * b + P],
                                  kT[l][n % GR][:, CT * b:CT * b + CT], start=True, stop=True)
                m.then_inc(s_smm[l], 1)

            def turn(l, i, n):
                pe.wait_ge(s_p[l], i + 1)
                pe.wait_ge(s_pt[l], i + 1)
                for b in range(GB):
                    m = pe.transpose(bank(3 + l, 512, CT)[:, P * b:P * b + P], prob[l][n % 2][:, b, :], ident[:, :])
                m.then_inc(s_t[l], 1)

            def attend(l, i, n):
                pe.wait_ge(s_pt[l], i + 2)
                pe.wait_ge(s_ktc, i + 1)
                pe.wait_ge(s_up[l], i + 1)
                for b in range(GB):
                    m = pe.matmul(bank(5 + l)[:, P * b:P * b + P],
                                  ktok[l][n % (GR if l else 2)][:, P * b:P * b + P],
                                  probT[l][:, P * b:P * b + P], start=True, stop=True)
                m.then_inc(s_av[l], 1)

            def step(t, n, last):
                if last < G:
                    scores(0, t, n, t + 1)
                if 2 <= last < G + 2:
                    scores(1, t - 2, n + 2, t + 1 if last < G else G)
                if 1 <= last < G + 1:
                    turn(0, t - 1, n + 1)
                if 3 <= last:
                    turn(1, t - 3, n + 1)
                if last < G - 1:
                    project(t + 1)
                    keys_product(0, t + 1)
                if 1 <= last < G + 1:
                    attend(0, t - 1, n - 1)
                if last < G - 1:
                    keys_product(1, t + 1)
                if 3 <= last:
                    attend(1, t - 3, n - 3)
                if last < G:
                    turn_keys(t, n)

            pe.wait_ge(s_trd, XP // 2)
            pe.wait_ge(s_trc, NQ + 2 + XP // 2)
            pe.wait_ge(s_iq, NP)
            keys_product(0, 0)
            keys_product(1, 0)
            project(0)
            attention_steps(lambda a, b, body: for_loop(pe, a, b, body), step)

            spread_max(Q_CAT)

            def hidden(i, c, b):
                pe.matmul(bank(b), f1T[:, 0, P * c:P * c + P], tok_b[:, g4(i)], start=True, stop=False)
                return pe.matmul(bank(b).rearrange("p (b s) -> p b s", b=GB), f1T[:, 1, P * c:P * c + P],
                                 avg_q[:, bass.ds(i * GB, GB)].unsqueeze(2).to_broadcast([P, GB, S]),
                                 start=False, stop=True)

            pe.sem_inc(s_hcp, 4)

            def hidden_chunks(i, n, r):
                if n == 0:
                    pe.wait_ge(s_catq, r + 2)
                for pair in range(2):
                    pe.wait_ge(s_hcp, i * 2 + (pair + 1))
                    hidden(i, 2 * pair, 4 * n + 2 * pair)
                    hidden(i, 2 * pair + 1, 4 * n + 2 * pair + 1).then_inc(s_h, 1)

            with pe.Fori(0, G // 2) as r:
                for n in range(2):
                    hidden_chunks(r * 2 + n, n, r)
            spread_max(Q_H)

            def out_product(i, n):
                pe.wait_ge(s_hq, i + 1)
                wait(pe, s_x1, i)
                for b in range(GB):
                    for c in range(NC):
                        m = pe.matmul(bank(4)[:, P * b:P * b + P], hq[n][:, c, P * b:P * b + P], f2T[:, c, :],
                                      start=(c == 0), stop=(c == NC - 1))
                m.then_inc(s_f2, 1)

            def turn_x2(i):
                pe.wait_ge(s_xn2, i + 1)
                wait(pe, s_x2c, i)
                for b in range(GB):
                    m = pe.transpose(bank(5)[:, P * b:P * b + P], xs[:, b, :], ident[:, :])
                m.then_inc(s_x2t, 1)

            def logits(i):
                pe.wait_ge(s_x2c, i + 1)
                for b in range(GB):
                    m = pe.matmul(psum[:, 6, bass.ds(i * GB * NX + b * NX, NX)], xsT[:, P * b:P * b + P], rwT,
                                  start=True, stop=True)
                m.then_inc(s_lg, 1)

            def step(t, n, last):
                if 4 <= last:
                    turn_x2(t - 4)
                if 0 <= last < G:
                    out_product(t, n)
                if 4 <= last:
                    logits(t - 4)
            hidden_steps(lambda a, b, body: for_loop(pe, a, b, body), step)

            pe.wait_ge(s_v, 1)
            for n in range(4):
                m = pe.transpose(bank(0)[:, P * n:P * n + P], route(2)[:, P * n:P * n + P], ident[:, :])
            m.then_inc(s_vt, 1)
            with pe.Fori(0, 2 * LEVELS) as k:
                pe.wait_ge(s_cnt, k + 1)
                pe.matmul(bank(1, 3), same_expert[:, :], cnt[:, :], start=True, stop=True).then_inc(s_cnt2, 1)
            pe.wait_ge(s_thr, 1)
            pe.transpose(psum[0:1, 2, 0:P], thr[:, :], ident[:, :]).then_inc(s_thr_r, 1)
            pe.wait_ge(s_thr_c, 1)
            pe.matmul(bank(3, NX), ones[0:1, :], t64[0][0:1, 0:NX], start=True, stop=True).then_inc(s_thr_s, 1)
            above, ties, final = (tok_b[:, n * 512:(n + 1) * 512] for n in range(3))
            pe.wait_ge(s_ms, 1)
            pe.matmul(bank(4), ones_b[:, :], above, start=True, stop=True)
            pe.matmul(bank(5), ones_b[:, :], ties, start=True, stop=True)
            pe.matmul(bank(6), not_before_b[:, :], ties, start=True, stop=True).then_inc(s_ps, 1)
            pe.wait_ge(s_ms, 2)
            pe.matmul(bank(0), ones_b[:, :], final, start=True, stop=True)
            pe.matmul(bank(1), not_before_b[:, :], final, start=True, stop=True).then_inc(s_ps, 1)
            def place(i):
                pe.wait_ge(s_hr, i + 1)
                pe.wait_ge(s_hp, i + 1)
                pe.wait_ge(s_hu, i + 1)
                rows_, tiles = hot_row[:, i * HT:(i + 1) * HT, :], hot_tile[:, i * HT:(i + 1) * HT, :, :]
                for t in range(HT):
                    m = pe.matmul(bank(2, 2 * NT), rows_[:, t, :], tiles[:, t, :, :].rearrange("p a c -> p (a c)"),
                                  start=i == 0 and t == 0, stop=i == B // HT - 1 and t == HT - 1)
                m.then_inc(s_inv_mm, 1)
            for i in range(B // HT):
                place(i)

            pe.wait_ge(s_idx, 3)
            pe.wait_ge(s_moe, 16 * 10)

            def turn_rows(a, n):
                pe.wait_ge(s_prep, a + 1)
                wait(pe, s_gc, a - 1)
                pe.transpose(bank(n % 2, P), gn[n % DEPTH], ident[:, :]).then_inc(s_gt, 1)

            def layer1(a, n):
                pe.wait_ge(s_gc, a + 1)
                wait(pe, s_hc, a - 1)
                wait(pe, s_hd, a - 1)
                for c in range(NC):
                    dst = bank(2 + n % 2)[:, P * c:P * c + P] if c < NC - 1 else bank(6 + n % 2, P)
                    m = pe.matmul(dst, w1_now[n % DEPTH][:, P * c:P * c + P], gT[n % DEPTH], start=True, stop=True)
                m.then_inc(s_l1, 1)

            def layer2(a, n):
                e = pe.value_load(expert_of[0:1, bass.ds(a, 1)], min_val=0, max_val=NX - 1)
                pe.wait_ge(s_hc, a + 1)
                pe.wait_ge(s_hd, a + 1)
                wait(pe, s_y, a - 1)
                for c in range(NC):
                    m = pe.matmul(bank(4 + n % 2, E), hT[n % DEPTH][:, P * c:P * c + P],
                                  w2s[:, bass.ds(e, 1), c, :].rearrange("p e d -> p (e d)"),
                                  start=(c == 0), stop=(c == NC - 1))
                m.then_inc(s_l2, 1)

            turn_rows(0, 0)
            turn_rows(1, 1)
            for a in range(RING):
                turn_rows(a + 2, a + 2)
                layer1(a, a)
                if a >= 2:
                    layer2(a - 2, a - 2)
            with pe.Fori(1, NT // RING - 1) as r:
                for n in range(RING):
                    turn_rows(r * RING + (n + 2), n + 2)
                    layer1(r * RING + n, n)
                    layer2(r * RING + (n - 2), n - 2)
            for a in range(NT - RING, USED + 2):
                if a + 2 < USED:
                    turn_rows(a + 2, a + 2)
                if a < USED:
                    layer1(a, a)
                layer2(a - 2, a - 2)

        @block.vector
        def _(dve):
            ch = Chain(dve, s_dve)

            def do(ins):
                ch.link(ins)
                ch.join()

            def global_scale(k, uses, meanwhile=(None, None)):
                if meanwhile[0]:
                    meanwhile[0]()
                dve.wait_ge(s_grow, k + 1)
                dve.tensor_reduce(gmax[0:1, k:k + 1], psum[0:1, 7, 0:P], AX, ALU.max).then_inc(s_gm, 1)
                if meanwhile[1]:
                    meanwhile[1]()
                dve.wait_ge(s_gcol, k + 1)
                do(dve.tensor_scalar(iscale[:, k:k + 1], psum[:, 7, P + k:P + k + 1], 1e-8, 1.0 / 127.0,
                                     ALU.max, ALU.mult))
                dve.reciprocal(inv[:, k:k + 1], iscale[:, k:k + 1]).then_inc(s_inv, 1)
                for w in uses:
                    ins = dve.tensor_tensor(scale[:, w:w + 1], ws[:, w:w + 1], iscale[:, k:k + 1], ALU.mult)
                    if w == uses[-1]:
                        ins.then_inc(s_sc, 1)

            def layer_norm_steps(st, mean, n, ready, count, done):
                me, m2e, mo, m2o = (st[:, :, j] for j in (1, 2, 4, 5))
                a, b_, v = tmp[:, 0, 0:n], tmp[:, 1, 0:n], tmp[:, 2, 0:n]

                def sums():
                    dve.wait_ge(ready, count)
                    ch.link(dve.tensor_tensor(a, me, mo, ALU.add))
                    ch.link(dve.tensor_tensor(b_, me, mo, ALU.subtract))
                    ch.link(dve.tensor_tensor(v, m2e, m2o, ALU.add))

                def square():
                    ch.join()
                    dve.tensor_scalar(mean, a, 0.5, None, ALU.mult).then_inc(s_mean, 1)
                    ch.link(dve.tensor_tensor(b_, b_, b_, ALU.mult))

                def combine():
                    ch.join()
                    ch.link(dve.scalar_tensor_tensor(v, b_, float(E) / 4, v, ALU.mult, ALU.add))

                def finish():
                    ch.join()
                    dve.tensor_scalar(v, v, 1.0 / E, EPS, ALU.mult, ALU.add).then_inc(done, 1)
                return sums, square, combine, finish

            w = CJ * DC // NP
            dve.wait_ge(s_const, 12)
            for n in range(NP):
                dve.wait_ge(s_ctx[n], 16)
                ch.link(dve.tensor_reduce(part[0:CP, 0, n:n + 1], ctx_raw[0:CP, w * n:w * n + w], AX, ALU.max,
                                          apply_absolute_value=True))
            ch.join()
            dve.tensor_reduce(amax[0:CP, Q_CTX:Q_CTX + 1], part[0:CP, 0, 0:NP], AX, ALU.max).then_inc(s_amax, 1)

            def weight_sums():
                dve.wait_ge(s_w, 16 * 7)
                for k in range(7):
                    rows_ = KV if k in (ATT0, ATT1) else P
                    dve.tensor_reduce(wsum[0:rows_, k:k + 1], wslice(wraw, k), AX, ALU.add,
                                      apply_absolute_value=True).then_inc(s_wsum, 1)

            global_scale(Q_CTX, [], (None, weight_sums))
            dve.wait_ge(s_wtot, 1)
            do(dve.tensor_tensor(ws[:, :], bank(6, 7), inv_counts[:, :], ALU.mult))
            do(dve.tensor_scalar(ws[:, :], ws[:, :], 1e-5, None, ALU.max))
            dve.tensor_tensor(scale[:, D2V:D2V + 1], ws[:, D2V:D2V + 1], iscale[:, Q_CTX:Q_CTX + 1], ALU.mult
                              ).then_inc(s_sc, 1)
            ch.link(dve.tensor_scalar(wlim[:, 0, :], ws[:, :], 0.5, None, ALU.mult))
            do(dve.tensor_scalar(wlim[:, 1, :], ws[:, :], -0.5, None, ALU.mult))
            for k in range(7):
                rows_ = KV if k in (ATT0, ATT1) else P
                ch.link(dve.tensor_scalar(wslice(wneg, k), wslice(wraw, k), wlim[0:rows_, 1, k:k + 1], None, ALU.is_lt))
            ch.join()
            for k in range(7):
                rows_ = KV if k in (ATT0, ATT1) else P
                dve.scalar_tensor_tensor(wslice(wq, k), wslice(wraw, k), wlim[0:rows_, 0, k:k + 1], wslice(wneg, k),
                                         ALU.is_gt, ALU.subtract).then_inc(s_wq, 1)
            for n in range(NP):
                dve.wait_ge(s_fs, n + 1)
                dve.tensor_scalar(ctx_q[:, w * n:w * n + w], ctx_raw[0:CP, w * n:w * n + w], MAGIC, None, ALU.subtract
                                  ).then_inc(s_cq, 1)

            for n in range(XP):
                dve.wait_ge(s_x[n], 16)
                for t in range(B // XP * n, B // XP * (n + 1)):
                    m = dve.bn_stats(stats[:, t, :], xall[:, t, 0:E])
            m.then_inc(s_bn0, 1)
            for small in layer_norm_steps(stats[:, :, :], xall[:, :, E], B, s_bn0, 1, s_var):
                small()

            def less_mean(n):
                t = slice(n * 2 * GB, (n + 1) * 2 * GB)
                dve.tensor_tensor(xn[:, t, :], xall[:, t, 0:E], xall[:, t, E:E + 1].to_broadcast([P, 2 * GB, E]),
                                  ALU.subtract).then_inc(s_lm, 1)

            def over_deviation(n):
                t = slice(n * 2 * GB, (n + 1) * 2 * GB)
                dve.wait_ge(s_lm, n + 1)
                ch.link(dve.tensor_tensor(xn[:, t, :], xn[:, t, :],
                                          xall[:, t, E + 1:E + 2].to_broadcast([P, 2 * GB, E]), ALU.mult))

            def maxima(first):
                for n in range(NP):
                    dve.wait_ge(s_mmc, first + 2 + -(-PC * (n + 1) // QC))
                    ch.link(dve.tensor_reduce(part[:, 0, n:n + 1], feat[:, PC * n:PC * n + PC], AX, ALU.max,
                                              apply_absolute_value=True))
                ch.join()

            def take_magic_off(dst, first, done, meanwhile=()):
                for n in range(NP):
                    if n < len(meanwhile):
                        meanwhile[n]()
                    dve.wait_ge(s_fs, first + n + 1)
                    dve.tensor_scalar(dst[:, PC * n:PC * n + PC], scaled[:, PC * n:PC * n + PC], MAGIC, None,
                                      ALU.subtract).then_inc(done, 1)

            maxima(0)
            dve.tensor_reduce(amax[:, Q_VIS:Q_VIS + 1], part[:, 0, 0:NP], AX, ALU.max).then_inc(s_amax, 1)
            dve.wait_ge(s_std, 1)
            dve.wait_ge(s_mean, 1)
            dve.reciprocal(xall[:, :, E + 1], tmp[:, 3, :]).then_inc(s_rs0, 1)
            dve.wait_ge(s_wtr, 3)
            global_scale(Q_VIS, [IMG], (lambda: less_mean(0), lambda: less_mean(1)))
            dve.wait_ge(s_rs0, 1)
            over_deviation(0)
            less_mean(2)
            take_magic_off(qb, NP, s_vq, [lambda n=n: (over_deviation(n), less_mean(n + 2))
                                          for n in range(1, VG // 2 - 2)])
            over_deviation(VG // 2 - 2)
            over_deviation(VG // 2 - 1)

            def ln_max(n):
                lo, hi = (n * VG * GT // (NP - 1), (n + 1) * VG * GT // (NP - 1)) if n < NP - 1 else (VG * GT, T)
                ch.link(dve.tensor_reduce(part[:, 1, n:n + 1], big[:, lo:hi], AX, ALU.max, apply_absolute_value=True))

            ch.join()
            ln_max(0)
            maxima(NQ)
            dve.tensor_reduce(amax[:, Q_IMG:Q_IMG + 1], part[:, 0, 0:NP], AX, ALU.max).then_inc(s_amax, 1)
            global_scale(Q_IMG, [ATT0, ATT1], (None, lambda: ln_max(1)))
            ln_max(2)
            dve.wait_ge(s_xn, (G - VG) // 2)
            ln_max(3)
            ch.join()
            dve.tensor_reduce(amax[:, Q_X:Q_X + 1], part[:, 1, 0:NP], AX, ALU.max).then_inc(s_amax, 1)
            global_scale(Q_X, [TXT], (lambda: take_magic_off(qa, 2 * NP, s_iq), None))

            def quantise_tokens(k, scaled_, done):
                w, waits = T // XP, 0
                for n in range(XP):
                    v = big[:, w * n:w * n + w]
                    if n in OWN:
                        dve.wait_ge(s_inv, k + 1)
                        do(dve.tensor_scalar(v, v, inv[:, k:k + 1], MAGIC, ALU.mult, ALU.add))
                    else:
                        waits += 1
                        dve.wait_ge(scaled_, waits)
                    dve.tensor_scalar(tok_b[:, w * n:w * n + w], v, MAGIC, None, ALU.subtract).then_inc(done, 1)
            quantise_tokens(Q_X, s_xs, s_xq)
            w = T // XP
            for n in range(XP // 2, XP):
                dve.wait_ge(s_tr, NQ + n + 1)
                dve.tensor_copy(xqT[:, w * n:w * n + w], bank_b(n)).then_inc(s_trd, 1)

            for l in range(2):
                dve.sem_inc(s_sub[l], 1)
                dve.sem_inc(s_up[l], 1)

            def scores_in(l):
                return bank(1 + l, GC).rearrange("p (b c) -> p b c", b=GB)

            def maximum(l, i):
                dve.wait_ge(s_smm[l], i + 1)
                dve.tensor_reduce(amx[:, l, :], scores_in(l), AX, ALU.max).then_inc(s_mx[l], 1)

            def less_max(l, i, n):
                dve.wait_ge(s_mx[l], i + 1)
                wait(dve, s_t[l], i)
                dve.tensor_tensor(prob[l][n % 2], scores_in(l), amx[:, l, :].unsqueeze(2).to_broadcast([P, GB, CT]),
                                  ALU.subtract).then_inc(s_sub[l], 1)

            def total(l, i, n):
                dve.wait_ge(s_e[l], i + 1)
                dve.tensor_reduce(asum[:, l, :], prob[l][n % 2], AX, ALU.add).then_inc(s_sum[l], 1)

            def invert(l, i):
                dve.wait_ge(s_sum[l], i + 1)
                wait(dve, s_p[l], i)
                dve.reciprocal(arec[:, l, :], asum[:, l, :]).then_inc(s_r[l], 1)

            def update(l, i, n):
                dve.wait_ge(s_av[l], i + 2)
                dst, src = (big[:, g4(i)], fused1[n % GR]) if l else (fused1[n % GR], fused0[n % GR])
                dve.scalar_tensor_tensor(dst, bank(5 + l), 0.1, src, ALU.mult, ALU.add).then_inc(s_up[l], 1)

            def maximum_fused(i):
                dve.wait_ge(s_up[1], i + 2)
                dve.tensor_reduce(part[:, 2, bass.ds(i, 1)], big[:, g4(i)], AX, ALU.max,
                                  apply_absolute_value=True).then_inc(s_fm, 1)

            def step(t, n, last):
                first, second = last < G, 2 <= last < G + 2
                if first:
                    maximum(0, t)
                if second:
                    maximum(1, t - 2)
                if first:
                    less_max(0, t, n)
                if second:
                    less_max(1, t - 2, n + 2)
                if first:
                    total(0, t, n)
                if second:
                    total(1, t - 2, n + 2)
                if first:
                    invert(0, t)
                if second:
                    invert(1, t - 2)
                if 1 <= last < G + 1:
                    update(0, t - 1, n - 1)
                if 3 <= last:
                    update(1, t - 3, n - 3)
                    maximum_fused(t - 3)
            attention_steps(lambda a, b, body: for_loop(dve, a, b, body), step)

            dve.wait_ge(s_avg, CT // 11 - 1 + 10)
            do(dve.tensor_scalar(avg[:, :], avg[:, :], 1.0 / CT, None, ALU.mult))
            ch.link(dve.tensor_reduce(part[:, 3, 0:1], avg[:, :], AX, ALU.max, apply_absolute_value=True))
            dve.wait_ge(s_fm, G)
            ch.join()
            do(dve.tensor_reduce(part[:, 3, 1:2], part[:, 2, 0:G], AX, ALU.max))
            dve.tensor_tensor(amax[:, Q_CAT:Q_CAT + 1], part[:, 3, 0:1], part[:, 3, 1:2], ALU.max).then_inc(s_amax, 1)
            global_scale(Q_CAT, [F1], (None, lambda: [dve.memset(v, -32768.0).then_inc(s_hrm, 1) for v in hrun]))
            dve.wait_ge(s_inv, Q_CAT + 1)
            do(dve.tensor_scalar(avg[:, :], avg[:, :], inv[:, Q_CAT:Q_CAT + 1], MAGIC, ALU.mult, ALU.add))
            dve.tensor_scalar(avg_q[:, :], avg[:, :], MAGIC, None, ALU.subtract).then_inc(s_catq, 1)
            quantise_tokens(Q_CAT, s_cs, s_catq)

            with dve.Fori(0, G) as i:
                for pair in range(2):
                    dve.wait_ge(s_hcp, i * 2 + (pair + 5))
                    dve.wait_ge(s_hrm, i * 2 + (pair + 1))
                    dve.sem_inc(s_passed2, 1)
                    dve.tensor_tensor(hrun[pair], hrun[pair],
                                      hint[pair][:, bass.ds(i, 1), :, :].rearrange("p g c n -> p (g c) n"), ALU.max
                                      ).then_inc(s_hrm, 1)
            dve.wait_ge(s_hrm, 2 * G + 2)
            ch.link(dve.tensor_reduce(part[:, 0, 0:2], hrun[0], AX, ALU.max))
            do(dve.tensor_reduce(part[:, 0, 2:4], hrun[1], AX, ALU.max))
            do(dve.scalar_tensor_tensor(part[:, 1, 0:NC], part[:, 0, 0:NC], scale[:, F1:F1 + 1], bcol[:, 5:5 + NC],
                                        ALU.mult, ALU.add))
            do(dve.tensor_scalar(part[:, 1, 0:NC], part[:, 1, 0:NC], 0.0, None, ALU.max))
            dve.tensor_reduce(amax[:, Q_H:Q_H + 1], part[:, 1, 0:NC], AX, ALU.max).then_inc(s_amax, 1)
            dve.wait_ge(s_grow, Q_H + 1)
            dve.tensor_reduce(gmax[0:1, Q_H:Q_H + 1], psum[0:1, 7, 0:P], AX, ALU.max).then_inc(s_gm, 1)
            dve.wait_ge(s_gcol, Q_H + 1)
            do(dve.tensor_scalar(iscale[:, Q_H:Q_H + 1], psum[:, 7, P + Q_H:P + Q_H + 1], 1e-8, 1.0 / 127.0,
                                 ALU.max, ALU.mult))
            do(dve.reciprocal(inv[:, Q_H:Q_H + 1], iscale[:, Q_H:Q_H + 1]))
            ch.link(dve.tensor_tensor(scale[:, F2:F2 + 1], ws[:, F2:F2 + 1], iscale[:, Q_H:Q_H + 1], ALU.mult))
            ch.link(dve.tensor_scalar(h_bias[:, :], bcol[:, 5:5 + NC], inv[:, Q_H:Q_H + 1], None, ALU.mult))
            ch.join()
            dve.tensor_tensor(h_scale[:, :], scale[:, F1:F1 + 1], inv[:, Q_H:Q_H + 1], ALU.mult).then_inc(s_sc, 1)

            def quantise_hidden(i, n):
                dve.wait_ge(s_relu, (i + 1) * 4)
                wait(dve, s_f2, i - 1)
                dve.tensor_scalar(hq[n], u[n], MAGIC, MAGIC, ALU.add, ALU.subtract).then_inc(s_hq, 1)

            def x1(i):
                xr = xall[:, bass.ds(i * GB, GB), 0:E]
                dve.wait_ge(s_f2, i + 1)
                dve.scalar_tensor_tensor(xr, bank(4).rearrange("p (b d) -> p b d", b=GB), scale[:, F2:F2 + 1],
                                         xr, ALU.mult, ALU.add).then_inc(s_x1, 1)

            def half_statistics(i, b):
                if b == 0:
                    dve.wait_ge(s_x1, i + 1)
                    dve.sem_inc(s_passed2, 1)
                m = dve.bn_stats(stats[:, b, :], xall[:, bass.ds(i * GB + b, 1), 0:E].rearrange("p t d -> p (t d)"))
                if b == GB - 1:
                    m.then_inc(s_bn, 1)

            def inverse_deviation(i):
                dve.wait_ge(s_std2, i + 1)
                dve.wait_ge(s_mean, i + 2)
                dve.reciprocal(xall[:, bass.ds(i * GB, GB), E + 1], tmp[:, 3, 0:GB]).then_inc(s_rs, 1)

            def step(t, n, last):
                first, second = 1 <= last < G + 1, 2 <= last < G + 2
                if 0 <= last < G:
                    quantise_hidden(t, n)
                if 3 <= last < G + 3:
                    inverse_deviation(t - 3)
                if first:
                    x1(t - 1)
                if second:
                    small = layer_norm_steps(st2, xall[:, bass.ds((t - 2) * GB, GB), E], GB, s_bn, t - 1, s_var2)
                for b in range(GB):
                    if second:
                        small[b]()
                    if first:
                        if second and b == 0:
                            ch.join()
                        half_statistics(t - 1, b)

            dve.wait_ge(s_res, G)
            hidden_steps(lambda a, b, body: ch.loop(a, b, 2 * 5, body), step)

            def v3(ap):
                return ap.rearrange("p (t e) -> p t e", e=NX)

            def over_e(ap):
                return ap.unsqueeze(2).to_broadcast([P, B, NX])

            def over_t(ap):
                return ap.unsqueeze(1).to_broadcast([P, B, NX])

            dve.wait_ge(s_lg, G)
            do(dve.tensor_reduce(t64[1][:, :], v3(bank(6)), AX, ALU.max))
            dve.tensor_tensor(v3(route(0)), v3(bank(6)), over_e(t64[1][:, :]), ALU.subtract).then_inc(s_d, 1)
            dve.wait_ge(s_ex, 1)
            do(dve.tensor_reduce(t64[1][:, :], v3(route(0)), AX, ALU.add))
            do(dve.reciprocal(t64[2][:, :], t64[1][:, :]))
            do(dve.tensor_tensor(v3(route(0)), v3(route(0)), over_e(t64[2][:, :]), ALU.mult))
            top = t64[3][:, :]
            do(dve.tensor_reduce(top, v3(route(0)), AX, ALU.max))
            do(dve.tensor_tensor(v3(route(0)), v3(route(0)), over_e(top), ALU.is_equal))
            do(dve.tensor_tensor(v3(route(0)), v3(route(0)), over_t(rank8[:, :]), ALU.mult))
            do(dve.tensor_reduce(t64[2][:, :], v3(route(0)), AX, ALU.max))
            do(dve.tensor_tensor(v3(route(1)), v3(route(0)), over_e(t64[2][:, :]), ALU.is_equal))
            dve.tensor_tensor(v3(route(2)), v3(route(1)), over_e(top), ALU.mult).then_inc(s_v, 1)
            dve.wait_ge(s_vt, 1)
            key = route(3)
            digits = route(8).bitcast(I16)[:, 0:512]
            ch.link(dve.tensor_copy(key, bank(0)))
            do(dve.tensor_scalar(route(4), bank(0), float(HALF), MAGIC, ALU.mult, ALU.add))
            do(dve.tensor_scalar(route(4), route(4), MAGIC, None, ALU.subtract))
            do(dve.scalar_tensor_tensor(route(5), key, float(HALF), route(4), ALU.mult, ALU.is_lt))
            do(dve.tensor_tensor(digits, route(4), route(5), ALU.subtract))

            def level(k, done):
                for j in range(3):
                    m = dve.tensor_scalar(route(4 + j).bitcast(I16)[:, 0:512], digits, cand[:, j:j + 1], None,
                                          ALU.is_ge, ALU.add, accum_out=cnt[:, j:j + 1])
                m.then_inc(s_cnt, 1)
                w = steps[:, bass.ds(k, 1), 0:3].rearrange("p a b -> p (a b)")
                below = steps[:, bass.ds(k + 1, 1), 3:6].rearrange("p a b -> p (a b)")
                ch.link(dve.tensor_scalar(base[:, :], below, thr[:, :], None, ALU.add))
                dve.wait_ge(s_cnt2, done)
                do(dve.tensor_scalar(reached[:, :], bank(1, 3), float(CAP), None, ALU.is_ge, ALU.add,
                                     accum_out=met[:, :]))
                ch.link(dve.scalar_tensor_tensor(cand[:, :], w, met[:, :], base[:, :], ALU.mult, ALU.add))
                do(dve.scalar_tensor_tensor(thr[:, :], w[:, 0:1], met[:, :], thr[:, :], ALU.mult, ALU.add))

            def search(n):
                ch.link(dve.memset(thr[:, :], 0.0))
                do(dve.tensor_copy(cand[:, :], steps[:, 0, 3:6]))
                level(0, n * LEVELS + 1)
                ch.loop(0, (LEVELS - 1) // 3, 4 * 3,
                        lambda r: [level(r * 3 + k, r * 3 + (k + n * LEVELS + 1)) for k in (1, 2, 3)])
                do(dve.tensor_scalar(half[:, n:n + 1], thr[:, :], 1.0 / HALF, None, ALU.mult))

            search(0)
            do(dve.tensor_scalar(route(4), key, half[:, 0:1], float(HALF) ** 2, ALU.subtract, ALU.mult))
            do(dve.tensor_scalar(digits, route(4), -1.0, float(HALF), ALU.max, ALU.min))
            search(1)
            dve.scalar_tensor_tensor(thr[:, :], half[:, 1:2], 1.0 / HALF, half[:, 0:1], ALU.mult, ALU.add
                                     ).then_inc(s_thr, 1)
            dve.wait_ge(s_thr_r, 1)
            dve.tensor_copy(t64[0][0:1, 0:NX], psum[0:1, 2, 0:NX]).then_inc(s_thr_c, 1)
            dve.wait_ge(s_thr_s, 1)
            do(dve.tensor_copy(thr8[:, :], bank(3, NX)))

            above, ties, final = (tok_b[:, n * 512:(n + 1) * 512] for n in range(3))

            def et(ap):
                return ap.rearrange("p (e t) -> p t e", e=NX)

            ch.link(dve.tensor_tensor(et(above), v3(route(2)), over_t(thr8[:, :]), ALU.is_gt))
            do(dve.tensor_tensor(v3(route(0)), v3(route(2)), over_t(thr8[:, :]), ALU.is_equal))
            dve.tensor_tensor(et(ties), v3(route(0)), v3(route(1)), ALU.mult).then_inc(s_ms, 1)

            def earlier(columns, rows_, full):
                do(dve.tensor_tensor_scan(full, seg[:, :], columns, 0.0, ALU.mult, ALU.add))
                do(dve.tensor_tensor(v3(route(7)), et(full), et(rows_), ALU.add))

            dve.wait_ge(s_ps, 1)
            do(dve.tensor_reduce(n8[0][:, :], bank(4).rearrange("p (e t) -> p e t", e=NX), AX, ALU.add))
            do(dve.tensor_scalar(n8[1][:, :], n8[0][:, :], -1.0, float(CAP), ALU.mult, ALU.add))
            earlier(bank(5), bank(6), route(6))
            do(dve.tensor_tensor(v3(route(7)), v3(route(7)), over_t(n8[1][:, :]), ALU.is_lt))
            do(dve.tensor_tensor(v3(route(7)), v3(route(7)), et(ties), ALU.mult))
            do(dve.tensor_tensor(v3(route(7)), v3(route(7)), et(above), ALU.add))
            do(dve.tensor_reduce(t64[1][:, :], v3(route(7)), AX, ALU.add))
            do(dve.tensor_scalar(t64[1][:, :], t64[1][:, :], -1.0, 1.0, ALU.mult, ALU.add))
            do(dve.tensor_tensor(v3(route(7))[:, :, 0], v3(route(7))[:, :, 0], t64[1][:, :], ALU.add))
            do(dve.tensor_copy(route(8), route(7)))
            dve.tensor_copy(et(final), v3(route(7))).then_inc(s_ms, 1)

            dve.wait_ge(s_ps, 2)
            earlier(bank(0), bank(1), route(6))
            do(dve.tensor_copy(n8[0][:, :], route(6).rearrange("p (e t) -> p e t", e=NX)[:, :, B - 1]))
            do(dve.tensor_scalar(n8i[0][:, :], n8[0][:, :], float(P - 1), None, ALU.add))
            do(dve.tensor_scalar(n8i[1][:, :], n8i[0][:, :], 7, None, ALU.arith_shift_right))
            do(dve.tensor_copy(n8[1][:, :], n8i[1][:, :]))
            do(dve.tensor_tensor_scan(n8[2][:, :], ones[:, 0:NX], n8[1][:, :], 0.0, ALU.mult, ALU.add))
            do(dve.tensor_tensor(n8[3][:, :], n8[2][:, :], n8[1][:, :], ALU.subtract))
            do(dve.tensor_scalar(n8[3][:, :], n8[3][:, :], float(P), None, ALU.mult))
            do(dve.tensor_tensor(v3(route(7)), v3(route(7)), over_t(n8[3][:, :]), ALU.add))
            do(dve.tensor_tensor(route(7), route(7), route(8), ALU.mult))
            do(dve.tensor_reduce(t64[1][:, :], v3(route(7)), AX, ALU.add))
            do(dve.tensor_copy(t64i[0][:, :], t64[1][:, :]))
            ch.link(dve.tensor_scalar(t64i[1][:, :], t64i[0][:, :], 7, None, ALU.arith_shift_right))
            ch.link(dve.tensor_scalar(t64i[2][:, :], t64i[0][:, :], P - 1, None, ALU.bitwise_and))
            ch.join()
            ch.link(dve.tensor_copy(t64[4][:, :], t64i[1][:, :]))
            ch.link(dve.tensor_copy(t64[5][:, :], t64i[2][:, :]))
            ch.join()

            def one_hots(i):
                t = slice(i * HT, (i + 1) * HT)
                dve.tensor_tensor(hot[:, t, :], tile_no_b[:, :].unsqueeze(1).to_broadcast([P, HT, NT]),
                                  t64[4][:, t].unsqueeze(2).to_broadcast([P, HT, NT]), ALU.is_equal).then_inc(s_ht, 1)
                dve.tensor_tensor(hot_row[:, t, :], row_no_b[:, :].unsqueeze(1).to_broadcast([P, HT, P]),
                                  t64[5][:, t].unsqueeze(2).to_broadcast([P, HT, P]), ALU.is_equal).then_inc(s_hr, 1)
            for i in range(B // HT):
                one_hots(i)

            m = big[0:1, 10 * 512:10 * 512 + NT * NX].rearrange("p (a e) -> p a e", e=NX)
            do(dve.tensor_tensor(m, tile_no[0:1, :].unsqueeze(2).to_broadcast([1, NT, NX]),
                                 n8[2][0:1, :].unsqueeze(1).to_broadcast([1, NT, NX]), ALU.is_ge))
            m2 = big[0:1, 12 * 512:12 * 512 + NT]
            do(dve.tensor_reduce(m2, m, AX, ALU.add))
            dve.tensor_scalar(expert_of[:, :], m2, float(NX - 1), None, ALU.min).then_inc(s_idx, 1)
            dve.wait_ge(s_inv_mm, B // HT)
            w = [big[:, (13 + j) * 512:(13 + j) * 512 + NT] for j in range(3)]
            do(dve.tensor_scalar(w[0], bank(2)[:, NT:2 * NT], float(P), -float(P), ALU.mult, ALU.add))
            do(dve.tensor_tensor(w[0], bank(2)[:, 0:NT], w[0], ALU.add))
            dve.tensor_scalar(src_of[:, :], w[0], 0.0, None, ALU.max).then_inc(s_idx, 1)
            do(dve.tensor_scalar(w[1], w[0], 0.0, float(FAR + P), ALU.is_lt, ALU.mult))
            dve.tensor_tensor(dst_of[:, :], w[0], w[1], ALU.add).then_inc(s_idx, 1)

            dve.wait_ge(s_moe, 16 * 10)
            dve.wait_ge(s_idx, 3)

            def prepare(a, n, turn_):
                e = dve.value_load(expert_of[0:1, bass.ds(a, 1)], min_val=0, max_val=NX - 1)
                k, m = n % RING, n % DEPTH
                wait(dve, s_l1, a - (DEPTH - 1))
                ch.link(dve.tensor_copy(w1_now[m], w1s[:, bass.ds(e, 1), :].rearrange("p e f -> p (e f)")))
                wait(dve, s_hc, a - (DEPTH - 1))
                wait(dve, s_hd, a - (DEPTH - 1))
                ch.link(dve.tensor_copy(b1_now[m][:, :], b1col[:, bass.ds(e, 1), :].rearrange("p e c -> p (e c)")))
                dve.wait_ge(s_g[k], turn_)
                wait(dve, s_o[k], turn_ - 16)
                ch.link(dve.tensor_tensor(y[k], xg[k][:, 0:E], b2bc[:, bass.ds(e * E, E)], ALU.add))
                dve.tensor_scalar(gn[m], xg[k][:, 0:E], xg[k][:, E:E + 1], xg[k][:, E + 1:E + 2],
                                  ALU.subtract, ALU.mult).then_inc(s_prep, 1)
                ch.join()

            def hidden_out(a, n):
                dve.wait_ge(s_l1, a + 1)
                wait(dve, s_l2, a - (DEPTH - 1))
                c = NC - 1
                dve.tensor_scalar(hT[n % DEPTH][:, P * c:P * c + P], bank(6 + n % 2, P),
                                  b1_now[n % DEPTH][:, c:c + 1], 0.0, ALU.add, ALU.max).then_inc(s_hd, 1)

            def result(a, n):
                dve.wait_ge(s_l2, a + 1)
                dve.tensor_tensor(y[n % RING], bank(4 + n % 2, E), y[n % RING], ALU.add).then_inc(s_y, 1)

            for a in range(3):
                prepare(a, a, 16)
            for a in range(RING):
                prepare(a + 3, a + 3, 16 * ((a + 3) // RING + 1))
                hidden_out(a, a)
                if a >= 2:
                    result(a - 2, a - 2)

            def body(r):
                for n in range(RING):
                    prepare(r * RING + (n + 3), n + 3, (r + ((n + 3) // RING + 1)) * 16)
                    hidden_out(r * RING + n, n)
                    result(r * RING + (n - 2), n - 2)
            ch.loop(1, NT // RING - 1, 3 * RING, body)
            for a in range(NT - RING, USED + 2):
                if a + 3 < USED:
                    prepare(a + 3, a + 3, 16 * ((a + 3) // RING + 1))
                if a < USED:
                    hidden_out(a, a)
                result(a - 2, a - 2)


_WEIGHTS = ["d2v", "img", "txt", "att0", "att1", "f1", "f2"]


def kernel(**inputs):
    import concourse.bacc as _bacc
    from concourse.bass_utils import run_bass_kernel_spmd as _run

    nc = _bacc.Bacc("TRN2", target_bir_lowering=False, num_devices=1)
    arrays = {}

    def given(name):
        a = np.ascontiguousarray(inputs[name])
        arrays[f"in_{name}"] = a
        return nc.dram_tensor(f"in_{name}", a.shape, mybir.dt.from_np(a.dtype), kind="ExternalInput").ap()

    args = [given("x"), given("ctx_768"), [given(f"L0_xattn_W_{w}") for w in _WEIGHTS],
            [given(f"L0_xattn_b_{w}") for w in _WEIGHTS], given("L0_ffn_router_w"), given("L0_ffn_W1"),
            given("L0_ffn_b1"), given("L0_ffn_W2"), given("L0_ffn_b2")]
    out = nc.dram_tensor("out_0", (B, S, E), F32, kind="ExternalOutput").ap()
    xattn_moe(nc, *args, out)
    r = _run(nc, [arrays], core_ids=[0])
    return r.results[0]["out_0"]
```
